# Optimizing a Trainium2 kernel written in Bass

```python
import numpy as np
import jax
import jax.numpy as jnp

def _softmax(x, axis=-1):
    return jax.nn.softmax(x, axis=axis)

def _gelu(x):
    return jax.nn.gelu(x, approximate=True)

def _silu(x):
    return jax.nn.silu(x)

def _sigmoid(x):
    return jax.nn.sigmoid(x)

def _layernorm(x, axis=-1, eps=1e-05):
    m = jnp.mean(x, axis=axis, keepdims=True)
    v = jnp.var(x, axis=axis, keepdims=True)
    return (x - m) / jnp.sqrt(v + eps)

def _scatter_add(tgt, idx, src, axis=0):
    return tgt.at[idx].add(src)

def _segment_sum(src, seg, n):
    return jax.ops.segment_sum(src, seg, n)
kernel_name = 'mk_flamingo_gated_d2_seqx_r4_94df68'

def setup_inputs(seed: int=0):
    np.random.seed(seed)
    _w = jnp.asarray

    def _rec_inputs():
        import jax
        import jax.numpy as jnp
        _rk = jax.random.key(seed)
        x = 7.22e-05 + 1 * jax.random.normal(jax.random.fold_in(_rk, 1), (8, 512, 256), jnp.float32)
        _lenS = 512 - jax.random.randint(jax.random.fold_in(_rk, 7), (8,), 0, max(1, 512 // 4) + 1, jnp.int32)
        _lenS2 = 512 - jax.random.randint(jax.random.fold_in(_rk, 8), (8,), 0, max(1, 512 // 4) + 1, jnp.int32)
        _ctx_1024P = jax.random.normal(jax.random.fold_in(_rk, 11), (8, 16, 256), jnp.float32)
        _ctx_1024c = jax.random.dirichlet(jax.random.fold_in(_rk, 511), 0.3 * jnp.ones((16,), jnp.float32), (8, 512))
        _ctx_1024t = jnp.einsum('bsk,bkd->bsd', _ctx_1024c, _ctx_1024P)
        _ctx_1024t = _ctx_1024t * jax.lax.rsqrt(jnp.mean(jnp.square(_ctx_1024t)) + 1e-12) * 0.953939
        ctx_1024 = 4.13588e-05 + 0.999923 * (_ctx_1024t + 0.3 * jax.random.normal(jax.random.fold_in(_rk, 611), (8, 512, 256), jnp.float32))
        _g = jax.random.normal(jax.random.fold_in(_rk, 9001), (2, 2), jnp.float32)
        _g = jnp.sign(_g) * jnp.maximum(jnp.abs(_g), 1.0) + (_g == 0) * 1.0
        g_xattn = _g[0]
        g_ffn = _g[1]
        return (x, ctx_1024, g_xattn, g_ffn)
    x, ctx_1024, g_xattn, g_ffn = _rec_inputs()

    def _L0_xattn_setup():
        import jax, jax.numpy as jnp
        import numpy as np
        B, S, D = (4, 512, 256)
        key = jax.random.key(seed)
        kq, kk, kv, kwq, kwk, kwv = jax.random.split(key, 6)
        scale = 0.02
        return {'q': jax.random.normal(kq, (B, S, D), jnp.float32), 'k': jax.random.normal(kk, (B, S, D), jnp.float32), 'v': jax.random.normal(kv, (B, S, D), jnp.float32), 'Wq': jax.random.normal(kwq, (D, D), jnp.float32) * scale, 'Wk': jax.random.normal(kwk, (D, D), jnp.float32) * scale, 'Wv': jax.random.normal(kwv, (D, D), jnp.float32) * scale, 'mask': 1}
    _L0_xattn_all = _L0_xattn_setup()
    _L0_xattn_in = {k: v for k, v in _L0_xattn_all.items() if k in ('Wq', 'Wk', 'Wv')}
    del _L0_xattn_all

    def _L0_ffn_setup():
        import jax, jax.numpy as jnp
        import numpy as np
        E, K, H, F = (64, 6, 256, 128)
        SHARED_F = 512
        B, S = (1, 512)
        T = B * S
        CAP = 2 * ((T * K + E - 1) // E)
        key = jax.random.key(seed)
        ks = jax.random.split(key, 6)
        s = 0.05
        return {'hidden_states': jax.random.normal(ks[0], (B, S, H), jnp.float32), 'router_weight': jax.random.normal(ks[1], (E, H), jnp.float32) * s, 'expert_bias': jnp.zeros((E,), jnp.float32), 'w1': jax.random.normal(ks[2], (E, H, F), jnp.float32) * s, 'w2': jax.random.normal(ks[3], (E, F, H), jnp.float32) * s, 'sw1': jax.random.normal(ks[4], (SHARED_F, H), jnp.float32) * s, 'sw2': jax.random.normal(ks[5], (H, SHARED_F), jnp.float32) * s}
    _L0_ffn_all = _L0_ffn_setup()
    _L0_ffn_in = {k: v for k, v in _L0_ffn_all.items() if k in ('router_weight', 'expert_bias', 'w1', 'w2', 'sw1', 'sw2')}
    del _L0_ffn_all

    def _L1_xattn_setup():
        import jax, jax.numpy as jnp
        import numpy as np
        EMBED = 256
        HEADS = 16
        HEAD_DIM = EMBED // HEADS
        key = jax.random.key(seed)
        ks = jax.random.split(key, 10)
        B, N, M = (4, 512, 512)
        s = 1.0 / np.sqrt(EMBED)
        return {'xq': jax.random.normal(ks[0], (B, N, EMBED), jnp.float32), 'xk': jax.random.normal(ks[1], (B, M, EMBED), jnp.float32), 'xv': jax.random.normal(ks[2], (B, M, EMBED), jnp.float32), 'Wq': jax.random.normal(ks[3], (EMBED, EMBED), jnp.float32) * s, 'bq': jnp.zeros((EMBED,), jnp.float32), 'Wk': jax.random.normal(ks[4], (EMBED, EMBED), jnp.float32) * s, 'bk': jnp.zeros((EMBED,), jnp.float32), 'Wv': jax.random.normal(ks[5], (EMBED, EMBED), jnp.float32) * s, 'bv': jnp.zeros((EMBED,), jnp.float32), 'Wo': jax.random.normal(ks[6], (EMBED, EMBED), jnp.float32) * s}
    _L1_xattn_all = _L1_xattn_setup()
    _L1_xattn_in = {k: v for k, v in _L1_xattn_all.items() if k in ('Wq', 'bq', 'Wk', 'bk', 'Wv', 'bv', 'Wo')}
    del _L1_xattn_all

    def _L1_ffn_setup():
        import jax, jax.numpy as jnp
        import numpy as np
        E = 8
        TOPK = 2

        def _moe_forward(x, Wg, W1, W2, W3):
            B, S, D = x.shape
            xt = x.reshape(-1, D)
            T = xt.shape[0]
            logits = xt @ Wg.T
            scores = jax.nn.softmax(logits, axis=-1)
            w, idx = jax.lax.top_k(scores, TOPK)
            w = w / (w.sum(axis=-1, keepdims=True) + 1e-20)
            cw = jnp.zeros((T, E), xt.dtype).at[jnp.arange(T)[:, None], idx].add(w)
            h = jax.nn.silu(jnp.einsum('td,ehd->teh', xt, W1)) * jnp.einsum('td,ehd->teh', xt, W3)
            out = jnp.einsum('teh,edh->ted', h, W2)
            y = jnp.einsum('te,ted->td', cw, out)
            return y.reshape(B, S, D)
        key = jax.random.key(seed)
        k0, k1, k2, k3, k4 = jax.random.split(key, 5)
        B, S, D, H = (1, 512, 256, 704)
        scale = 0.02
        x = jax.random.normal(k0, (B, S, D), jnp.float32)
        Wg = jax.random.normal(k1, (E, D), jnp.float32) * scale
        W1 = jax.random.normal(k2, (E, H, D), jnp.float32) * scale
        W2 = jax.random.normal(k3, (E, D, H), jnp.float32) * scale
        W3 = jax.random.normal(k4, (E, H, D), jnp.float32) * scale
        return {'x': x, 'Wg': Wg, 'W1': W1, 'W2': W2, 'W3': W3}
    _L1_ffn_all = _L1_ffn_setup()
    _L1_ffn_in = {k: v for k, v in _L1_ffn_all.items() if k in ('Wg', 'W1', 'W2', 'W3')}
    del _L1_ffn_all
    return {'x': x, 'ctx_1024': ctx_1024, 'g_xattn': g_xattn, 'g_ffn': g_ffn, 'L0_xattn_Wq': _L0_xattn_in['Wq'], 'L0_xattn_Wk': _L0_xattn_in['Wk'], 'L0_xattn_Wv': _L0_xattn_in['Wv'], 'L0_ffn_router_weight': _L0_ffn_in['router_weight'], 'L0_ffn_expert_bias': _L0_ffn_in['expert_bias'], 'L0_ffn_w1': _L0_ffn_in['w1'], 'L0_ffn_w2': _L0_ffn_in['w2'], 'L0_ffn_sw1': _L0_ffn_in['sw1'], 'L0_ffn_sw2': _L0_ffn_in['sw2'], 'L1_xattn_Wq': _L1_xattn_in['Wq'], 'L1_xattn_bq': _L1_xattn_in['bq'], 'L1_xattn_Wk': _L1_xattn_in['Wk'], 'L1_xattn_bk': _L1_xattn_in['bk'], 'L1_xattn_Wv': _L1_xattn_in['Wv'], 'L1_xattn_bv': _L1_xattn_in['bv'], 'L1_xattn_Wo': _L1_xattn_in['Wo'], 'L1_ffn_Wg': _L1_ffn_in['Wg'], 'L1_ffn_W1': _L1_ffn_in['W1'], 'L1_ffn_W2': _L1_ffn_in['W2'], 'L1_ffn_W3': _L1_ffn_in['W3']}

def reference(x, ctx_1024, g_xattn, g_ffn, L0_xattn_Wq, L0_xattn_Wk, L0_xattn_Wv, L0_ffn_router_weight, L0_ffn_expert_bias, L0_ffn_w1, L0_ffn_w2, L0_ffn_sw1, L0_ffn_sw2, L1_xattn_Wq, L1_xattn_bq, L1_xattn_Wk, L1_xattn_bk, L1_xattn_Wv, L1_xattn_bv, L1_xattn_Wo, L1_ffn_Wg, L1_ffn_W1, L1_ffn_W2, L1_ffn_W3):
    import jax
    import jax.numpy as jnp

    def _L0_xattn_ref(q, k, v, Wq, Wk, Wv, mask):
        import jax, jax.numpy as jnp
        import numpy as np
        B, S, D = (4, 512, 256)
        Q = jnp.einsum('bsd,de->bse', q, Wq)
        K = jnp.einsum('bsd,de->bse', k, Wk)
        V = jnp.einsum('bsd,de->bse', v, Wv)
        d_k = Q.shape[-1]
        scores = jnp.einsum('bqd,bkd->bqk', Q, K) / jnp.sqrt(jnp.float32(d_k))
        if mask:
            causal = jnp.triu(jnp.ones((S, S), dtype=bool), k=1)
            scores = jnp.where(causal[None, :, :], -jnp.inf, scores)
        attn = jax.nn.softmax(scores, axis=-1)
        return jnp.einsum('bqk,bkd->bqd', attn, V)

    def _L0_ffn_ref(hidden_states, router_weight, expert_bias, w1, w2, sw1, sw2):
        import jax, jax.numpy as jnp
        import numpy as np
        E, K, H, F = (64, 6, 256, 128)
        SHARED_F = 512
        B, S = (1, 512)
        T = B * S
        CAP = 2 * ((T * K + E - 1) // E)
        b, s, h = hidden_states.shape
        x = hidden_states.reshape(-1, h)
        t = x.shape[0]
        logits = x @ router_weight.T
        scores = jax.nn.sigmoid(logits)
        _, top_idx = jax.lax.top_k(scores + expert_bias[None, :], K)
        top_scores = jnp.take_along_axis(scores, top_idx, axis=1)
        probs = top_scores / (jnp.sum(top_scores, axis=-1, keepdims=True) + 1e-20)
        flat_e = top_idx.reshape(-1)
        order = jnp.argsort(flat_e)
        sorted_e = flat_e[order]
        token_of = order // K
        counts = jnp.bincount(flat_e, length=E)
        offsets = jnp.cumsum(counts) - counts
        pos = jnp.arange(t * K) - offsets[sorted_e]
        valid = pos < CAP
        slot = jnp.where(valid, sorted_e * CAP + pos, E * CAP)
        xs = jnp.zeros((E * CAP + 1, h), x.dtype).at[slot].set(x[token_of])
        xs = xs[:-1].reshape(E, CAP, h)
        hmid = jax.nn.gelu(jnp.einsum('ech,ehf->ecf', xs, w1), approximate=True)
        y = jnp.einsum('ecf,efh->ech', hmid, w2).reshape(E * CAP, h)
        pair_w = jnp.where(valid, probs.reshape(-1)[order], 0.0)
        y_pair = y[jnp.minimum(slot, E * CAP - 1)] * pair_w[:, None]
        out = jnp.zeros((t, h), x.dtype).at[token_of].add(y_pair)
        shared = jax.nn.gelu(x @ sw1.T, approximate=True) @ sw2.T
        return (out + shared).reshape(b, s, h)

    def _L1_xattn_ref(xq, xk, xv, Wq, bq, Wk, bk, Wv, bv, Wo):
        import jax, jax.numpy as jnp
        import numpy as np
        EMBED = 256
        HEADS = 16
        HEAD_DIM = EMBED // HEADS
        B, N, _ = xq.shape
        M = xk.shape[1]
        scale = HEAD_DIM ** (-0.5)
        q = (xq @ Wq.T + bq).reshape(B, N, HEADS, HEAD_DIM).transpose(0, 2, 1, 3)
        k = (xk @ Wk.T + bk).reshape(B, M, HEADS, HEAD_DIM).transpose(0, 2, 1, 3)
        v = (xv @ Wv.T + bv).reshape(B, M, HEADS, HEAD_DIM).transpose(0, 2, 1, 3)
        scores = jnp.einsum('bhnd,bhmd->bhnm', q, k) * scale
        weights = jax.nn.softmax(scores, axis=-1)
        out = jnp.einsum('bhnm,bhmd->bhnd', weights, v)
        out = out.transpose(0, 2, 1, 3).reshape(B, N, EMBED)
        return out @ Wo.T

    def _L1_ffn_ref(x, Wg, W1, W2, W3):
        import jax, jax.numpy as jnp
        import numpy as np
        E = 8
        TOPK = 2

        def _moe_forward(x, Wg, W1, W2, W3):
            B, S, D = x.shape
            xt = x.reshape(-1, D)
            T = xt.shape[0]
            logits = xt @ Wg.T
            scores = jax.nn.softmax(logits, axis=-1)
            w, idx = jax.lax.top_k(scores, TOPK)
            w = w / (w.sum(axis=-1, keepdims=True) + 1e-20)
            cw = jnp.zeros((T, E), xt.dtype).at[jnp.arange(T)[:, None], idx].add(w)
            h = jax.nn.silu(jnp.einsum('td,ehd->teh', xt, W1)) * jnp.einsum('td,ehd->teh', xt, W3)
            out = jnp.einsum('teh,edh->ted', h, W2)
            y = jnp.einsum('te,ted->td', cw, out)
            return y.reshape(B, S, D)
        return _moe_forward(x, Wg, W1, W2, W3)
    x = x + jnp.tanh(g_xattn[0]) * _L0_xattn_ref(_layernorm(x, axis=-1), ctx_1024, ctx_1024, L0_xattn_Wq, L0_xattn_Wk, L0_xattn_Wv, 1)
    x = x + jnp.tanh(g_ffn[0]) * _L0_ffn_ref(_layernorm(x, axis=-1), L0_ffn_router_weight, L0_ffn_expert_bias, L0_ffn_w1, L0_ffn_w2, L0_ffn_sw1, L0_ffn_sw2)
    x = x + jnp.tanh(g_xattn[1]) * _L1_xattn_ref(_layernorm(x, axis=-1), ctx_1024, ctx_1024, L1_xattn_Wq, L1_xattn_bq, L1_xattn_Wk, L1_xattn_bk, L1_xattn_Wv, L1_xattn_bv, L1_xattn_Wo)
    x = x + jnp.tanh(g_ffn[1]) * _L1_ffn_ref(_layernorm(x, axis=-1), L1_ffn_Wg, L1_ffn_W1, L1_ffn_W2, L1_ffn_W3)
    return x

_drawn_inputs = setup_inputs


def setup_inputs(seed=0):
    import zlib

    import numpy as np

    out = dict(_drawn_inputs(seed))
    spreads = {'g_ffn': (-1.0, 0.6),
     'L0_ffn_expert_bias': (0.0, 0.1),
     'L1_xattn_bq': (0.0, 0.471),
     'L1_xattn_bk': (0.0, 0.8),
     'L1_xattn_bv': (0.0, 0.1)}
    factors = {'L0_xattn_Wq': 8.0,
     'L0_xattn_Wk': 8.0,
     'L1_ffn_Wg': 4.796,
     'L1_ffn_W1': 4.201,
     'L1_ffn_W2': 4.146,
     'L1_ffn_W3': 4.145}
    for name, (base, spread) in spreads.items():
        noise = np.random.default_rng([zlib.crc32(name.encode()), seed]).standard_normal(out[name].shape)
        drawn = base * np.exp(spread * noise) if base else spread * noise
        out[name] = jnp.asarray(drawn.astype(out[name].dtype))
    for name, factor in factors.items():
        out[name] = (out[name] * factor).astype(out[name].dtype)
    return out
```

```python
import concourse.bass as bass
from concourse import mybir
from contextlib import ExitStack


F32 = mybir.dt.float32
BF16 = mybir.dt.bfloat16
I32 = mybir.dt.int32
U32 = mybir.dt.uint32
ALU = mybir.AluOpType
ACT = mybir.ActivationFunctionType
AX = mybir.AxisListType

P = 128
B, S, D = 8, 512, 256
T = B * S
DT = D // P
CT = S // P
NT = T // P
EPS = 1e-5
NEG = -3.0e38


def counter(nc, m, ctx, name):
    sem = ctx.enter_context(nc.semaphore(name))
    assert sem.num not in m.counted
    m.counted.add(sem.num)
    return sem


def clear_counters(nc, m):
    runs = []
    for num in sorted(m.counted):
        if runs and runs[-1][1] == num:
            runs[-1][1] = num + 1
        else:
            runs.append([num, num + 1])
    m.counted.clear()
    with nc.Block() as block:
        @block.gpsimd
        def _(pool):
            for first, end in runs:
                pool.sem_clear(range(first, end))


def apart(m, eng):
    eng.sem_inc(m.passed, 1)


def at_least(eng, sem, value):
    if isinstance(value, int) and value <= 0:
        return
    eng.wait_ge(sem, value)


def constants(nc, m):
    with ExitStack() as ctx:
        def sb(name, shape, dt=F32):
            return ctx.enter_context(nc.sbuf_tensor(name, shape, dt))

        def sem(name):
            return counter(nc, m, ctx, name)

        wqT = sb("c_wqT", [P, DT, D])
        wkT = sb("c_wkT", [P, DT, D])
        gates = sb("c_gates", [P, 4])
        ps = ctx.enter_context(nc.psum_tensor("c_ps", [P, DT, 512], F32))
        w_in = sem("c_w_in")
        g_in = sem("c_g_in")
        x_in = sem("c_x_in")
        wv_in = sem("c_wv_in")
        zeroed = sem("c_zeroed")
        ident_made = sem("c_ident_made")
        a_done = sem("c_a_done")
        a_out = sem("c_a_out")
        gate_made = sem("c_gate_made")
        block = ctx.enter_context(nc.Block())

        @block.sync
        def _(sp):
            sp.dma_start(wqT[:, :, :], m.ins["WqT0"].rearrange("(t p) n -> p t n", p=P)).then_inc(w_in, 16)
            sp.dma_start(wkT[:, :, :], m.ins["WkT0"].rearrange("(t p) n -> p t n", p=P)).then_inc(w_in, 16)
            sp.dma_start(m.x[:, :, :], m.ins["x"].rearrange("b (t p) d -> p (b t) d", p=P)).then_inc(x_in, 16)
            sp.wait_ge(x_in, 16)

        @block.gpsimd
        def _(pool):
            pool.memset(m.ident[:, :], 0.0).then_inc(zeroed, 1)
            pool.memset(m.ident_bf[:, :], 0.0).then_inc(zeroed, 1)
            pool.memset(m.causal[:, :], 0.0).then_inc(zeroed, 1)
            pool.memset(m.minus_half[:, :], -0.5)
            pool.wait_ge(zeroed, 3)
            for t in (m.ident, m.ident_bf):
                pool.affine_select(out=t[:, :], in_=t[:, :], compare_op=ALU.not_equal, fill=1.0, base=0,
                                   pattern=[[-1, P]], channel_multiplier=1)
            pool.affine_select(out=m.causal[:, :], in_=m.causal[:, :], compare_op=ALU.is_ge, fill=NEG, base=0,
                               pattern=[[-1, P]], channel_multiplier=1).then_inc(ident_made, 1)

        @block.tensor
        def _(pe):
            pe.wait_ge(w_in, 32)
            for d in range(DT):
                for e in range(DT):
                    last = pe.matmul(ps[:, d, 0:D], wqT[:, e, d * P:(d + 1) * P], wkT[:, e, :],
                                     start=(e == 0), stop=(e == DT - 1))
                last.then_inc(a_done, 1)

        @block.scalar
        def _(act):
            act.dma_start(gates[:, 0:2], m.ins["g_xattn"].rearrange("(a n) -> a n", a=1).to_broadcast([P, 2])).then_inc(g_in, 16)
            act.dma_start(gates[:, 2:4], m.ins["g_ffn"].rearrange("(a n) -> a n", a=1).to_broadcast([P, 2])).then_inc(g_in, 16)
            act.dma_start(m.wv0[:, :, :], m.ins["Wv0"].rearrange("(t p) n -> p t n", p=P)).then_inc(wv_in, 16)
            act.wait_ge(g_in, 32)
            act.activation(m.gate[:, :], gates[:, :], ACT.Tanh).then_inc(gate_made, 1)
            act.wait_ge(gate_made, 1)
            act.activation(m.half_gate[:, :], m.gate[:, :], ACT.Copy, scale=0.5).then_inc(m.ready, 1)
            for d in range(DT):
                act.wait_ge(a_done, d + 1)
                act.activation(m.A[:, d, :], ps[:, d, 0:D], ACT.Copy, scale=float(D) ** -0.5).then_inc(a_out, 1)
            act.wait_ge(a_out, DT)
            act.wait_ge(wv_in, 16)


def attention_0(nc, m):
    with ExitStack() as ctx:
        def sb(name, shape, dt=F32):
            return ctx.enter_context(nc.sbuf_tensor(name, shape, dt))

        def sem(name):
            return counter(nc, m, ctx, name)

        cT = [sb(f"a_cT{u}", [P, DT, S]) for u in range(2)]
        h = sb("a_h", [P, CT, D])
        hT = sb("a_hT", [P, DT, S])
        qT = sb("a_qT", [P, DT, S])
        V = sb("a_V", [P, CT, D])
        prob = [sb(f"a_prob{u}", [P, S]) for u in range(2)]
        probT = [sb(f"a_probT{u}", [P, S]) for u in range(2)]
        st = sb("a_st", [P, CT, 6])
        mv = sb("a_mv", [P, CT, 2])
        ve = sb("a_ve", [P, CT])
        rstd = sb("a_rstd", [P, CT])
        nm = sb("a_nm", [P, CT])
        rowsum = sb("a_rowsum", [P, CT])
        rec = sb("a_rec", [P, CT])
        sc = sb("a_sc", [P, CT])
        ps = ctx.enter_context(nc.psum_tensor("a_ps", [P, 8, 512], F32))

        ctx_in = [sem(f"a_ctx_in{u}") for u in range(2)]
        bn_done = sem("a_bn_done")
        aggr_done = sem("a_aggr_done")
        ve_done = sem("a_ve_done")
        rstd_done = sem("a_rstd_done")
        h_done = sem("a_h_done")
        tr_done = sem("a_tr_done")
        hT_act = sem("a_hT_act")
        hT_dve = sem("a_hT_dve")
        q_done = sem("a_q_done")
        qT_act = sem("a_qT_act")
        qT_dve = sem("a_qT_dve")
        v_done = sem("a_v_done")
        V_act = sem("a_V_act")
        V_dve = sem("a_V_dve")
        s_done = sem("a_s_done")
        nm_done = sem("a_nm_done")
        p_done = sem("a_p_done")
        pT_done = sem("a_pT_done")
        pT_out = sem("a_pT_out")
        o_done = sem("a_o_done")
        rec_done = sem("a_rec_done")
        sc_done = sem("a_sc_done")
        x_done = sem("a_x_done")
        block = ctx.enter_context(nc.Block())

        def turns(eng, body):
            with eng.Fori(0, B // 2) as i:
                for u in range(2):
                    body(2 * i + u, i, u)

        @block.sync
        def _(sp):
            def load(n, u):
                sp.dma_start(cT[u][:, :, :], m.ins["ctxT"].rearrange("(t p) n -> p t n", p=P)[:, :, bass.ds(n * S, S)])\
                  .then_inc(ctx_in[u], 16)

            for u in range(2):
                load(u, u)
            with sp.Fori(0, B // 2 - 1) as i:
                for u in range(2):
                    sp.wait_ge(s_done, CT * (2 * i + u + 1))
                    load(2 * i + 2 + u, u)

        @block.gpsimd
        def _(pool):
            with pool.Fori(0, B + 1) as n:
                pool.wait_ge(ve_done, n + 1)
                pool.tensor_tensor(rstd[:, :], ve[:, :], m.minus_half[:, 0:CT], ALU.pow).then_inc(rstd_done, 1)

        @block.tensor
        def _(pe):
            def body(n, i, u):
                pe.wait_ge(V_act, n)
                pe.wait_ge(V_dve, n)
                for j in range(CT):
                    pe.wait_ge(h_done, CT * n + j + 1)
                    for d in range(DT):
                        last = pe.transpose(ps[:, d, j * P:(j + 1) * P], h[:, j, d * P:(d + 1) * P], m.ident[:, :])
                last.then_inc(tr_done, 1)
                pe.wait_ge(pT_out, CT * n)
                pe.wait_ge(hT_act, n + 1)
                pe.wait_ge(hT_dve, n + 1)
                for e in range(DT):
                    for d in range(DT):
                        last = pe.matmul(ps[:, 2 + e, :], m.A[:, d, e * P:(e + 1) * P], hT[:, d, :],
                                         start=(d == 0), stop=(d == DT - 1))
                    last.then_inc(q_done, 1)
                pe.wait_ge(ctx_in[u], 16 * i + 16)
                for k in range(CT):
                    for d in range(DT):
                        last = pe.matmul(ps[:, k // 2, (k % 2) * D:(k % 2 + 1) * D], cT[u][:, d, k * P:(k + 1) * P],
                                         m.wv0[:, d, :], start=(d == 0), stop=(d == DT - 1))
                    if k % 2:
                        last.then_inc(v_done, 1)
                pe.wait_ge(qT_act, n + 1)
                pe.wait_ge(qT_dve, n + 1)

                def scores(t):
                    pe.wait_ge(p_done, CT * n + max(t - 1, 0))
                    for d in range(DT):
                        pe.matmul(ps[:, 4 + t % 2, 0:(t + 1) * P], qT[:, d, t * P:(t + 1) * P],
                                  cT[u][:, d, 0:(t + 1) * P], start=(d == 0), stop=False)
                    pe.matmul(ps[:, 4 + t % 2, t * P:(t + 1) * P], m.ident_bf[:, :], m.causal[:, :],
                              start=False, stop=True).then_inc(s_done, 1)

                def transposes(t):
                    pe.wait_ge(p_done, CT * n + t + 1)
                    if t >= 2:
                        pe.wait_ge(pT_out, CT * n + t - 1)
                    for k in range(t + 1):
                        last = pe.transpose(ps[:, 2 + t % 2, k * P:(k + 1) * P], prob[t % 2][:, k * P:(k + 1) * P],
                                            m.ident[:, :])
                    last.then_inc(pT_done, 1)

                def weighted(t):
                    pe.wait_ge(pT_out, CT * n + t + 1)
                    pe.wait_ge(x_done, CT * n + max(t - 1, 0))
                    if t == 0:
                        pe.wait_ge(V_act, n + 1)
                        pe.wait_ge(V_dve, n + 1)
                    for k in range(t + 1):
                        last = pe.matmul(ps[:, 6 + t % 2, 0:D], probT[t % 2][:, k * P:(k + 1) * P], V[:, k, :],
                                         start=(k == 0), stop=(k == t))
                    last.then_inc(o_done, 1)

                scores(0)
                scores(1)
                transposes(0)
                scores(2)
                transposes(1)
                weighted(0)
                scores(3)
                transposes(2)
                weighted(1)
                transposes(3)
                weighted(2)
                weighted(3)

            turns(pe, body)

        @block.scalar
        def _(act):
            def body(n, i, u):
                act.wait_ge(tr_done, n + 1)
                act.wait_ge(q_done, DT * n)
                act.activation(hT[:, 0, :], ps[:, 0, :], ACT.Copy).then_inc(hT_act, 1)
                act.wait_ge(q_done, DT * n + 1)
                act.wait_ge(s_done, CT * n)
                act.activation(qT[:, 0, :], ps[:, 2, :], ACT.Copy).then_inc(qT_act, 1)
                act.wait_ge(v_done, 2 * n + 1)
                act.wait_ge(o_done, CT * n)
                act.activation(V[:, 0:2, :], ps[:, 0, :].rearrange("p (k n) -> p k n", k=2), ACT.Copy).then_inc(V_act, 1)
                for t in range(CT):
                    act.wait_ge(nm_done, CT * n + t + 1)
                    act.wait_ge(pT_done, CT * n + max(t - 1, 0))
                    act.activation(prob[t % 2][:, 0:(t + 1) * P], ps[:, 4 + t % 2, 0:(t + 1) * P], ACT.Exp,
                                   bias=nm[:, t:t + 1], accum_out=rowsum[:, t:t + 1]).then_inc(p_done, 1)

            turns(act, body)

        @block.vector
        def _(dve):
            def stats(n, chunk):
                for j in range(CT):
                    dve.bn_stats(st[:, j, :], m.x[:, bass.ds(chunk * CT + j, 1), :]).then_inc(bn_done, 1)
                for j in range(CT):
                    dve.wait_ge(bn_done, CT * n + j + 1)
                    apart(m, dve)
                    dve.bn_aggr(mv[:, j, :], st[:, j, :]).then_inc(aggr_done, 1)
                dve.wait_ge(aggr_done, CT * n + CT)
                dve.tensor_scalar(ve[:, :], mv[:, :, 1], EPS, None, ALU.add).then_inc(ve_done, 1)

            def normalise(n, chunk):
                dve.wait_ge(rstd_done, n + 1)
                dve.wait_ge(tr_done, n)
                for j in range(CT):
                    dve.tensor_scalar(h[:, j, :], m.x[:, bass.ds(chunk * CT + j, 1), :], mv[:, j, 0:1],
                                      rstd[:, j:j + 1], ALU.subtract, ALU.mult).then_inc(h_done, 1)

            def body(n, i, u):
                dve.wait_ge(tr_done, n + 1)
                dve.wait_ge(q_done, DT * n)
                dve.tensor_copy(hT[:, 1, :], ps[:, 1, :]).then_inc(hT_dve, 1)
                dve.wait_ge(q_done, DT * n + 2)
                dve.wait_ge(s_done, CT * n)
                dve.tensor_copy(qT[:, 1, :], ps[:, 3, :]).then_inc(qT_dve, 1)
                dve.wait_ge(v_done, 2 * n + 2)
                dve.wait_ge(o_done, CT * n)
                dve.tensor_copy(V[:, 2:4, :], ps[:, 1, :].rearrange("p (k n) -> p k n", k=2)).then_inc(V_dve, 1)

                def row_max(t):
                    dve.wait_ge(s_done, CT * n + t + 1)
                    dve.tensor_reduce(nm[:, t:t + 1], ps[:, 4 + t % 2, 0:(t + 1) * P], AX.X, ALU.max,
                                      negate=True).then_inc(nm_done, 1)

                def probT_out(t):
                    dve.wait_ge(pT_done, CT * n + t + 1)
                    dve.wait_ge(o_done, CT * n + max(t - 1, 0))
                    dve.tensor_copy(probT[t % 2][:, 0:(t + 1) * P], ps[:, 2 + t % 2, 0:(t + 1) * P]).then_inc(pT_out, 1)

                def add_to_x(t):
                    dve.wait_ge(p_done, CT * n + t + 1)
                    dve.reciprocal(rec[:, t:t + 1], rowsum[:, t:t + 1]).then_inc(rec_done, 1)
                    dve.wait_ge(rec_done, CT * n + t + 1)
                    dve.tensor_scalar(sc[:, t:t + 1], rec[:, t:t + 1], m.gate[:, 0:1], None, ALU.mult).then_inc(sc_done, 1)
                    dve.wait_ge(sc_done, CT * n + t + 1)
                    dve.wait_ge(o_done, CT * n + t + 1)
                    xt = m.x[:, bass.ds(n * CT + t, 1), :]
                    dve.scalar_tensor_tensor(xt, ps[:, 6 + t % 2:7 + t % 2, 0:D], sc[:, t:t + 1], xt, ALU.mult, ALU.add)\
                       .then_inc(x_done, 1)

                row_max(0)
                row_max(1)
                stats(n + 1, (n + 1) % B)
                probT_out(0)
                row_max(2)
                probT_out(1)
                normalise(n + 1, (n + 1) % B)
                row_max(3)
                add_to_x(0)
                probT_out(2)
                add_to_x(1)
                probT_out(3)
                add_to_x(2)
                add_to_x(3)

            stats(0, 0)
            normalise(0, 0)
            turns(dve, body)


E0, K0, F0, SF = 64, 6, 128, 512
CAP = 2 * ((512 * K0 + E0 - 1) // E0)
R8 = 8
ROUNDS = CAP // R8
ROW = D + E0
LOW = -2.0e38
GELU_A, GELU_C = 0.044715, 0.7978845608028654


def route_0(nc, m):
    with ExitStack() as ctx:
        def sb(name, shape, dt=F32):
            return ctx.enter_context(nc.sbuf_tensor(name, shape, dt))

        def sem(name):
            return counter(nc, m, ctx, name)

        row = [sb(f"b_row{u}", [P, CT, ROW]) for u in range(2)]
        hT = [sb(f"b_hT{u}", [P, DT, S]) for u in range(2)]
        rwT = sb("b_rwT", [P, DT, E0])
        bias = sb("b_bias", [P, E0])
        zero = sb("b_zero", [P, 2048])
        keyc = sb("b_keyc", [P, NT])
        st = sb("b_st", [P, CT, 6])
        mv = sb("b_mv", [P, CT, 2])
        ve = sb("b_ve", [P, CT])
        rstd = sb("b_rstd", [P, CT])
        ex = [sb(f"b_ex{u}", [P, CT, E0]) for u in range(2)]
        ex1 = sb("b_expp", [P, CT, E0])
        score = sb("b_score", [P, CT, E0])
        biased = sb("b_biased", [P, CT, E0 + 2])
        top8 = sb("b_top8", [P, CT, R8])
        take8 = sb("b_take8", [P, CT, R8])
        left = sb("b_left", [P, CT, E0 + 2])
        chosen = sb("b_chosen", [P, CT, E0])
        wgt = sb("b_wgt", [P, CT, E0])
        wsum = sb("b_wsum", [P, CT])
        wrec = sb("b_wrec", [P, CT])
        key = [sb(f"b_key{u}", [P, CT, E0]) for u in range(2)]
        ps = ctx.enter_context(nc.psum_tensor("b_ps", [P, 8, 512], F32))

        w_in = sem("b_w_in")
        zeroed = sem("b_zeroed")
        zero_out = sem("b_zero_out")
        keyc_made = sem("b_keyc_made")
        preset = sem("b_preset")
        bn_done = sem("b_bn_done")
        aggr_done = sem("b_aggr_done")
        ve_done = sem("b_ve_done")
        rstd_done = sem("b_rstd_done")
        h_done = sem("b_h_done")
        tr_done = sem("b_tr_done")
        hT_out = sem("b_hT_out")
        hT_kept = sem("b_hT_kept")
        l_done = sem("b_l_done")
        ex_done = sem("b_ex_done")
        chain = sem("b_chain")
        row_done = sem("b_row_done")
        row_out = [sem(f"b_row_out{u}") for u in range(2)]
        key_done = sem("b_key_done")
        keyT_done = sem("b_keyT_done")
        keyT_out = sem("b_keyT_out")
        block = ctx.enter_context(nc.Block())

        @block.sync
        def _(sp):
            sp.dma_start(rwT[:, :, :], m.ins["rwT"].rearrange("(t p) n -> p t n", p=P)).then_inc(w_in, 16)
            sp.dma_start(bias[:, :], m.ins["ebias"].rearrange("(a n) -> a n", a=1).to_broadcast([P, E0])).then_inc(w_in, 16)
            sp.wait_ge(zeroed, 1)
            for a in m.acc:
                for c in range(T * D // (P * 2048)):
                    sp.dma_start(a[0:T, :].rearrange("(c p r) n -> c p (r n)", p=P, r=8)[c], zero[:, :]).then_inc(zero_out, 16)
                sp.dma_start(a[T:T + CAP, :], zero[0:CAP, 0:D]).then_inc(zero_out, 16)
            sp.dma_start(m.rows[T:T + CAP, :], zero[0:CAP, 0:ROW]).then_inc(zero_out, 16)
            with sp.Fori(0, B // 2) as i:
                for u in range(2):
                    n = 2 * i + u
                    sp.wait_ge(row_done, n + 1)
                    sp.dma_start(m.rows[bass.ds(n * S, S), :].rearrange("(t p) n -> p t n", p=P), row[u][:, :, :])\
                      .then_inc(row_out[u], 16)
            sp.wait_ge(zero_out, 16 * (2 * (T * D // (P * 2048) + 1) + 1))
            for u in range(2):
                sp.wait_ge(row_out[u], 16 * (B // 2))

        @block.gpsimd
        def _(pool):
            pool.memset(zero[:, :], 0.0).then_inc(zeroed, 1)
            pool.iota(keyc[:, :], pattern=[[-P, NT]], base=T, channel_multiplier=-1,
                      allow_small_or_imprecise_dtypes=True).then_inc(keyc_made, 1)
            with pool.Fori(0, B // 2) as i:
                for u in range(2):
                    n = 2 * i + u
                    pool.wait_ge(ve_done, n + 1)
                    pool.tensor_tensor(rstd[:, :], ve[:, :], m.minus_half[:, 0:CT], ALU.pow).then_inc(rstd_done, 1)
                    pool.wait_ge(hT_out, DT * (n + 1))
                    apart(m, pool)
                    pool.tensor_copy(m.hT_all[:, :, bass.ds(n * S, S)], hT[u][:, :, :]).then_inc(hT_kept, 1)

        @block.tensor
        def _(pe):
            pe.wait_ge(w_in, 32)
            with pe.Fori(0, B // 2) as i:
                for u in range(2):
                    n = 2 * i + u
                    pe.wait_ge(hT_out, DT * n)
                    for j in range(CT):
                        pe.wait_ge(h_done, CT * n + j + 1)
                        for d in range(DT):
                            last = pe.transpose(ps[:, d, j * P:(j + 1) * P], row[u][:, j, d * P:(d + 1) * P], m.ident[:, :])
                    last.then_inc(tr_done, 1)
                    pe.wait_ge(hT_out, DT * (n + 1))
                    pe.wait_ge(ex_done, n)
                    for j in range(CT):
                        for d in range(DT):
                            last = pe.matmul(ps[:, 2, j * E0:(j + 1) * E0], hT[u][:, d, j * P:(j + 1) * P], rwT[:, d, :],
                                             start=(d == 0), stop=(d == DT - 1))
                    last.then_inc(l_done, 1)
                    pe.wait_ge(key_done, n + 1)
                    pe.wait_ge(keyT_out, n)
                    for j in range(CT // 2):
                        last = pe.transpose(ps[:, 3, j * P:(j + 1) * P],
                                            key[u][:, 2 * j:2 * j + 2, :].rearrange("p a e -> p (a e)"), m.ident[:, :])
                    last.then_inc(keyT_done, 1)

        @block.scalar
        def _(act):
            with act.Fori(0, B // 2) as i:
                for u in range(2):
                    n = 2 * i + u
                    act.wait_ge(tr_done, n + 1)
                    act.wait_ge(hT_kept, n)
                    act.wait_ge(l_done, n)
                    for d in range(DT):
                        act.activation(hT[u][:, d, :], ps[:, d, :], ACT.Copy).then_inc(hT_out, 1)
                    act.wait_ge(l_done, n + 1)
                    act.wait_ge(key_done, n)
                    act.activation(ex[u][:, :, :], ps[:, 2, 0:CT * E0].rearrange("p (t e) -> p t e", t=CT), ACT.Exp,
                                   scale=-1.0).then_inc(ex_done, 1)
                    act.wait_ge(keyT_done, n + 1)
                    act.activation(m.keyT[:, bass.ds(n * 2 * P, 2 * P)], ps[:, 3, 0:2 * P], ACT.Copy).then_inc(keyT_out, 1)

        LINKS = 4 * CT + 9

        @block.vector
        def _(dve):
            dve.memset(biased[:, :, E0:E0 + 2], NEG).then_inc(preset, 1)
            dve.memset(take8[:, :, K0:R8], NEG).then_inc(preset, 1)
            dve.wait_ge(preset, 2)
            dve.wait_ge(w_in, 32)
            dve.wait_ge(keyc_made, 1)

            with dve.Fori(0, B // 2) as i:
                for u in range(2):
                    n = 2 * i + u
                    at = [0]

                    def link(ins):
                        at[0] += 1
                        ins.then_inc(chain, 1)

                    def linked():
                        dve.wait_ge(chain, n * LINKS + at[0])

                    for j in range(CT):
                        link(dve.bn_stats(st[:, j, :], m.x[:, bass.ds(n * CT + j, 1), :]))
                    linked()
                    apart(m, dve)
                    for j in range(CT):
                        link(dve.bn_aggr(mv[:, j, :], st[:, j, :]))
                    linked()
                    dve.tensor_scalar(ve[:, :], mv[:, :, 1], EPS, None, ALU.add).then_inc(ve_done, 1)
                    dve.wait_ge(rstd_done, n + 1)
                    dve.wait_ge(row_out[u], 16 * i)
                    for j in range(CT):
                        dve.tensor_scalar(row[u][:, j, 0:D], m.x[:, bass.ds(n * CT + j, 1), :], mv[:, j, 0:1],
                                          rstd[:, j:j + 1], ALU.subtract, ALU.mult).then_inc(h_done, 1)
                    dve.wait_ge(ex_done, n + 1)
                    link(dve.tensor_scalar(ex1[:, :, :], ex[u][:, :, :], 1.0, None, ALU.add))
                    linked()
                    link(dve.reciprocal(score[:, :, :], ex1[:, :, :]))
                    linked()
                    link(dve.tensor_tensor(biased[:, :, 0:E0], score[:, :, :],
                                           bias[:, :].unsqueeze(1).to_broadcast([P, CT, E0]), ALU.add))
                    linked()
                    apart(m, dve)
                    for j in range(CT):
                        link(dve.max(top8[:, j, :], biased[:, j, :]))
                    linked()
                    link(dve.tensor_copy(take8[:, :, 0:K0], top8[:, :, 0:K0]))
                    linked()
                    apart(m, dve)
                    for j in range(CT):
                        link(dve.match_replace(left[:, j, :], take8[:, j, :], biased[:, j, :], LOW))
                    linked()
                    link(dve.tensor_scalar(chosen[:, :, :], left[:, :, 0:E0], LOW, None, ALU.is_equal))
                    linked()
                    dve.tensor_tensor(key[u][:, :, :], chosen[:, :, :],
                                      keyc[:, bass.ds(n * CT, CT)].unsqueeze(2).to_broadcast([P, CT, E0]), ALU.mult)\
                       .then_inc(key_done, 1)
                    link(dve.tensor_tensor(wgt[:, :, :], chosen[:, :, :], score[:, :, :], ALU.mult))
                    linked()
                    link(dve.tensor_reduce(wsum[:, :], wgt[:, :, :], AX.X, ALU.add))
                    linked()
                    link(dve.tensor_scalar(wsum[:, :], wsum[:, :], 1e-20, None, ALU.add))
                    linked()
                    link(dve.reciprocal(wrec[:, :], wsum[:, :]))
                    linked()
                    assert at[0] + 0 == LINKS, at[0]
                    dve.scalar_tensor_tensor(row[u][:, :, D:ROW], wgt[:, :, :], m.half_gate[:, 2:3],
                                             wrec[:, :].unsqueeze(2).to_broadcast([P, CT, E0]), ALU.mult, ALU.mult)\
                       .then_inc(row_done, 1)


def shared_0(nc, m):
    with ExitStack() as ctx:
        def sb(name, shape, dt=F32):
            return ctx.enter_context(nc.sbuf_tensor(name, shape, dt))

        def sem(name):
            return counter(nc, m, ctx, name)

        FT = SF // P
        w1 = sb("s_w1", [P, DT, SF])
        w2 = sb("s_w2", [P, FT, D])
        NG = 4
        sq = [sb(f"s_sq{u}", [P, S]) for u in range(2)]
        poly = [sb(f"s_poly{u}", [P, S]) for u in range(2)]
        arg = [sb(f"s_arg{u}", [P, S]) for u in range(2)]
        th = [sb(f"s_th{u}", [P, S]) for u in range(2)]
        g = [sb(f"s_g{u}", [P, FT, S]) for u in range(2)]
        eight = [sb(f"s_eight{r}", [P, R8]) for r in range(ROUNDS // (B // 2))]
        cand = sb("s_cand", [P, CAP])
        both = sb("s_both", [E0, 2 * CAP])
        first = sb("s_first", [E0, CAP])
        empty = sb("s_empty", [CAP, E0])
        slotp = sb("s_slotp", [CAP, 1])
        tok = sb("s_tok", [CAP, E0])
        tok2 = sb("s_tok2", [CAP, E0])
        ps = ctx.enter_context(nc.psum_tensor("s_ps", [P, 8, 512], F32))

        w_in = sem("s_w_in")
        slotp_made = sem("s_slotp_made")
        mid_done = sem("s_mid_done")
        sq_done = sem("s_sq_done")
        poly_done = sem("s_poly_done")
        arg_done = sem("s_arg_done")
        th_done = sem("s_th_done")
        g_done = sem("s_g_done")
        y_done = sem("s_y_done")
        x_done = sem("s_x_done")
        found = sem("s_found")
        kept = sem("s_kept")
        moved = sem("s_moved")
        firstT = sem("s_firstT")
        tok_step = sem("s_tok_step")
        block = ctx.enter_context(nc.Block())

        @block.sync
        def _(sp):
            sp.dma_start(w1[:, :, :], m.ins["sw1T"].rearrange("(t p) n -> p t n", p=P)).then_inc(w_in, 16)
            sp.dma_start(w2[:, :, :], m.ins["sw2T"].rearrange("(t p) n -> p t n", p=P)).then_inc(w_in, 16)
            sp.wait_ge(kept, ROUNDS)
            sp.dma_start(both[:, 0:CAP], cand[0:E0, :]).then_inc(moved, 16)
            sp.dma_start(both[:, CAP:2 * CAP], cand[E0:2 * E0, :]).then_inc(moved, 16)

        @block.gpsimd
        def _(pool):
            pool.iota(slotp[:, :], pattern=[[0, 1]], base=0, channel_multiplier=1,
                      allow_small_or_imprecise_dtypes=True).then_inc(slotp_made, 1)
            with pool.Fori(0, B) as n:
                for f in range(FT):
                    pool.wait_ge(sq_done, FT * n + f + 1)
                    pool.wait_ge(arg_done, FT * n + max(f - 1, 0))
                    apart(m, pool)
                    pool.tensor_scalar(poly[f % 2][:, :], sq[f % 2][:, :], GELU_A, 1.0, ALU.mult, ALU.add)\
                        .then_inc(poly_done, 1)

        @block.tensor
        def _(pe):
            pe.wait_ge(w_in, 32)
            with pe.Fori(0, B // 2) as i:
                for u in range(2):
                    n = 2 * i + u
                    for f in range(FT):
                        pe.wait_ge(g_done, FT * n)
                        for d in range(DT):
                            last = pe.matmul(ps[:, f, :], w1[:, d, f * P:(f + 1) * P],
                                             m.hT_all[:, d, bass.ds(n * S, S)], start=(d == 0), stop=(d == DT - 1))
                        last.then_inc(mid_done, 1)
                    pe.wait_ge(g_done, FT * n + FT)
                    for t in range(CT):
                        pe.wait_ge(x_done, CT * n)
                        for f in range(FT):
                            last = pe.matmul(ps[:, 4 + t, 0:D], g[u][:, f, t * P:(t + 1) * P], w2[:, f, :],
                                             start=(f == 0), stop=(f == FT - 1))
                        last.then_inc(y_done, 1)
            pe.wait_ge(found, 4 * ROUNDS)
            pe.wait_ge(x_done, CT * B)
            pe.transpose(ps[0:CAP, 4, 0:E0], first[:, :], m.ident[0:E0, 0:E0]).then_inc(firstT, 1)

        @block.scalar
        def _(act):
            with act.Fori(0, B) as n:
                for f in range(FT + 1):
                    if f < FT:
                        act.wait_ge(mid_done, FT * n + f + 1)
                        act.wait_ge(poly_done, FT * n + max(f - 1, 0))
                        act.activation(sq[f % 2][:, :], ps[:, f, :], ACT.Square).then_inc(sq_done, 1)
                    if f:
                        act.wait_ge(arg_done, FT * n + f)
                        act.wait_ge(g_done, FT * n + max(f - 2, 0))
                        act.activation(th[(f - 1) % 2][:, :], arg[(f - 1) % 2][:, :], ACT.Tanh, scale=GELU_C)\
                           .then_inc(th_done, 1)

        @block.vector
        def _(dve):
            def find(keys, out, at):
                dve.wait_ge(found, at)
                apart(m, dve)
                dve.max(out, keys).then_inc(found, 1)
                dve.wait_ge(found, at + 1)
                apart(m, dve)
                dve.match_replace(keys, out, keys, 0.0).then_inc(found, 1)

            per_pass = ROUNDS // (B // 2)
            with dve.Fori(0, B // 2) as i:
                for u in range(2):
                    n = 2 * i + u
                    for f in range(FT + 1):
                        if f < FT:
                            dve.wait_ge(poly_done, FT * n + f + 1)
                            dve.wait_ge(th_done, FT * n + max(f - 1, 0))
                            dve.tensor_tensor(arg[f % 2][:, :], poly[f % 2][:, :], ps[:, f, :], ALU.mult).then_inc(arg_done, 1)
                        if f:
                            dve.wait_ge(th_done, FT * n + f)
                            dve.wait_ge(y_done, CT * n)
                            dve.scalar_tensor_tensor(g[u][:, f - 1, :], th[(f - 1) % 2][:, :], 1.0, ps[:, f - 1, :],
                                                     ALU.add, ALU.mult).then_inc(g_done, 1)
                    for r in range(per_pass * u // 2 + 0, per_pass * (u + 1) // 2):
                        find(m.keyT[:, :], eight[r][:, :], 2 * (per_pass * i + r))
                        dve.tensor_copy(cand[:, bass.ds((per_pass * i + r) * R8, R8)], eight[r][:, :]).then_inc(kept, 1)
                    for t in range(CT):
                        dve.wait_ge(y_done, CT * n + t + 1)
                        xt = m.x[:, bass.ds(n * CT + t, 1), :]
                        dve.scalar_tensor_tensor(xt, ps[:, 4 + t:5 + t, 0:D], m.half_gate[:, 2:3], xt, ALU.mult, ALU.add)\
                           .then_inc(x_done, 1)
            dve.wait_ge(moved, 32)
            for r in range(ROUNDS):
                find(both[:, :], first[:, r * R8:(r + 1) * R8], 2 * ROUNDS + 2 * r)
            dve.wait_ge(firstT, 1)
            dve.wait_ge(slotp_made, 1)
            dve.tensor_scalar(empty[:, :], ps[0:CAP, 4, 0:E0], 0.0, slotp[:, 0:1], ALU.is_equal, ALU.mult).then_inc(tok_step, 1)
            dve.tensor_scalar(tok[:, :], ps[0:CAP, 4, 0:E0], -1.0, float(T), ALU.mult, ALU.add).then_inc(tok_step, 1)
            dve.wait_ge(tok_step, 2)
            dve.tensor_tensor(tok2[:, :], tok[:, :], empty[:, :], ALU.add).then_inc(tok_step, 1)
            dve.wait_ge(tok_step, 3)
            dve.tensor_copy(m.slots0[:, :], tok2[:, :]).then_inc(tok_step, 1)
            dve.wait_ge(tok_step, 4)


def experts_0(nc, m):
    NB = 8
    AHEAD = 4
    with ExitStack() as ctx:
        def sb(name, shape, dt=F32):
            return ctx.enter_context(nc.sbuf_tensor(name, shape, dt))

        def sem(name):
            return counter(nc, m, ctx, name)

        w1 = [sb(f"e_w1{u}", [P, DT, F0]) for u in range(NB)]
        w2 = [sb(f"e_w2{u}", [P, D]) for u in range(NB)]
        idx = [sb(f"e_idx{u}", [CAP, 1], I32) for u in range(NB)]
        xg = [sb(f"e_xg{u}", [CAP, ROW]) for u in range(NB)]
        xgT = [sb(f"e_xgT{u}", [P, DT, CAP]) for u in range(2)]
        mid = [sb(f"e_mid{u}", [P, CAP]) for u in range(2)]
        sq = [sb(f"e_sq{u}", [P, CAP]) for u in range(2)]
        poly = [sb(f"e_poly{u}", [P, CAP]) for u in range(2)]
        arg = [sb(f"e_arg{u}", [P, CAP]) for u in range(2)]
        th = [sb(f"e_th{u}", [P, CAP]) for u in range(2)]
        g = [sb(f"e_g{u}", [P, CAP]) for u in range(2)]
        y = [sb(f"e_y{u}", [CAP, D]) for u in range(NB)]
        ps = ctx.enter_context(nc.psum_tensor("e_ps", [P, 8, 512], F32))

        w_in = [sem(f"e_w_in{u}") for u in range(NB)]
        idx_done = sem("e_idx_done")
        x_in = [sem(f"e_x_in{u}") for u in range(NB)]
        xT_done = sem("e_xT_done")
        xT_out = sem("e_xT_out")
        mid_done = sem("e_mid_done")
        mid_out = sem("e_mid_out")
        step = sem("e_step")
        th_done = sem("e_th_done")
        g_done = sem("e_g_done")
        y_done = sem("e_y_done")
        y_out = sem("e_y_out")
        added = [sem(f"e_added{u}") for u in range(NB)]
        block = ctx.enter_context(nc.Block())

        def experts(eng, body):
            with eng.Fori(0, E0 // NB - 1) as i:
                for u in range(NB):
                    body(NB * i + u, i, u)
            for u in range(NB):
                body(E0 - NB + u, E0 // NB - 1, u)

        def there(e):
            return not (isinstance(e, int) and e >= E0)

        @block.sync
        def _(sp):
            with sp.Fori(0, E0 // NB) as i:
                for u in range(NB):
                    e = NB * i + u
                    sp.wait_ge(added[u], 16 * i)
                    sp.dma_start(w1[u][:, :, :], m.ins["w1"][bass.ds(e, 1)].rearrange("a (t p) f -> p (a t) f", p=P)).then_inc(w_in[u], 16)
                    sp.dma_start(w2[u][:, :], m.ins["w2"][bass.ds(e, 1)].rearrange("a f d -> f (a d)")).then_inc(w_in[u], 16)

        @block.gpsimd
        def _(pool):
            def gather(e, u):
                pool.wait_ge(idx_done, e + 1)
                apart(m, pool)
                pool.indirect_dma_start(xg[u][:, :], None, m.rows[:, :],
                                        bass.IndirectOffsetOnAxis(ap=idx[u][:, :], axis=0)).then_inc(x_in[u], 16)

            for e in range(AHEAD):
                gather(e, e)

            def body(e, i, u):
                if there(e + AHEAD):
                    gather(e + AHEAD, (u + AHEAD) % NB)
                pool.wait_ge(y_out, e + 1)
                if u >= 2:
                    pool.wait_ge(added[u - 2], 16 * i + 16)
                else:
                    pool.wait_ge(added[NB + u - 2], 16 * i)
                apart(m, pool)
                pool.indirect_dma_start(m.acc[u % 2], bass.IndirectOffsetOnAxis(ap=idx[u][:, :], axis=0),
                                        y[u][:, :], None, compute_op=ALU.add).then_inc(added[u], 16)

            experts(pool, body)
            for u in range(NB):
                pool.wait_ge(added[u], 16 * (E0 // NB))

        @block.tensor
        def _(pe):
            def rows(e, i, u):
                v = u % 2
                pe.wait_ge(x_in[u], 16 * i + 16)
                if not (isinstance(e, int) and e < 2):
                    pe.wait_ge(xT_out, e - 1)
                for d in range(DT):
                    last = pe.transpose(ps[:, v, d * P:d * P + CAP], xg[u][:, d * P:(d + 1) * P], m.ident[0:CAP, 0:CAP])
                last.then_inc(xT_done, 1)

            def first_layer(e, i, u):
                v = u % 2
                pe.wait_ge(xT_out, e + 1)
                pe.wait_ge(w_in[u], 32 * i + 32)
                if not (isinstance(e, int) and e < 2):
                    pe.wait_ge(mid_out, e - 1)
                for d in range(DT):
                    last = pe.matmul(ps[:, 2 + v, 0:CAP], w1[u][:, d, :], xgT[v][:, d, :],
                                     start=(d == 0), stop=(d == DT - 1))
                last.then_inc(mid_done, 1)

            rows(0, 0, 0)
            rows(1, 0, 1)
            first_layer(0, 0, 0)

            def body(e, i, u):
                v = u % 2
                if there(e + 2):
                    rows(e + 2, i + (u + 2) // NB, (u + 2) % NB)
                if there(e + 1):
                    first_layer(e + 1, i + (u + 1) // NB, (u + 1) % NB)
                pe.wait_ge(g_done, e + 1)
                if u >= 2:
                    pe.wait_ge(y_out, e - 1)
                elif not (isinstance(i, int) and i == 0):
                    pe.wait_ge(y_out, e)
                pe.matmul(ps[0:CAP, 4 + v, 0:D], g[v][:, :], w2[u][:, :], start=True, stop=True).then_inc(y_done, 1)

            experts(pe, body)

        @block.scalar
        def _(act):
            def rows(e, v):
                act.wait_ge(xT_done, e + 1)
                if not (isinstance(e, int) and e < 2):
                    act.wait_ge(mid_done, e - 1)
                act.activation(xgT[v][:, :, :], ps[:, v, 0:DT * P].rearrange("p (d c) -> p d c", d=DT)[:, :, 0:CAP],
                               ACT.Copy).then_inc(xT_out, 1)

            def hidden(e, v):
                act.wait_ge(mid_done, e + 1)
                if not (isinstance(e, int) and e < 2):
                    act.wait_ge(g_done, e - 1)
                act.activation(mid[v][:, :], ps[:, 2 + v, 0:CAP], ACT.Copy).then_inc(mid_out, 1)

            def tanh(e, v):
                act.wait_ge(step, 3 * e + 3)
                act.activation(th[v][:, :], arg[v][:, :], ACT.Tanh, scale=GELU_C).then_inc(th_done, 1)

            rows(0, 0)
            rows(1, 1)
            hidden(0, 0)
            tanh(0, 0)

            def body(e, i, u):
                v = u % 2
                if there(e + 2):
                    rows(e + 2, v)
                if there(e + 1):
                    hidden(e + 1, 1 - v)
                act.wait_ge(y_done, e + 1)
                act.wait_ge(added[u], 16 * i)
                act.wait_ge(x_in[u], 16 * i + 16)
                act.activation(y[u][:, :], ps[0:CAP, 4 + v, 0:D], ACT.Copy, scale=xg[u][:, bass.ds(D + e, 1)])\
                   .then_inc(y_out, 1)
                if there(e + 1):
                    tanh(e + 1, 1 - v)

            experts(act, body)

        @block.vector
        def _(dve):
            def index(e, i, u):
                if not (isinstance(i, int) and i == 0):
                    dve.wait_ge(added[u], 16 * i)
                dve.tensor_copy(idx[u][:, :], m.slots0[:, bass.ds(e, 1)]).then_inc(idx_done, 1)

            def gelu(e, v):
                dve.wait_ge(mid_out, e + 1)
                dve.tensor_tensor(sq[v][:, :], mid[v][:, :], mid[v][:, :], ALU.mult).then_inc(step, 1)
                dve.wait_ge(step, 3 * e + 1)
                dve.tensor_scalar(poly[v][:, :], sq[v][:, :], GELU_A, 1.0, ALU.mult, ALU.add).then_inc(step, 1)
                dve.wait_ge(step, 3 * e + 2)
                dve.tensor_tensor(arg[v][:, :], poly[v][:, :], mid[v][:, :], ALU.mult).then_inc(step, 1)
                dve.wait_ge(th_done, e + 1)
                if not (isinstance(e, int) and e < 2):
                    dve.wait_ge(y_done, e - 1)
                dve.scalar_tensor_tensor(g[v][:, :], th[v][:, :], 1.0, mid[v][:, :], ALU.add, ALU.mult).then_inc(g_done, 1)

            for e in range(AHEAD):
                index(e, 0, e)
            gelu(0, 0)

            def body(e, i, u):
                if there(e + AHEAD):
                    index(e + AHEAD, i + (u + AHEAD) // NB, (u + AHEAD) % NB)
                if there(e + 1):
                    gelu(e + 1, (u + 1) % 2)

            experts(dve, body)


H1, HD = 16, 16
HG = 4
NGRP = H1 // HG
PARTS = 3
KS = 6 * HD
Q_BANDS = (0, 1, 2, 0, 1, 0)
K_BANDS = (0, 0, 0, 1, 1, 2)
VW = 32


def project_1(nc, m):
    with ExitStack() as ctx:
        def sb(name, shape, dt=F32):
            return ctx.enter_context(nc.sbuf_tensor(name, shape, dt))

        def sem(name):
            return counter(nc, m, ctx, name)

        acc = [[sb(f"p_acc{a}{u}", [P, CT, D]) for u in range(2)] for a in range(2)]
        cT = [sb(f"p_cT{u}", [P, DT, S]) for u in range(2)]
        h = sb("p_h", [P, CT, D])
        hT = sb("p_hT", [P, DT, S])
        wq = sb("p_wq", [P, DT, D])
        wk = sb("p_wk", [P, DT, D])
        wv = sb("p_wv", [P, DT, D])
        qkb = sb("p_qkb", [P, 2, DT])
        vb = sb("p_vb", [P, D])
        st = sb("p_st", [P, CT, 6])
        mv = sb("p_mv", [P, CT, 2])
        ve = sb("p_ve", [P, CT])
        rstd = sb("p_rstd", [P, CT])
        full = [sb(f"p_full{a}", [P, DT, S]) for a in range(2)]
        rest = [sb(f"p_rest{a}", [P, DT, S]) for a in range(2)]
        part = [[sb(f"p_part{a}{c}", [P, DT, S], BF16) for c in range(PARTS)] for a in range(2)]
        v = [sb(f"p_v{u}", [P, CT, H1, VW]) for u in range(2)]
        ps = ctx.enter_context(nc.psum_tensor("p_ps", [P, 8, 512], F32))

        w_in = sem("p_w_in")
        b_in = sem("p_b_in")
        acc_in = [sem(f"p_acc_in{u}") for u in range(2)]
        ctx_in = [sem(f"p_ctx_in{u}") for u in range(2)]
        preset = sem("p_preset")
        chain = sem("p_chain")
        x_done = sem("p_x_done")
        ve_done = sem("p_ve_done")
        rstd_done = sem("p_rstd_done")
        h_done = sem("p_h_done")
        tr_done = sem("p_tr_done")
        hT_out = sem("p_hT_out")
        q_done = sem("p_q_done")
        k_done = sem("p_k_done")
        v_done = sem("p_v_done")
        full_done = [sem(f"p_full_done{a}") for a in range(2)]
        hi_done = [sem(f"p_hi_done{a}") for a in range(2)]
        rest_done = [sem(f"p_rest_done{a}") for a in range(2)]
        mid_done = [sem(f"p_mid_done{a}") for a in range(2)]
        lo_done = [sem(f"p_lo_done{a}") for a in range(2)]
        part_out = [sem(f"p_part_out{a}") for a in range(2)]
        v_out = sem("p_v_out")
        v_stored = [sem(f"p_v_stored{u}") for u in range(2)]
        block = ctx.enter_context(nc.Block())

        def chunks(eng, body):
            with eng.Fori(0, B // 2 - 1) as i:
                for u in range(2):
                    body(2 * i + u, i, u, True)
            for u in range(2):
                body(B - 2 + u, B // 2 - 1, u, u == 0)

        @block.sync
        def _(sp):
            def load_acc(n, u):
                for a in range(2):
                    sp.dma_start(acc[a][u][:, :, :], m.acc[a][0:T, :].rearrange("(c t p) d -> p c t d", p=P, t=CT)
                                 [:, bass.ds(n, 1)].rearrange("p a t d -> p (a t) d")).then_inc(acc_in[u], 16)

            def load_ctx(n, u):
                sp.dma_start(cT[u][:, :, :], m.ins["ctxT"].rearrange("(t p) n -> p t n", p=P)[:, :, bass.ds(n * S, S)])\
                  .then_inc(ctx_in[u], 16)

            def store(a, n):
                sp.wait_ge(hi_done[a], n + 1)
                apart(m, sp)
                sp.wait_ge(mid_done[a], n + 1)
                sp.wait_ge(lo_done[a], n + 1)
                for c in range(PARTS):
                    dst = m.qk[a].rearrange("b c (t p) s -> p b c t s", p=P)[:, bass.ds(n, 1), c]
                    sp.dma_start(dst.rearrange("p b t s -> p (b t) s"), part[a][c][:, :, :]).then_inc(part_out[a], 16)

            load_acc(0, 0)
            load_ctx(0, 0)
            for w, name in ((wk, "WkT1"), (wv, "WvT1"), (wq, "WqT1")):
                sp.dma_start(w[:, :, :], m.ins[name].rearrange("(t p) n -> p t n", p=P)).then_inc(w_in, 16)
            load_acc(1, 1)
            load_ctx(1, 1)

            def body(n, i, u, ahead):
                more = not isinstance(i, int)
                if more:
                    sp.wait_ge(x_done, n + 1)
                    load_acc(n + 2, u)
                store(1, n)
                sp.wait_ge(v_out, 2 * n + 2)
                sp.dma_start(m.v.rearrange("(c t p) e -> p c t e", p=P, t=CT)[:, bass.ds(n, 1)]
                             .rearrange("p a t e -> p (a t) e"), v[u][:, :, :, :].rearrange("p t h w -> p t (h w)"))\
                  .then_inc(v_stored[u], 16)
                if more:
                    sp.wait_ge(v_done, 2 * n + 2)
                    load_ctx(n + 2, u)
                store(0, n)

            chunks(sp, body)
            for a in range(2):
                sp.wait_ge(part_out[a], 16 * PARTS * B)
            for u in range(2):
                sp.wait_ge(v_stored[u], 16 * (B // 2))

        @block.gpsimd
        def _(pool):
            for u in range(2):
                pool.memset(v[u][:, :, :, HD:VW], 0.0).then_inc(preset, 1)
            pool.wait_ge(preset, 2)
            for u in range(2):
                pool.memset(v[u][:, :, :, HD:HD + 1], 1.0).then_inc(preset, 1)
            with pool.Fori(0, B) as n:
                pool.wait_ge(ve_done, n + 1)
                pool.tensor_tensor(rstd[:, :], ve[:, :], m.minus_half[:, 0:CT], ALU.pow).then_inc(rstd_done, 1)

        @block.tensor
        def _(pe):
            pe.wait_ge(w_in, 48)

            def body(n, i, u, ahead):
                pe.wait_ge(hT_out, DT * n)
                for j in range(CT):
                    pe.wait_ge(h_done, CT * n + j + 1)
                    for d in range(DT):
                        last = pe.transpose(ps[:, d, j * P:(j + 1) * P], h[:, j, d * P:(d + 1) * P], m.ident[:, :])
                last.then_inc(tr_done, 1)
                pe.wait_ge(ctx_in[u], 16 * i + 16)
                pe.wait_ge(full_done[1], DT * n)
                for e in range(DT):
                    for d in range(DT):
                        last = pe.matmul(ps[:, 4 + e, :], wk[:, d, e * P:(e + 1) * P], cT[u][:, d, :],
                                         start=(d == 0), stop=(d == DT - 1))
                    last.then_inc(k_done, 1)
                pe.wait_ge(v_out, 2 * n)
                for t in range(CT):
                    for d in range(DT):
                        last = pe.matmul(ps[:, 6 + t // 2, (t % 2) * D:(t % 2 + 1) * D], cT[u][:, d, t * P:(t + 1) * P],
                                         wv[:, d, :], start=(d == 0), stop=(d == DT - 1))
                    if t % 2:
                        last.then_inc(v_done, 1)
                pe.wait_ge(hT_out, DT * (n + 1))
                pe.wait_ge(full_done[0], DT * n)
                for e in range(DT):
                    for d in range(DT):
                        last = pe.matmul(ps[:, 2 + e, :], wq[:, d, e * P:(e + 1) * P], hT[:, d, :],
                                         start=(d == 0), stop=(d == DT - 1))
                    last.then_inc(q_done, 1)

            chunks(pe, body)

        @block.scalar
        def _(act):
            act.dma_start(qkb[:, 0, :], m.ins["bq"]).then_inc(b_in, 16)
            act.dma_start(qkb[:, 1, :], m.ins["bk"]).then_inc(b_in, 16)
            act.dma_start(vb[:, :], m.ins["bv"].rearrange("(a n) -> a n", a=1).to_broadcast([P, D])).then_inc(b_in, 16)
            act.wait_ge(b_in, 48)

            def body(n, i, u, ahead):
                def biased(a, done):
                    act.wait_ge(rest_done[a], n)
                    for e in range(DT):
                        act.wait_ge(done, DT * n + e + 1)
                        act.activation(full[a][:, e, :], ps[:, (2, 4)[a] + e, :], ACT.Identity, bias=qkb[:, a, e:e + 1])\
                           .then_inc(full_done[a], 1)

                def part_0(a):
                    act.wait_ge(full_done[a], DT * (n + 1))
                    act.wait_ge(part_out[a], 16 * PARTS * n)
                    act.activation(part[a][0][:, :, :], full[a][:, :, :], ACT.Copy).then_inc(hi_done[a], 1)

                def part_1(a):
                    act.wait_ge(rest_done[a], n + 1)
                    act.activation(part[a][1][:, :, :], rest[a][:, :, :], ACT.Copy).then_inc(mid_done[a], 1)

                act.wait_ge(tr_done, n + 1)
                act.wait_ge(q_done, DT * n)
                for d in range(DT):
                    act.activation(hT[:, d, :], ps[:, d, :], ACT.Copy).then_inc(hT_out, 1)
                biased(1, k_done)
                part_0(1)
                part_1(1)
                biased(0, q_done)
                part_0(0)
                part_1(0)

            chunks(act, body)

        LINKS = 1 + 2 * CT

        @block.vector
        def _(dve):
            def statistics(n, i, u):
                at = [0]

                def link(ins):
                    at[0] += 1
                    ins.then_inc(chain, 1)

                def linked():
                    dve.wait_ge(chain, n * LINKS + at[0])

                xc = m.x[:, bass.ds(n * CT, CT), :]
                dve.wait_ge(acc_in[u], 32 * i + 32)
                link(dve.tensor_tensor(xc, xc, acc[0][u][:, :, :], ALU.add))
                linked()
                dve.tensor_tensor(xc, xc, acc[1][u][:, :, :], ALU.add).then_inc(x_done, 1)
                dve.wait_ge(x_done, n + 1)
                apart(m, dve)
                for j in range(CT):
                    link(dve.bn_stats(st[:, j, :], m.x[:, bass.ds(n * CT + j, 1), :]))
                linked()
                apart(m, dve)
                for j in range(CT):
                    link(dve.bn_aggr(mv[:, j, :], st[:, j, :]))
                linked()
                assert at[0] == LINKS
                dve.tensor_scalar(ve[:, :], mv[:, :, 1], EPS, None, ALU.add).then_inc(ve_done, 1)

            def normalised(n):
                dve.wait_ge(rstd_done, n + 1)
                if not (isinstance(n, int) and n == 0):
                    dve.wait_ge(tr_done, n)
                for j in range(CT):
                    dve.tensor_scalar(h[:, j, :], m.x[:, bass.ds(n * CT + j, 1), :], mv[:, j, 0:1],
                                      rstd[:, j:j + 1], ALU.subtract, ALU.mult).then_inc(h_done, 1)

            statistics(0, 0, 0)
            normalised(0)
            dve.wait_ge(preset, 4)
            dve.wait_ge(b_in, 48)

            def body(n, i, u, ahead):
                def remainders(a):
                    dve.wait_ge(hi_done[a], n + 1)
                    dve.tensor_tensor(rest[a][:, :, :], full[a][:, :, :], part[a][0][:, :, :], ALU.subtract)\
                       .then_inc(rest_done[a], 1)

                def last_part(a):
                    dve.wait_ge(mid_done[a], n + 1)
                    dve.tensor_tensor(part[a][2][:, :, :], rest[a][:, :, :], part[a][1][:, :, :], ALU.subtract)\
                       .then_inc(lo_done[a], 1)

                if ahead:
                    statistics(n + 1, i + u, 1 - u)
                remainders(1)
                if ahead:
                    normalised(n + 1)
                for w in range(2):
                    dve.wait_ge(v_done, 2 * n + w + 1)
                    if w == 0:
                        dve.wait_ge(v_stored[u], 16 * i)
                    dve.tensor_tensor(v[u][:, 2 * w:2 * w + 2, :, 0:HD],
                                      ps[:, 6 + w, :].rearrange("p (t h w) -> p t h w", t=2, w=HD),
                                      vb[:, :].rearrange("p (a h w) -> p a h w", a=1, w=HD).to_broadcast([P, 2, H1, HD]),
                                      ALU.add).then_inc(v_out, 1)
                last_part(1)
                remainders(0)
                last_part(0)

            chunks(dve, body)


def attention_1(nc, m):
    GROUPS = B * NGRP
    NB = 4
    NBANK = 3
    NPR = 8
    LAG_T, LAG_O = 6, 7
    STEPS = CT * HG
    MR = PARTS * HG
    with ExitStack() as ctx:
        def sb(name, shape, dt=F32):
            return ctx.enter_context(nc.sbuf_tensor(name, shape, dt))

        def sem(name):
            return counter(nc, m, ctx, name)

        qs = [sb(f"t_qs{g}", [P, HG, S], BF16) for g in range(NB)]
        ks = [sb(f"t_ks{g}", [P, HG, S], BF16) for g in range(NB)]
        va = [sb(f"t_va{g}", [P, CT, HG * VW]) for g in range(NB)]
        pr = sb("t_pr", [P, NPR, S])
        nm = [sb(f"t_nm{u}", [P, STEPS]) for u in range(2)]
        nr = [sb(f"t_nr{w}", [P, STEPS]) for w in range(2)]
        n3 = [sb(f"t_n3{u}", [P, STEPS, PARTS], BF16) for u in range(2)]
        mT = sb("t_mT", [P, S], BF16)
        pick = sb("t_pick", [P, HG], BF16)
        ot = [sb(f"t_ot{u}", [P, S]) for u in range(2)]
        rec = [sb(f"t_rec{u}", [P, STEPS]) for u in range(2)]
        ps = ctx.enter_context(nc.psum_tensor("t_ps", [P, 8, 512], F32))
        O, X = 2 * NBANK, 2 * NBANK + 1

        preset = sem("t_preset")
        picked = sem("t_picked")
        q_in = [sem(f"t_q_in{g}") for g in range(NB)]
        k_in = [sem(f"t_k_in{g}") for g in range(NB)]
        s_done = sem("t_s_done")
        max_done = sem("t_max_done")
        cut = sem("t_cut")
        mT_done = sem("t_mT_done")
        mT_out = sem("t_mT_out")
        mT_spread = sem("t_mT_spread")
        z_done = sem("t_z_done")
        p_done = sem("t_p_done")
        o_done = sem("t_o_done")
        pv_done = sem("t_pv_done")
        ot_out = sem("t_ot_out")
        oT_done = sem("t_oT_done")
        rec_done = sem("t_rec_done")
        att_done = sem("t_att_done")
        block = ctx.enter_context(nc.Block())

        def parts(eng, part, last=GROUPS + 2):
            def whole(k):
                part(k, k // NB + 1, k % NB, (k - 2) // NGRP, (k < GROUPS, 1 <= k < GROUPS + 1, k >= 2))
            whole(0)
            whole(1)
            with eng.Fori(0, (GROUPS - NB) // NB) as i:
                for w in range(NB):
                    part(NB * i + 2 + w, i + (2 + w) // NB + 1, (2 + w) % NB, i, (True, True, True))
            for k in range(GROUPS - 2, last):
                whole(k)

        def lagged(k, b, lag):
            back = -((b - lag) // CT)
            return back, (b - lag) % CT

        @block.sync
        def _(sp):
            def load(g, n):
                def rows(a, c):
                    whole = m.qk[a].rearrange("b c (g j d) s -> b c g d j s", g=NGRP, d=HD)
                    return whole[bass.ds(n, 1), c, g].rearrange("a d j s -> (a d) j s")
                for r, c in enumerate(Q_BANDS):
                    sp.dma_start(qs[g][r * HD:(r + 1) * HD, :, :], rows(0, c)).then_inc(q_in[g], 16)
                for r, c in enumerate(K_BANDS):
                    sp.dma_start(ks[g][r * HD:(r + 1) * HD, :, :], rows(1, c)).then_inc(k_in[g], 16)
                src = m.v.rearrange("(b t p) (g e) -> p b g t e", p=P, t=CT, g=NGRP)
                sp.dma_start(va[g][:, :, :], src[:, bass.ds(n, 1), g].rearrange("p a t e -> p (a t) e"))\
                  .then_inc(k_in[g], 16)

            for g in range(NB):
                load(g, 0)

            def part(k, turn, g, n, live):
                if live[1]:
                    sp.wait_ge(mT_out, k)
                    sp.dma_start(qs[(g - 1) % NB][KS:KS + MR, :, :],
                                 mT[KS:KS + MR, :].unsqueeze(1).to_broadcast([MR, HG, S])).then_inc(mT_spread, 16)
                if live[2] and not (isinstance(k, int) and k + 2 >= GROUPS):
                    sp.wait_ge(o_done, k - 1)
                    load((g + 2) % NB, n + 1)

            parts(sp, part, GROUPS + 1)

        @block.gpsimd
        def _(pool):
            pool.memset(pick[KS:P, :], 0.0).then_inc(preset, 1)
            for c in range(PARTS):
                pool.wait_ge(preset, c + 1)
                pool.affine_select(out=pick[KS:P, :], in_=pick[KS:P, :], compare_op=ALU.not_equal, fill=1.0,
                                   base=-c, pattern=[[-PARTS, HG]], channel_multiplier=1).then_inc(preset, 1)

            def part(k, turn, g, n, live):
                if live[0]:
                    u = g % 2
                    pool.wait_ge(max_done, STEPS * (k + 1))
                    at_least(pool, mT_done, k - 1)
                    apart(m, pool)
                    pool.tensor_copy(n3[u][:, :, 0], nm[u][:, :]).then_inc(cut, 1)
                    pool.wait_ge(cut, 5 * k + 1)
                    pool.tensor_tensor(nr[0][:, :], nm[u][:, :], n3[u][:, :, 0], ALU.subtract).then_inc(cut, 1)
                    pool.wait_ge(cut, 5 * k + 2)
                    apart(m, pool)
                    pool.tensor_copy(n3[u][:, :, 1], nr[0][:, :]).then_inc(cut, 1)
                    pool.wait_ge(cut, 5 * k + 3)
                    pool.tensor_tensor(nr[1][:, :], nr[0][:, :], n3[u][:, :, 1], ALU.subtract).then_inc(cut, 1)
                    pool.wait_ge(cut, 5 * k + 4)
                    apart(m, pool)
                    pool.tensor_copy(n3[u][:, :, 2], nr[1][:, :]).then_inc(cut, 1)

            parts(pool, part, GROUPS)

        @block.tensor
        def _(pe):
            def maxima_scores(k, turn, g, b, j):
                if b == 0 and j == 0:
                    pe.wait_ge(q_in[g], 16 * 6 * turn)
                    pe.wait_ge(k_in[g], 16 * 7 * turn)
                x = HG * b + j
                at_least(pe, max_done, STEPS * k + (0 if x < NBANK else x - NBANK + 1))
                pe.matmul(ps[:, x % NBANK, :], qs[g][0:KS, j, b * P:(b + 1) * P], ks[g][0:KS, j, :],
                          start=True, stop=True).then_inc(s_done, 1)

            def probability_scores(k, g, b, j):
                if b == 0 and j == 0:
                    if isinstance(k, int) and k < NB:
                        pe.wait_ge(picked, k + 1)
                    pe.wait_ge(mT_spread, 16 * (k + 1))
                x = HG * b + j
                at_least(pe, p_done, STEPS * k + (0 if x < NBANK else x - NBANK + 1))
                pe.matmul(ps[:, NBANK + x % NBANK, :], ks[g][0:KS + MR, j, b * P:(b + 1) * P], qs[g][0:KS + MR, j, :],
                          start=True, stop=True).then_inc(z_done, 1)

            def times_v(k, g, b):
                if b == 0:
                    at_least(pe, ot_out, k)
                pe.wait_ge(p_done, STEPS * k + HG * b + HG)
                for j in range(HG):
                    last = pe.matmul(ps[j * VW:(j + 1) * VW, O, :], va[g][:, b, j * VW:(j + 1) * VW],
                                     pr[:, (HG * b + j) % NPR, :], start=(b == 0), stop=(b == CT - 1),
                                     tile_position=(0, j * VW))
                if b == CT - 1:
                    last.then_inc(o_done, 1)
                else:
                    last.then_inc(pv_done, 1)

            def maxima_rows(k, g):
                pe.wait_ge(cut, 5 * k + 5)
                at_least(pe, att_done, k - 1)
                for t in range(CT):
                    last = pe.transpose(ps[KS:KS + MR, X, 0:S // 2].bitcast(BF16)[:, t * P:(t + 1) * P],
                                        n3[g % 2][:, HG * t:HG * (t + 1), :].rearrange("p j c -> p (j c)"),
                                        m.ident_bf[:, :], tile_position=(0, KS))
                last.then_inc(mT_done, 1)

            def sums_rows(k, g):
                pe.wait_ge(ot_out, k + 1)
                at_least(pe, att_done, k)
                pe.wait_ge(mT_out, min(k + 2, GROUPS) if isinstance(k, int) else k + 2)
                for t in range(CT):
                    last = pe.transpose(ps[:, X, t * P:(t + 1) * P], ot[g % 2][:, t * P:(t + 1) * P], m.ident[:, :])
                last.then_inc(oT_done, 1)

            def part(k, turn, g, n, live):
                for b in range(CT):
                    back, tb = lagged(k, b, LAG_T)
                    for j in range(HG):
                        if live[0]:
                            maxima_scores(k, turn, g, b, j)
                        if live[back]:
                            probability_scores(k - back, (g - back) % NB, tb, j)
                    back, ob = lagged(k, b, LAG_O)
                    if live[back]:
                        times_v(k - back, (g - back) % NB, ob)
                    if b == 0 and live[1]:
                        maxima_rows(k - 1, (g - 1) % NB)
                    if b == CT - 1 and live[2]:
                        sums_rows(k - 2, (g - 2) % NB)

            parts(pe, part)

        @block.scalar
        def _(act):
            def probabilities(k, g, b):
                for j in range(HG):
                    x = HG * b + j
                    act.wait_ge(z_done, STEPS * k + x + 1)
                    if j == 0:
                        pr_free(k, b)
                    act.activation(pr[:, x % NPR, :], ps[:, NBANK + x % NBANK, :], ACT.Exp, scale=float(HD) ** -0.5)\
                       .then_inc(p_done, 1)

            def pr_free(k, b):
                if b >= 2:
                    at_least(act, pv_done, (CT - 1) * k + b - 1)
                elif b == 1:
                    at_least(act, o_done, k)
                else:
                    at_least(act, pv_done, (CT - 1) * k)

            def part(k, turn, g, n, live):
                for b in range(CT):
                    back, tb = lagged(k, b, LAG_T)
                    if live[back]:
                        probabilities(k - back, (g - back) % NB, tb)
                    back, ob = lagged(k, b, LAG_O)
                    if live[back] and ob == CT - 1:
                        kk = k - back
                        act.wait_ge(o_done, kk + 1)
                        at_least(act, oT_done, kk)
                        act.activation(ot[(g - back) % 2][:, :], ps[:, O, :], ACT.Copy).then_inc(ot_out, 1)

            parts(act, part)

        @block.vector
        def _(dve):
            dve.wait_ge(preset, 1 + PARTS)
            for g in range(NB):
                dve.tensor_copy(ks[g][KS:P, :, :], pick[KS:P, :].unsqueeze(2).to_broadcast([P - KS, HG, S]))\
                   .then_inc(picked, 1)

            def maxima_parts_out(k):
                dve.wait_ge(mT_done, k + 1)
                at_least(dve, mT_spread, 16 * k)
                dve.tensor_copy(mT[KS:KS + MR, :], ps[KS:KS + MR, X, 0:S // 2].bitcast(BF16)).then_inc(mT_out, 1)

            def part(k, turn, g, n, live):
                for b in range(CT):
                    if live[0]:
                        if b == 0:
                            at_least(dve, cut, 5 * (k - 1))
                        for j in range(HG):
                            x = HG * b + j
                            dve.wait_ge(s_done, STEPS * k + x + 1)
                            dve.tensor_reduce(nm[g % 2][:, x:x + 1], ps[:, x % NBANK, :], AX.X, ALU.max, negate=True)\
                               .then_inc(max_done, 1)
                            if b == 1 and j == 0 and live[1]:
                                maxima_parts_out(k - 1)
                    elif b == 1 and live[1]:
                        maxima_parts_out(k - 1)
                    if b == CT - 1 and live[2]:
                        kk = k - 2
                        u = g % 2
                        sums = ps[:, X, :].rearrange("p (x w) -> p x w", w=VW)
                        dve.wait_ge(oT_done, kk + 1)
                        dve.reciprocal(rec[u][:, :], sums[:, :, HD]).then_inc(rec_done, 1)
                        dve.wait_ge(rec_done, kk + 1)
                        gg = (g - 2) % NB
                        out = m.att[:, bass.ds(n * CT, CT), gg * HG * HD:(gg + 1) * HG * HD]
                        dve.tensor_tensor(out.rearrange("p t (j w) -> p t j w", w=HD),
                                          sums[:, :, 0:HD].rearrange("p (t j) w -> p t j w", t=CT),
                                          rec[u][:, :].rearrange("p (t j) -> p t j", t=CT).unsqueeze(3)
                                          .to_broadcast([P, CT, HG, HD]), ALU.mult).then_inc(att_done, 1)

            parts(dve, part)


E1, K1, H2 = 8, 2, 704
ROW1 = D + E1
SENT = 6
BLOCKS = (T * K1 + E1 * (P - 1)) // P
SLOTS = E1 * T
HH = H2 // 2
FT1 = -(-H2 // P)
FL = H2 - (FT1 - 1) * P
WE = 2 * DT * H2 + FT1 * D


def finish_1(nc, m):
    with ExitStack() as ctx:
        def sb(name, shape, dt=F32):
            return ctx.enter_context(nc.sbuf_tensor(name, shape, dt))

        def sem(name):
            return counter(nc, m, ctx, name)

        wo = sb("f_wo", [P, DT, D])
        wg = sb("f_wg", [P, DT, E1])
        spare = sb("f_spare", [P, 2, P], I32)
        tokid = sb("f_tokid", [P, NT], I32)
        tri = sb("f_tri", [P, P], BF16)
        ones = sb("f_ones", [P, P], BF16)
        att = [sb(f"f_att{u}", [P, CT, D]) for u in range(2)]
        x3 = [sb(f"f_x3{u}", [P, CT, D]) for u in range(2)]
        row = [sb(f"f_row{u}", [P, CT, ROW1]) for u in range(2)]
        attT = sb("f_attT", [P, DT, S])
        hT = sb("f_hT", [P, DT, S])
        st = sb("f_st", [P, CT, 6])
        mv = sb("f_mv", [P, CT, 2])
        ve = sb("f_ve", [P, CT])
        rstd = sb("f_rstd", [P, CT])
        nmx = sb("f_nmx", [P, CT])
        lg = sb("f_lg", [P, CT, E1])
        ex = sb("f_ex", [P, CT, E1])
        sm = sb("f_sm", [P, CT])
        rs = sb("f_rs", [P, CT])
        score = sb("f_score", [P, CT, E1 + SENT])
        top8 = sb("f_top8", [P, CT, 8])
        take8 = sb("f_take8", [P, CT, 8])
        left = sb("f_left", [P, CT, E1 + SENT])
        chosen = sb("f_chosen", [P, CT, E1])
        chosen_bf = [sb(f"f_chosen_bf{u}", [P, CT, E1], BF16) for u in range(2)]
        wgt = sb("f_wgt", [P, CT, E1])
        wsum = sb("f_wsum", [P, CT])
        wrec = sb("f_wrec", [P, CT])
        slot = sb("f_slot", [P, CT, E1])
        both = sb("f_both", [P, CT, E1])
        high = sb("f_high", [P, CT])
        total = sb("f_total", [P, CT])
        dst = [sb(f"f_dst{u}", [P, K1, CT], I32) for u in range(2)]
        src = [sb(f"f_src{u}", [P, CT], I32) for u in range(2)]
        ps = ctx.enter_context(nc.psum_tensor("f_ps", [P, 8, 512], F32))

        w_in = sem("f_w_in")
        made = sem("f_made")
        spare_out = sem("f_spare_out")
        att_here = sem("f_att_here")
        preset = sem("f_preset")
        aT_done = sem("f_aT_done")
        aT_out = sem("f_aT_out")
        o_done = sem("f_o_done")
        x_done = sem("f_x_done")
        ve_done = sem("f_ve_done")
        rstd_done = sem("f_rstd_done")
        h_done = sem("f_h_done")
        tr_done = sem("f_tr_done")
        hT_out = sem("f_hT_out")
        l_done = sem("f_l_done")
        lg_done = sem("f_lg_done")
        ex_done = sem("f_ex_done")
        chain = sem("f_chain")
        stats = sem("f_stats")
        slots = sem("f_slots")
        row_done = sem("f_row_done")
        chosen_done = sem("f_chosen_done")
        pos_done = sem("f_pos_done")
        pos_used = sem("f_pos_used")
        src_done = sem("f_src_done")
        dst_done = sem("f_dst_done")
        scattered = [sem(f"f_scattered{u}") for u in range(2)]
        x_out = [sem(f"f_x_out{u}") for u in range(2)]
        row_out = [sem(f"f_row_out{u}") for u in range(2)]
        block = ctx.enter_context(nc.Block())

        def steps(eng, body):
            def chunk(n):
                return (n, n // 2, n % 2) if 0 <= n < B else None
            for s in range(2):
                body(chunk(s), chunk(s - 1), chunk(s - 2))
            with eng.Fori(0, B // 2 - 2) as i:
                for u in range(2):
                    body((2 * i + 2 + u, i + 1, u), (2 * i + 1 + u, i + u, 1 - u), (2 * i + u, i, u))
            for s in range(B - 2, B + 2):
                body(chunk(s), chunk(s - 1), chunk(s - 2))

        def follows(a):
            if a is None or (isinstance(a[0], int) and a[0] + 1 >= B):
                return None
            return a[0] + 1, a[1] + a[2], 1 - a[2]

        @block.sync
        def _(sp):
            sp.dma_start(wo[:, :, :], m.ins["WoT1"].rearrange("(t p) n -> p t n", p=P)).then_inc(w_in, 16)
            sp.dma_start(wg[:, :, :], m.ins["WgT"].rearrange("(t p) n -> p t n", p=P)).then_inc(w_in, 16)
            sp.wait_ge(made, 1)
            sp.dma_start(m.slots1[0:SLOTS, :].rearrange("(p r s) a -> p r (s a)", p=P, s=2 * P)[:, 0:1, :],
                         spare[:, :, :].rearrange("p r s -> p (r s)").unsqueeze(1)).then_inc(spare_out, 16)
            sp.dma_start(m.slots1[SLOTS:SLOTS + P, :].rearrange("s a -> a s"), spare[0:1, 0, :]).then_inc(spare_out, 16)

            def body(a, b, c):
                if a:
                    n, i, u = a
                    sp.wait_ge(x_done, CT * (n + 1))
                    sp.dma_start(m.sums[bass.ds(n * S, S), :].rearrange("(t p) n -> p t n", p=P), x3[u][:, :, :])\
                      .then_inc(x_out[u], 16)
                if b:
                    n, i, u = b
                    sp.wait_ge(row_done, n + 1)
                    sp.dma_start(m.rows1[bass.ds(n * S, S), :].rearrange("(t p) n -> p t n", p=P), row[u][:, :, :])\
                      .then_inc(row_out[u], 16)

            steps(sp, body)
            for u in range(2):
                sp.wait_ge(x_out[u], 16 * (B // 2))
                sp.wait_ge(row_out[u], 16 * (B // 2))

        @block.gpsimd
        def _(pool):
            pool.iota(spare[:, :, :], pattern=[[0, 2], [1, P]], base=T, channel_multiplier=0).then_inc(made, 1)
            pool.iota(tokid[:, :], pattern=[[P, NT]], base=0, channel_multiplier=1).then_inc(made, 1)
            pool.iota(m.next_slot[:, :], pattern=[[T, E1]], base=0, channel_multiplier=0,
                      allow_small_or_imprecise_dtypes=True).then_inc(made, 1)
            pool.memset(ones[:, :], 1.0).then_inc(made, 1)
            pool.memset(tri[:, :], 1.0).then_inc(made, 1)
            pool.wait_ge(made, 5)
            pool.affine_select(out=tri[:, :], in_=tri[:, :], compare_op=ALU.is_gt, fill=0.0, base=0,
                               pattern=[[1, P]], channel_multiplier=-1).then_inc(made, 1)
            pool.wait_ge(spare_out, 32)

            def body(a, b, c):
                if a:
                    n, i, u = a
                    pool.wait_ge(ve_done, n + 1)
                    pool.tensor_tensor(rstd[:, :], ve[:, :], m.minus_half[:, 0:CT], ALU.pow).then_inc(rstd_done, 1)
                if c:
                    n, i, u = c
                    at_least(pool, scattered[u], 16 * K1 * CT * i)
                    apart(m, pool)
                    pool.tensor_copy(src[u][:, :], tokid[:, bass.ds(n * CT, CT)]).then_inc(src_done, 1)
                    pool.wait_ge(src_done, n + 1)
                    pool.wait_ge(dst_done, 2 * (n + 1))
                    apart(m, pool)
                    for k in range(K1):
                        for j in range(CT):
                            pool.indirect_dma_start(m.slots1, bass.IndirectOffsetOnAxis(ap=dst[u][:, k, j:j + 1], axis=0),
                                                    src[u][:, j:j + 1], None).then_inc(scattered[u], 16)

            steps(pool, body)
            for u in range(2):
                pool.wait_ge(scattered[u], 16 * K1 * CT * (B // 2))

        @block.tensor
        def _(pe):
            pe.wait_ge(w_in, 32)
            pe.wait_ge(made, 6)

            def turned(n, i, u):
                pe.wait_ge(att_here, n + 1)
                at_least(pe, aT_out, DT * n)
                for j in range(CT):
                    for d in range(DT):
                        last = pe.transpose(ps[:, d, j * P:(j + 1) * P], att[u][:, j, d * P:(d + 1) * P], m.ident[:, :])
                last.then_inc(aT_done, 1)

            def projected(n, i, u):
                pe.wait_ge(aT_out, DT * (n + 1))
                at_least(pe, x_done, CT * n)
                for j in range(CT):
                    for d in range(DT):
                        last = pe.matmul(ps[:, 2 + j // 2, (j % 2) * D:(j % 2 + 1) * D], attT[:, d, j * P:(j + 1) * P],
                                         wo[:, d, :], start=(d == 0), stop=(d == DT - 1))
                    if j % 2:
                        last.then_inc(o_done, 1)

            def logits(n, i, u):
                at_least(pe, hT_out, DT * n)
                for j in range(CT):
                    pe.wait_ge(h_done, CT * n + j + 1)
                    for d in range(DT):
                        last = pe.transpose(ps[:, 4 + d, j * P:(j + 1) * P], row[u][:, j, d * P:(d + 1) * P], m.ident[:, :])
                last.then_inc(tr_done, 1)
                pe.wait_ge(hT_out, DT * (n + 1))
                at_least(pe, lg_done, n)
                for j in range(CT):
                    for d in range(DT):
                        last = pe.matmul(ps[:, 6, j * E1:(j + 1) * E1], hT[:, d, j * P:(j + 1) * P], wg[:, d, :],
                                         start=(d == 0), stop=(d == DT - 1))
                last.then_inc(l_done, 1)

            def places(n, i, u):
                pe.wait_ge(chosen_done, n + 1)
                at_least(pe, pos_used, 2 * n)
                for j in range(CT + 1):
                    for k in range(min(j + 1, CT)):
                        last = pe.matmul(ps[:, 7, j * E1:(j + 1) * E1], tri[:, :] if k == j else ones[:, :],
                                         chosen_bf[u][:, k, :], start=(k == 0), stop=(k == min(j, CT - 1)))
                last.then_inc(pos_done, 1)

            turned(0, 0, 0)

            def body(a, b, c):
                if a:
                    projected(*a)
                if c:
                    places(*c)
                if b:
                    logits(*b)
                if follows(a):
                    turned(*follows(a))

            steps(pe, body)

        @block.scalar
        def _(act):
            def turned(n, i, u):
                at_least(act, aT_done, n - 1)
                act.activation(att[u][:, :, :], m.att[:, bass.ds(n * CT, CT), :], ACT.Copy).then_inc(att_here, 1)

            def turned_out(n, i, u):
                act.wait_ge(aT_done, n + 1)
                at_least(act, o_done, 2 * n)
                for d in range(DT):
                    act.activation(attT[:, d, :], ps[:, d, :], ACT.Copy).then_inc(aT_out, 1)

            turned(0, 0, 0)
            turned_out(0, 0, 0)

            def body(a, b, c):
                if follows(a):
                    turned(*follows(a))
                if b:
                    n, i, u = b
                    act.wait_ge(tr_done, n + 1)
                    at_least(act, l_done, n)
                    for d in range(DT):
                        act.activation(hT[:, d, :], ps[:, 4 + d, :], ACT.Copy).then_inc(hT_out, 1)
                    act.wait_ge(lg_done, n + 1)
                    act.activation(ex[:, :, :], lg[:, :, :], ACT.Exp).then_inc(ex_done, 1)
                if follows(a):
                    turned_out(*follows(a))

            steps(act, body)

        ROUTE_LINKS = 4 + CT + 1 + CT + 1 + 4

        @block.vector
        def _(dve):
            dve.memset(score[:, :, E1:], NEG).then_inc(preset, 1)
            dve.memset(take8[:, :, K1:8], NEG).then_inc(preset, 1)
            dve.wait_ge(preset, 2)
            dve.wait_ge(made, 3)

            def wide(t, width=E1):
                return t.unsqueeze(2).to_broadcast([P, CT, width])

            def statistics(n, i, u):
                at_least(dve, x_out[u], 16 * i)
                for j in range(CT):
                    dve.wait_ge(o_done, 2 * n + j // 2 + 1)
                    dve.scalar_tensor_tensor(x3[u][:, j, :], ps[:, 2 + j // 2, (j % 2) * D:(j % 2 + 1) * D],
                                             m.gate[:, 1:2], m.x[:, bass.ds(n * CT + j, 1), :].rearrange("p a d -> p (a d)"),
                                             ALU.mult, ALU.add).then_inc(x_done, 1)
                for j in range(CT):
                    dve.wait_ge(x_done, CT * n + j + 1)
                    apart(m, dve)
                    dve.bn_stats(st[:, j, :], x3[u][:, j, :]).then_inc(stats, 1)
                dve.wait_ge(stats, 2 * CT * n + CT)
                apart(m, dve)
                for j in range(CT):
                    dve.bn_aggr(mv[:, j, :], st[:, j, :]).then_inc(stats, 1)
                dve.wait_ge(stats, 2 * CT * (n + 1))
                dve.tensor_scalar(ve[:, :], mv[:, :, 1], EPS, None, ALU.add).then_inc(ve_done, 1)

            def normalised(n, i, u):
                dve.wait_ge(rstd_done, n + 1)
                at_least(dve, row_out[u], 16 * i)
                for j in range(CT):
                    dve.tensor_scalar(row[u][:, j, 0:D], x3[u][:, j, :], mv[:, j, 0:1], rstd[:, j:j + 1],
                                      ALU.subtract, ALU.mult).then_inc(h_done, 1)

            def routed(n, i, u):
                at = [0]

                def link(ins):
                    at[0] += 1
                    ins.then_inc(chain, 1)

                def linked():
                    dve.wait_ge(chain, n * ROUTE_LINKS + at[0])

                logits = ps[:, 6, 0:CT * E1].rearrange("p (t e) -> p t e", t=CT)
                dve.wait_ge(l_done, n + 1)
                link(dve.tensor_reduce(nmx[:, :], logits, AX.X, ALU.max, negate=True))
                linked()
                dve.tensor_tensor(lg[:, :, :], logits, wide(nmx[:, :]), ALU.add).then_inc(lg_done, 1)
                dve.wait_ge(ex_done, n + 1)
                link(dve.tensor_reduce(sm[:, :], ex[:, :, :], AX.X, ALU.add))
                linked()
                link(dve.reciprocal(rs[:, :], sm[:, :]))
                linked()
                link(dve.tensor_tensor(score[:, :, 0:E1], ex[:, :, :], wide(rs[:, :]), ALU.mult))
                linked()
                apart(m, dve)
                for j in range(CT):
                    link(dve.max(top8[:, j, :], score[:, j, :]))
                linked()
                link(dve.tensor_copy(take8[:, :, 0:K1], top8[:, :, 0:K1]))
                linked()
                apart(m, dve)
                for j in range(CT):
                    link(dve.match_replace(left[:, j, :], take8[:, j, :], score[:, j, :], LOW))
                linked()
                link(dve.tensor_scalar(chosen[:, :, :], left[:, :, 0:E1], LOW, None, ALU.is_equal))
                linked()
                dve.tensor_copy(chosen_bf[u][:, :, :], chosen[:, :, :]).then_inc(chosen_done, 1)
                link(dve.tensor_tensor(wgt[:, :, :], chosen[:, :, :], score[:, :, 0:E1], ALU.mult))
                linked()
                link(dve.tensor_reduce(wsum[:, :], wgt[:, :, :], AX.X, ALU.add))
                linked()
                link(dve.tensor_scalar(wsum[:, :], wsum[:, :], 1e-20, None, ALU.add))
                linked()
                link(dve.reciprocal(wrec[:, :], wsum[:, :]))
                linked()
                assert at[0] == ROUTE_LINKS, at[0]
                dve.scalar_tensor_tensor(row[u][:, :, D:ROW1], wgt[:, :, :], m.half_gate[:, 3:4], wide(wrec[:, :]),
                                         ALU.mult, ALU.mult).then_inc(row_done, 1)

            def slotted(n, i, u):
                dve.wait_ge(pos_done, n + 1)
                dve.tensor_tensor(slot[:, :, :], ps[:, 7, 0:CT * E1].rearrange("p (t e) -> p t e", t=CT),
                                  m.next_slot[:, :].unsqueeze(1).to_broadcast([P, CT, E1]), ALU.add).then_inc(pos_used, 1)
                dve.wait_ge(pos_used, 2 * n + 1)
                dve.tensor_tensor(m.next_slot[:, :], m.next_slot[:, :], ps[:, 7, CT * E1:(CT + 1) * E1], ALU.add)\
                   .then_inc(pos_used, 1)
                dve.tensor_tensor(both[:, :, :], chosen[:, :, :], slot[:, :, :], ALU.mult).then_inc(slots, 1)
                dve.wait_ge(slots, 3 * n + 1)
                dve.tensor_reduce(high[:, :], both[:, :, :], AX.X, ALU.max).then_inc(slots, 1)
                dve.tensor_reduce(total[:, :], both[:, :, :], AX.X, ALU.add).then_inc(slots, 1)
                dve.wait_ge(slots, 3 * n + 3)
                at_least(dve, scattered[u], 16 * K1 * CT * i)
                dve.tensor_copy(dst[u][:, 0, :], high[:, :]).then_inc(dst_done, 1)
                dve.tensor_tensor(dst[u][:, 1, :], total[:, :], high[:, :], ALU.subtract).then_inc(dst_done, 1)

            def body(a, b, c):
                if b:
                    normalised(*b)
                if a:
                    statistics(*a)
                if c:
                    slotted(*c)
                if b:
                    routed(*b)

            steps(dve, body)


def experts_1(nc, m):
    NBUF = 4
    with ExitStack() as ctx:
        def sb(name, shape, dt=F32):
            return ctx.enter_context(nc.sbuf_tensor(name, shape, dt))

        def sem(name):
            return counter(nc, m, ctx, name)

        W = sb("d_W", [P, E1 * WE])
        zero = sb("d_zero", [P, ROW1])
        jb = sb("d_jb", [P, BLOCKS, E1])
        tile_no = sb("d_tile_no", [P, E1, NT])
        eT = sb("d_eT", [P, E1])
        count = sb("d_count", [P, E1])
        more = sb("d_more", [P, E1, NT])
        nblk = sb("d_nblk", [P, E1])
        end = sb("d_end", [P, E1])
        one8 = sb("d_one8", [P, E1])
        begin = sb("d_begin", [P, E1])
        base = sb("d_base", [P, E1])
        in_end = sb("d_in_end", [P, BLOCKS, E1])
        mine = sb("d_mine", [P, BLOCKS, E1])
        tmp = sb("d_tmp", [P, BLOCKS, E1])
        some = sb("d_some", [P, BLOCKS])
        row0 = sb("d_row0", [P, BLOCKS])
        row1 = sb("d_row1", [P, BLOCKS])
        expert = sb("d_expert", [P, BLOCKS])
        table = sb("d_table", [P, 3, BLOCKS], I32)
        idx = [sb(f"d_idx{g}", [P, 1], I32) for g in range(NBUF)]
        xg = [sb(f"d_xg{g}", [P, ROW1]) for g in range(NBUF)]
        xT = [sb(f"d_xT{u}", [P, DT, P]) for u in range(2)]
        th = sb("d_th", [P, 2, HH])
        a = sb("d_a", [P, 2, HH])
        b = [sb(f"d_b{u}", [P, 2, HH]) for u in range(2)]
        bT = [sb(f"d_bT{u}", [P, FT1, P]) for u in range(2)]
        y = [sb(f"d_y{g}", [P, D]) for g in range(NBUF)]
        ps = ctx.enter_context(nc.psum_tensor("d_ps", [P, 8, 512], F32))
        XB, HB, TB, YB = 0, 1, 5, 7

        w_in = sem("d_w_in")
        zeroed = sem("d_zeroed")
        zero_out = sem("d_zero_out")
        chain = sem("d_chain")
        idx_in = [sem(f"d_idx_in{g}") for g in range(NBUF)]
        x_in = [sem(f"d_x_in{g}") for g in range(NBUF)]
        xT_done = sem("d_xT_done")
        xT_out = sem("d_xT_out")
        h_done = sem("d_h_done")
        th_done = sem("d_th_done")
        a_done = sem("d_a_done")
        b_done = sem("d_b_done")
        bT_done = sem("d_bT_done")
        bT_act = sem("d_bT_act")
        bT_dve = sem("d_bT_dve")
        tail = sem("d_tail")
        y_done = sem("d_y_done")
        y_out = sem("d_y_out")
        added = [sem(f"d_added{g}") for g in range(NBUF)]
        out_in = sem("d_out_in")
        block = ctx.enter_context(nc.Block())
        TABLE = 19

        def parts(eng, part):
            LEAD = NBUF - 1
            for j in range(LEAD):
                part(j, 0, j, True, j > 0)
            passes = (BLOCKS - LEAD - 2) // NBUF
            with eng.Fori(0, passes) as i:
                for w in range(NBUF):
                    j = LEAD + w
                    part(NBUF * i + j, i + j // NBUF, j % NBUF, True, True)
            for j in range(LEAD + NBUF * passes, BLOCKS + 1):
                part(j, j // NBUF, j % NBUF, j < BLOCKS, True)

        def before(t, g, back):
            return t + (g - back) // NBUF, (g - back) % NBUF

        @block.sync
        def _(sp):
            for e in range(E1):
                at = e * WE
                for w in (m.ins["W1T"], m.ins["W3T"]):
                    sp.dma_start(W[:, at:at + DT * H2].rearrange("p (t h) -> p t h", t=DT),
                                 w[e].rearrange("(t p) h -> p t h", p=P)).then_inc(w_in, 16)
                    at += DT * H2
                sp.dma_start(W[:, at:at + (FT1 - 1) * D].rearrange("p (t d) -> p t d", d=D),
                             m.ins["W2T"][e, 0:(FT1 - 1) * P, :].rearrange("(t p) d -> p t d", p=P)).then_inc(w_in, 16)
                at += (FT1 - 1) * D
                sp.dma_start(W[0:FL, at:at + D], m.ins["W2T"][e, (FT1 - 1) * P:H2, :]).then_inc(w_in, 16)
            sp.wait_ge(zeroed, 1)
            sp.dma_start(m.rows1[T:T + P, :], zero[:, :]).then_inc(zero_out, 16)
            sp.dma_start(m.sums[T:T + P, :], zero[:, 0:D]).then_inc(zero_out, 16)
            sp.wait_ge(chain, TABLE)

            def load(j, t, g):
                r = sp.value_load(table[0:1, 0, bass.ds(j, 1)], min_val=0, max_val=SLOTS)
                sp.dma_start(idx[g][:, :], m.slots1[bass.ds(r, P), :]).then_inc(idx_in[g], 16)

            for g in range(NBUF - 1):
                load(g, 0, g)

            with sp.Fori(0, (BLOCKS - NBUF + 1) // NBUF) as i:
                for w in range(NBUF):
                    g = (w + NBUF - 1) % NBUF
                    if w == 0:
                        sp.wait_ge(added[g], 16 * i)
                    else:
                        sp.wait_ge(added[g], 16 * (i + 1))
                    apart(m, sp)
                    load(NBUF * i + NBUF - 1 + w, i, g)
            assert (BLOCKS - NBUF + 1) % NBUF == 0
            for g in range(NBUF):
                sp.wait_ge(added[g], 16 * len(range(g, BLOCKS, NBUF)))
            sp.dma_start(m.out.rearrange("b s d -> (b s) d"), m.sums[0:T, :]).then_inc(out_in, 16)
            sp.wait_ge(out_in, 16)

        @block.gpsimd
        def _(pool):
            pool.memset(zero[:, :], 0.0).then_inc(zeroed, 1)
            pool.iota(jb[:, :, :], pattern=[[1, BLOCKS], [0, E1]], base=0, channel_multiplier=0,
                      allow_small_or_imprecise_dtypes=True).then_inc(zeroed, 1)
            pool.iota(tile_no[:, :, :], pattern=[[0, E1], [P, NT]], base=0, channel_multiplier=0,
                      allow_small_or_imprecise_dtypes=True).then_inc(zeroed, 1)
            pool.iota(eT[:, :], pattern=[[T, E1]], base=0, channel_multiplier=0,
                      allow_small_or_imprecise_dtypes=True).then_inc(zeroed, 1)
            pool.memset(one8[:, :], 1.0).then_inc(zeroed, 1)
            pool.wait_ge(zero_out, 32)

            def gather(t, g):
                pool.wait_ge(idx_in[g], 16 * (t + 1))
                apart(m, pool)
                pool.indirect_dma_start(xg[g][:, :], None, m.rows1[:, :],
                                        bass.IndirectOffsetOnAxis(ap=idx[g][:, :], axis=0)).then_inc(x_in[g], 16)

            for g in range(2):
                gather(0, g)

            def part(j, t, g, hid, res):
                ahead = j + 2
                if not isinstance(j, int) or ahead < BLOCKS:
                    tt, gg = before(t, g, -2)
                    if not (isinstance(j, int) and j < 2):
                        pool.wait_ge(added[gg], 16 * tt)
                    gather(tt, gg)
                if res:
                    tt, gg = before(t, g, 1)
                    pool.wait_ge(y_out, j)
                    if not (isinstance(j, int) and j < 2):
                        t2, g2 = before(t, g, 2)
                        pool.wait_ge(added[g2], 16 * (t2 + 1))
                    apart(m, pool)
                    pool.indirect_dma_start(m.sums, bass.IndirectOffsetOnAxis(ap=idx[gg][:, :], axis=0),
                                            y[gg][:, :], None, compute_op=ALU.add).then_inc(added[gg], 16)

            parts(pool, part)

        @block.tensor
        def _(pe):
            pe.wait_ge(w_in, 16 * 4 * E1)
            pe.wait_ge(chain, TABLE)

            def x_rows(j, t, g):
                pe.wait_ge(x_in[g], 16 * (t + 1))
                if not (isinstance(j, int) and j == 0):
                    pe.wait_ge(xT_out, j)
                for d in range(DT):
                    last = pe.transpose(ps[:, XB, d * P:(d + 1) * P], xg[g][:, d * P:(d + 1) * P], m.ident[:, :])
                last.then_inc(xT_done, 1)

            def hidden(j, u, half, off):
                for w in range(2):
                    if not (isinstance(j, int) and j == 0):
                        pe.wait_ge(b_done, 2 * j - 1 + half)
                    for d in range(DT):
                        last = pe.matmul(ps[:, HB + 2 * half + w, 0:HH], xT[u][:, d, :],
                                         W[:, bass.ds(off + ((w * DT + d) * H2 + half * HH), HH)],
                                         start=(d == 0), stop=(d == DT - 1))
                last.then_inc(h_done, 1)

            def part(j, t, g, hid, res):
                if isinstance(j, int) and j == 0:
                    x_rows(0, 0, 0)
                if hid:
                    off = pe.value_load(table[0:1, 1, bass.ds(j, 1)], min_val=0, max_val=(E1 - 1) * WE)
                    pe.wait_ge(xT_out, j + 1)
                    hidden(j, g % 2, 0, off)
                if res:
                    u = (g - 1) % 2
                    pe.wait_ge(b_done, 2 * j)
                    if not (isinstance(j, int) and j == 1):
                        pe.wait_ge(bT_act, j - 1)
                        pe.wait_ge(bT_dve, j - 1)
                    flat = b[u][:, :, :].rearrange("p a h -> p (a h)")
                    for f in range(FT1):
                        rows = P if f < FT1 - 1 else FL
                        last = pe.transpose(ps[0:rows, TB + f // CT, (f % CT) * P:(f % CT + 1) * P],
                                            flat[:, f * P:f * P + rows], m.ident[:, :])
                        if f == CT - 1 or f == FT1 - 1:
                            last.then_inc(bT_done, 1)
                if hid:
                    hidden(j, g % 2, 1, off)
                    tt, gg = before(t, g, -1)
                    if not isinstance(j, int) or j + 1 < BLOCKS:
                        x_rows(j + 1, tt, gg)
                if res:
                    u = (g - 1) % 2
                    off2 = pe.value_load(table[0:1, 1, bass.ds(j - 1, 1)], min_val=0, max_val=(E1 - 1) * WE)
                    pe.wait_ge(bT_act, j)
                    pe.wait_ge(bT_dve, j)
                    if not (isinstance(j, int) and j == 1):
                        pe.wait_ge(y_out, j - 1)
                    for f in range(FT1):
                        rows = P if f < FT1 - 1 else FL
                        last = pe.matmul(ps[:, YB, 0:D], bT[u][0:rows, f, :],
                                         W[0:rows, bass.ds(off2 + (2 * DT * H2 + f * D), D)],
                                         start=(f == 0), stop=(f == FT1 - 1))
                    last.then_inc(y_done, 1)

            parts(pe, part)

        @block.scalar
        def _(act):
            def x_out(j, u):
                act.wait_ge(xT_done, j + 1)
                if not (isinstance(j, int) and j < 2):
                    act.wait_ge(h_done, 2 * (j - 1))
                act.activation(xT[u][:, :, :], ps[:, XB, 0:D].rearrange("p (d t) -> p d t", d=DT), ACT.Copy).then_inc(xT_out, 1)

            act.wait_ge(chain, TABLE)

            def part(j, t, g, hid, res):
                if isinstance(j, int) and j == 0:
                    x_out(0, 0)
                if hid:
                    act.wait_ge(h_done, 2 * j + 1)
                    if not (isinstance(j, int) and j == 0):
                        act.wait_ge(a_done, 2 * j - 1)
                    act.activation(th[:, 0, :], ps[:, HB, 0:HH], ACT.Tanh, scale=0.5).then_inc(th_done, 1)
                if res:
                    u = (g - 1) % 2
                    act.wait_ge(bT_done, 2 * j - 1)
                    if not (isinstance(j, int) and j < 3):
                        act.wait_ge(y_done, j - 2)
                    act.activation(bT[u][:, 0:CT, :], ps[:, TB, :].rearrange("p (f t) -> p f t", f=CT), ACT.Copy)\
                       .then_inc(bT_act, 1)
                if hid:
                    act.wait_ge(h_done, 2 * j + 2)
                    if not (isinstance(j, int) and j == 0):
                        act.wait_ge(a_done, 2 * j)
                    act.activation(th[:, 1, :], ps[:, HB + 2, 0:HH], ACT.Tanh, scale=0.5).then_inc(th_done, 1)
                    if not isinstance(j, int) or j + 1 < BLOCKS:
                        x_out(j + 1, (g + 1) % 2)
                if res:
                    tt, gg = before(t, g, 1)
                    e = act.value_load(table[0:1, 2, bass.ds(j - 1, 1)], min_val=0, max_val=E1 - 1)
                    act.wait_ge(y_done, j)
                    if not (isinstance(j, int) and j - 1 < NBUF):
                        act.wait_ge(added[gg], 16 * tt)
                    act.activation(y[gg][:, :], ps[:, YB, 0:D], ACT.Copy, scale=xg[gg][:, bass.ds(e + D, 1)]).then_inc(y_out, 1)

            parts(act, part)

        @block.vector
        def _(dve):
            at = [0]

            def link(ins):
                at[0] += 1
                ins.then_inc(chain, 1)
                dve.wait_ge(chain, at[0])

            def over_blocks(t):
                return t.unsqueeze(1).to_broadcast([P, BLOCKS, E1])

            dve.wait_ge(zeroed, 5)
            link(dve.tensor_tensor(count[:, :], m.next_slot[:, :], eT[:, :], ALU.subtract))
            link(dve.tensor_tensor(more[:, :, :], count[:, :].unsqueeze(2).to_broadcast([P, E1, NT]), tile_no[:, :, :], ALU.is_gt))
            link(dve.tensor_reduce(nblk[:, :], more[:, :, :], AX.X, ALU.add))
            link(dve.tensor_tensor_scan(end[:, :], one8[:, :], nblk[:, :], 0.0, ALU.mult, ALU.add))
            link(dve.tensor_tensor(begin[:, :], end[:, :], nblk[:, :], ALU.subtract))
            link(dve.tensor_tensor(in_end[:, :, :], over_blocks(end[:, :]), jb[:, :, :], ALU.is_gt))
            link(dve.tensor_tensor(tmp[:, :, :], over_blocks(begin[:, :]), jb[:, :, :], ALU.is_gt))
            link(dve.tensor_tensor(mine[:, :, :], in_end[:, :, :], tmp[:, :, :], ALU.subtract))
            link(dve.tensor_reduce(some[:, :], mine[:, :, :], AX.X, ALU.add))
            link(dve.scalar_tensor_tensor(base[:, :], begin[:, :], -float(P), eT[:, :], ALU.mult, ALU.add))
            link(dve.scalar_tensor_tensor(tmp[:, :, :], jb[:, :, :], float(P), over_blocks(base[:, :]), ALU.mult, ALU.add))
            link(dve.tensor_tensor(in_end[:, :, :], tmp[:, :, :], mine[:, :, :], ALU.mult))
            link(dve.tensor_reduce(row0[:, :], in_end[:, :, :], AX.X, ALU.add))
            link(dve.tensor_scalar(row1[:, :], some[:, :], -float(SLOTS), float(SLOTS), ALU.mult, ALU.add))
            link(dve.tensor_tensor(table[:, 0, :], row0[:, :], row1[:, :], ALU.add))
            link(dve.tensor_tensor(tmp[:, :, :], over_blocks(eT[:, :]), mine[:, :, :], ALU.mult))
            link(dve.tensor_reduce(expert[:, :], tmp[:, :, :], AX.X, ALU.add))
            link(dve.tensor_scalar(table[:, 1, :], expert[:, :], float(WE) / T, None, ALU.mult))
            link(dve.tensor_scalar(table[:, 2, :], expert[:, :], 1.0 / T, None, ALU.mult))
            assert at[0] == TABLE

            def part(j, t, g, hid, res):
                def gated(half, u):
                    dve.wait_ge(th_done, 2 * j + half + 1)
                    dve.scalar_tensor_tensor(a[:, half, :], th[:, half, :], 1.0, ps[:, HB + 2 * half, 0:HH], ALU.add, ALU.mult)\
                       .then_inc(a_done, 1)
                    dve.wait_ge(a_done, 2 * j + half + 1)
                    if not (isinstance(j, int) and j < 2):
                        dve.wait_ge(bT_done, 2 * (j - 1))
                    dve.tensor_tensor(b[u][:, half, :], a[:, half, :], ps[:, HB + 2 * half + 1, 0:HH], ALU.mult)\
                       .then_inc(b_done, 1)

                if hid:
                    gated(0, g % 2)
                if res:
                    u = (g - 1) % 2
                    dve.wait_ge(bT_done, 2 * j)
                    if not (isinstance(j, int) and j < 3):
                        dve.wait_ge(y_done, j - 2)
                    dve.tensor_copy(bT[u][:, CT, :], ps[:, TB + 1, 0:P]).then_inc(tail, 1)
                    dve.tensor_copy(bT[u][0:FL, CT + 1, :], ps[0:FL, TB + 1, P:2 * P]).then_inc(bT_dve, 1)
                if hid:
                    gated(1, g % 2)

            parts(dve, part)



class Memory:
    pass


def flamingo_kernel(nc, ins, out):
    m = Memory()
    m.ins, m.out = ins, out

    def dram(name, shape, dt=F32):
        return nc.dram_tensor(name, shape, dt, kind="Internal").ap()

    m.acc = [dram(f"acc{u}", (T + CAP, D)) for u in range(2)]
    m.rows = dram("rows0", (T + CAP, ROW))
    m.qk = [dram(f"qk{a}", (B, PARTS, D, S), BF16) for a in range(2)]
    m.v = dram("v_heads", (T, H1 * VW))
    m.rows1 = dram("rows1", (T + P, ROW1))
    m.sums = dram("sums", (T + P, D))
    m.slots1 = dram("slots1", (SLOTS + P, 1), I32)

    with ExitStack() as keep:
        m.keep = keep

        def sb(where, name, shape, dt=F32):
            return where.enter_context(nc.sbuf_tensor(name, shape, dt))

        m.counted = set()
        m.ready = keep.enter_context(nc.semaphore("ready"))
        m.passed = keep.enter_context(nc.semaphore("passed"))
        m.ident = sb(keep, "ident", [P, P])
        m.ident_bf = sb(keep, "ident_bf", [P, P], BF16)
        m.causal = sb(keep, "causal", [P, P], BF16)
        m.minus_half = sb(keep, "minus_half", [P, CT])
        m.gate = sb(keep, "gate", [P, 4])
        m.half_gate = sb(keep, "half_gate", [P, 4])
        m.next_slot = sb(keep, "next_slot", [P, E1])
        with ExitStack() as stream:
            m.x = sb(stream, "x", [P, NT, D])
            with ExitStack() as first:
                m.A = sb(first, "A", [P, DT, D])
                m.wv0 = sb(first, "wv0", [P, DT, D])
                constants(nc, m)
                attention_0(nc, m)
            with ExitStack() as experts:
                m.hT_all = sb(experts, "hT_all", [P, DT, T])
                m.keyT = sb(experts, "keyT", [P, T // 2])
                m.slots0 = sb(experts, "slots0", [CAP, E0], I32)
                route_0(nc, m)
                shared_0(nc, m)
                experts_0(nc, m)
            clear_counters(nc, m)
            project_1(nc, m)
            m.att = sb(stream, "att", [P, NT, D])
            attention_1(nc, m)
            finish_1(nc, m)
        experts_1(nc, m)


def kernel(**inputs):
    import numpy as _np
    import concourse.bacc as _bacc
    from concourse import mybir as _mybir
    from concourse.bass_utils import run_bass_kernel_spmd as _run

    a = {k: _np.asarray(v) for k, v in inputs.items()}
    laid = {
        "x": a["x"],
        "ctxT": a["ctx_1024"].reshape(T, D).T,
        "g_xattn": a["g_xattn"],
        "g_ffn": a["g_ffn"],
        "WqT0": a["L0_xattn_Wq"].T,
        "WkT0": a["L0_xattn_Wk"].T,
        "Wv0": a["L0_xattn_Wv"],
        "rwT": a["L0_ffn_router_weight"].T,
        "ebias": a["L0_ffn_expert_bias"],
        "w1": a["L0_ffn_w1"],
        "w2": a["L0_ffn_w2"],
        "sw1T": a["L0_ffn_sw1"].T,
        "sw2T": a["L0_ffn_sw2"].T,
        "WqT1": a["L1_xattn_Wq"].T,
        "WkT1": a["L1_xattn_Wk"].T,
        "WvT1": a["L1_xattn_Wv"].T,
        "WoT1": a["L1_xattn_Wo"].T,
        "bq": a["L1_xattn_bq"].reshape(DT, P).T,
        "bk": a["L1_xattn_bk"].reshape(DT, P).T,
        "bv": a["L1_xattn_bv"],
        "WgT": a["L1_ffn_Wg"].T,
        "W1T": a["L1_ffn_W1"].transpose(0, 2, 1),
        "W3T": a["L1_ffn_W3"].transpose(0, 2, 1),
        "W2T": a["L1_ffn_W2"].transpose(0, 2, 1),
    }
    nc = _bacc.Bacc("TRN2", target_bir_lowering=False, num_devices=1)
    arrays, ins = {}, {}
    for name, value in laid.items():
        value = _np.ascontiguousarray(value)
        arrays[f"in_{name}"] = value
        ins[name] = nc.dram_tensor(f"in_{name}", value.shape, _mybir.dt.from_np(value.dtype), kind="ExternalInput").ap()
    out = nc.dram_tensor("out_0", (B, S, D), _mybir.dt.float32, kind="ExternalOutput").ap()
    flamingo_kernel(nc, ins, out)
    r = _run(nc, [arrays], core_ids=[0])
    return r.results[0]["out_0"]
```

```python
import concourse.bass as bass
from concourse import mybir
from contextlib import ExitStack


F32 = mybir.dt.float32
BF16 = mybir.dt.bfloat16
I32 = mybir.dt.int32
ALU = mybir.AluOpType
ACT = mybir.ActivationFunctionType
AX = mybir.AxisListType

P = 128
B, S, D = 8, 512, 256
T = B * S
DT = D // P
CT = S // P
NT = T // P
EPS = 1e-5
NEG = -3.0e38


def dma_counter(nc, m, name):
    return m.keep.enter_context(nc.semaphore(name))


def counter(nc, m, ctx, name):
    sem = ctx.enter_context(nc.semaphore(name))
    assert sem.num not in m.counted
    m.counted.add(sem.num)
    return sem


def clear_counters(nc, m):
    runs = []
    for num in sorted(m.counted):
        if runs and runs[-1][1] == num:
            runs[-1][1] = num + 1
        else:
            runs.append([num, num + 1])
    m.counted.clear()
    with nc.Block() as block:
        @block.gpsimd
        def _(pool):
            for first, end in runs:
                pool.sem_clear(range(first, end))


def apart(m, eng):
    eng.sem_inc(m.passed, 1)


def at_least(eng, sem, value):
    if isinstance(value, int) and value <= 0:
        return
    eng.wait_ge(sem, value)


def constants(nc, m):
    with ExitStack() as ctx:
        def sb(name, shape, dt=F32):
            return ctx.enter_context(nc.sbuf_tensor(name, shape, dt))

        def sem(name):
            return counter(nc, m, ctx, name)

        wqT = sb("c_wqT", [P, DT, D])
        wkT = sb("c_wkT", [P, DT, D])
        gates = sb("c_gates", [P, 4])
        ps = ctx.enter_context(nc.psum_tensor("c_ps", [P, DT, 512], F32))
        w_in = sem("c_w_in")
        g_in = sem("c_g_in")
        wv_in = sem("c_wv_in")
        zeroed = sem("c_zeroed")
        ident_made = sem("c_ident_made")
        a_done = sem("c_a_done")
        a_out = sem("c_a_out")
        gate_made = sem("c_gate_made")
        block = ctx.enter_context(nc.Block())

        @block.sync
        def _(sp):
            sp.dma_start(wqT[:, :, :], m.ins["WqT0"].rearrange("(t p) n -> p t n", p=P)).then_inc(w_in, 16)
            sp.dma_start(wkT[:, :, :], m.ins["WkT0"].rearrange("(t p) n -> p t n", p=P)).then_inc(w_in, 16)
            sp.dma_start(m.x[:, 0:CT, :], m.ins["x"][0].rearrange("(t p) d -> p t d", p=P)).then_inc(m.x0_in, 16)
            sp.wait_ge(w_in, 32)

        @block.gpsimd
        def _(pool):
            pool.memset(m.ident[:, :], 0.0).then_inc(zeroed, 1)
            pool.memset(m.ident_bf[:, :], 0.0).then_inc(zeroed, 1)
            pool.memset(m.causal[:, :], 0.0).then_inc(zeroed, 1)
            pool.memset(m.minus_half[:, :], -0.5)
            pool.wait_ge(zeroed, 3)
            for t in (m.ident, m.ident_bf):
                pool.affine_select(out=t[:, :], in_=t[:, :], compare_op=ALU.not_equal, fill=1.0, base=0,
                                   pattern=[[-1, P]], channel_multiplier=1)
            pool.affine_select(out=m.causal[:, :], in_=m.causal[:, :], compare_op=ALU.is_ge, fill=NEG, base=0,
                               pattern=[[-1, P]], channel_multiplier=1).then_inc(ident_made, 1)

        @block.tensor
        def _(pe):
            pe.wait_ge(w_in, 32)
            for d in range(DT):
                for e in range(DT):
                    last = pe.matmul(ps[:, d, 0:D], wqT[:, e, d * P:(d + 1) * P], wkT[:, e, :],
                                     start=(e == 0), stop=(e == DT - 1))
                last.then_inc(a_done, 1)

        @block.scalar
        def _(act):
            act.dma_start(gates[:, 0:2], m.ins["g_xattn"].rearrange("(a n) -> a n", a=1).to_broadcast([P, 2])).then_inc(g_in, 16)
            act.dma_start(gates[:, 2:4], m.ins["g_ffn"].rearrange("(a n) -> a n", a=1).to_broadcast([P, 2])).then_inc(g_in, 16)
            act.dma_start(m.wv0[:, :, :], m.ins["Wv0"].rearrange("(t p) n -> p t n", p=P)).then_inc(wv_in, 16)
            act.wait_ge(g_in, 32)
            act.activation(m.gate[:, :], gates[:, :], ACT.Tanh).then_inc(gate_made, 1)
            act.wait_ge(gate_made, 1)
            act.activation(m.half_gate[:, :], m.gate[:, :], ACT.Copy, scale=0.5).then_inc(gate_made, 1)
            for d in range(DT):
                act.wait_ge(a_done, d + 1)
                act.activation(m.A[:, d, :], ps[:, d, 0:D], ACT.Copy, scale=float(D) ** -0.5).then_inc(a_out, 1)
            act.wait_ge(a_out, DT)
            act.wait_ge(wv_in, 16)


def attention_0(nc, m):
    with ExitStack() as ctx:
        def sb(name, shape, dt=F32):
            return ctx.enter_context(nc.sbuf_tensor(name, shape, dt))

        def sem(name):
            return counter(nc, m, ctx, name)

        cT = [sb(f"a_cT{u}", [P, DT, S]) for u in range(2)]
        h = sb("a_h", [P, CT, D])
        hT = sb("a_hT", [P, DT, S])
        qT = sb("a_qT", [P, DT, S])
        V = sb("a_V", [P, CT, D])
        prob = [sb(f"a_prob{u}", [P, S]) for u in range(2)]
        probT = [sb(f"a_probT{u}", [P, S]) for u in range(2)]
        st = sb("a_st", [P, CT, 6])
        mv = sb("a_mv", [P, CT, 2])
        ve = sb("a_ve", [P, CT])
        rstd = sb("a_rstd", [P, CT])
        nm = sb("a_nm", [P, CT])
        rowsum = sb("a_rowsum", [P, CT])
        rec = sb("a_rec", [P, CT])
        sc = sb("a_sc", [P, CT])
        ps = ctx.enter_context(nc.psum_tensor("a_ps", [P, 8, 512], F32))

        ctx_in = [sem(f"a_ctx_in{u}") for u in range(2)]
        x_in = sem("a_x_in")
        bn_done = sem("a_bn_done")
        aggr_done = sem("a_aggr_done")
        ve_done = sem("a_ve_done")
        rstd_done = sem("a_rstd_done")
        h_done = sem("a_h_done")
        tr_done = sem("a_tr_done")
        hT_out = sem("a_hT_out")
        q_done = sem("a_q_done")
        qT_act = sem("a_qT_act")
        qT_dve = sem("a_qT_dve")
        v_done = sem("a_v_done")
        V_act = sem("a_V_act")
        V_dve = sem("a_V_dve")
        s_done = sem("a_s_done")
        nm_done = sem("a_nm_done")
        p_done = sem("a_p_done")
        pT_done = sem("a_pT_done")
        pT_out = sem("a_pT_out")
        o_done = sem("a_o_done")
        rec_done = sem("a_rec_done")
        sc_done = sem("a_sc_done")
        x_done = sem("a_x_done")
        block = ctx.enter_context(nc.Block())

        def turns(eng, body):
            with eng.Fori(0, B // 2 - 1) as i:
                for u in range(2):
                    body(2 * i + u, i, u)
            for u in range(2):
                body(B - 2 + u, B // 2 - 1, u)

        @block.sync
        def _(sp):
            def load(n, u):
                sp.dma_start(cT[u][:, :, :], m.ins["ctxT"].rearrange("(t p) n -> p t n", p=P)[:, :, bass.ds(n * S, S)])\
                  .then_inc(ctx_in[u], 16)

            load(0, 0)
            sp.dma_start(m.x[:, CT:NT, :].rearrange("p (b t) d -> p b t d", t=CT),
                         m.ins["x"][1:B].rearrange("b (t p) d -> p b t d", p=P)).then_inc(x_in, 16)
            load(1, 1)
            with sp.Fori(0, B // 2 - 1) as i:
                for u in range(2):
                    sp.wait_ge(s_done, CT * (2 * i + u + 1))
                    load(2 * i + 2 + u, u)

        @block.gpsimd
        def _(pool):
            with pool.Fori(0, B) as n:
                pool.wait_ge(ve_done, n + 1)
                pool.tensor_tensor(rstd[:, :], ve[:, :], m.minus_half[:, 0:CT], ALU.pow).then_inc(rstd_done, 1)

        @block.tensor
        def _(pe):
            def turned(n):
                at_least(pe, V_act, n)
                at_least(pe, V_dve, n)
                for j in range(CT):
                    pe.wait_ge(h_done, CT * n + j + 1)
                    for d in range(DT):
                        last = pe.transpose(ps[:, d, j * P:(j + 1) * P], h[:, j, d * P:(d + 1) * P], m.ident[:, :])
                last.then_inc(tr_done, 1)

            def body(n, i, u):
                at_least(pe, pT_out, CT * n)
                pe.wait_ge(hT_out, DT * (n + 1))
                for e in range(DT):
                    for d in range(DT):
                        last = pe.matmul(ps[:, 2 + e, :], m.A[:, d, e * P:(e + 1) * P], hT[:, d, :],
                                         start=(d == 0), stop=(d == DT - 1))
                    last.then_inc(q_done, 1)
                pe.wait_ge(ctx_in[u], 16 * i + 16)
                for k in range(CT):
                    for d in range(DT):
                        last = pe.matmul(ps[:, k // 2, (k % 2) * D:(k % 2 + 1) * D], cT[u][:, d, k * P:(k + 1) * P],
                                         m.wv0[:, d, :], start=(d == 0), stop=(d == DT - 1))
                    if k % 2:
                        last.then_inc(v_done, 1)
                pe.wait_ge(qT_act, n + 1)
                pe.wait_ge(qT_dve, n + 1)

                def scores(t):
                    pe.wait_ge(p_done, CT * n + max(t - 1, 0))
                    for d in range(DT):
                        pe.matmul(ps[:, 4 + t % 2, 0:(t + 1) * P], qT[:, d, t * P:(t + 1) * P],
                                  cT[u][:, d, 0:(t + 1) * P], start=(d == 0), stop=False)
                    pe.matmul(ps[:, 4 + t % 2, t * P:(t + 1) * P], m.ident_bf[:, :], m.causal[:, :],
                              start=False, stop=True).then_inc(s_done, 1)

                def transposes(t):
                    pe.wait_ge(p_done, CT * n + t + 1)
                    if t >= 2:
                        pe.wait_ge(pT_out, CT * n + t - 1)
                    for k in range(t + 1):
                        last = pe.transpose(ps[:, 2 + t % 2, k * P:(k + 1) * P], prob[t % 2][:, k * P:(k + 1) * P],
                                            m.ident[:, :])
                    last.then_inc(pT_done, 1)

                def weighted(t):
                    pe.wait_ge(pT_out, CT * n + t + 1)
                    pe.wait_ge(x_done, CT * n + max(t - 1, 0))
                    if t == 0:
                        pe.wait_ge(V_act, n + 1)
                        pe.wait_ge(V_dve, n + 1)
                    for k in range(t + 1):
                        last = pe.matmul(ps[:, 6 + t % 2, 0:D], probT[t % 2][:, k * P:(k + 1) * P], V[:, k, :],
                                         start=(k == 0), stop=(k == t))
                    last.then_inc(o_done, 1)

                scores(0)
                scores(1)
                transposes(0)
                scores(2)
                transposes(1)
                weighted(0)
                scores(3)
                transposes(2)
                weighted(1)
                transposes(3)
                if not (isinstance(n, int) and n + 1 == B):
                    turned(n + 1)
                weighted(2)
                weighted(3)

            turned(0)
            turns(pe, body)

        @block.scalar
        def _(act):
            def body(n, i, u):
                act.wait_ge(tr_done, n + 1)
                act.wait_ge(q_done, DT * n)
                for d in range(DT):
                    act.activation(hT[:, d, :], ps[:, d, :], ACT.Copy).then_inc(hT_out, 1)
                act.wait_ge(q_done, DT * n + 1)
                act.wait_ge(s_done, CT * n)
                act.activation(qT[:, 0, :], ps[:, 2, :], ACT.Copy).then_inc(qT_act, 1)
                act.wait_ge(v_done, 2 * n + 1)
                act.wait_ge(o_done, CT * n)
                act.activation(V[:, 0:2, :], ps[:, 0, :].rearrange("p (k n) -> p k n", k=2), ACT.Copy).then_inc(V_act, 1)
                for t in range(CT):
                    act.wait_ge(nm_done, CT * n + t + 1)
                    act.wait_ge(pT_done, CT * n + max(t - 1, 0))
                    act.activation(prob[t % 2][:, 0:(t + 1) * P], ps[:, 4 + t % 2, 0:(t + 1) * P], ACT.Exp,
                                   bias=nm[:, t:t + 1], accum_out=rowsum[:, t:t + 1]).then_inc(p_done, 1)

            turns(act, body)

        @block.vector
        def _(dve):
            def stats(n):
                for j in range(CT):
                    dve.bn_stats(st[:, j, :], m.x[:, bass.ds(n * CT + j, 1), :]).then_inc(bn_done, 1)
                for j in range(CT):
                    dve.wait_ge(bn_done, CT * n + j + 1)
                    apart(m, dve)
                    dve.bn_aggr(mv[:, j, :], st[:, j, :]).then_inc(aggr_done, 1)
                dve.wait_ge(aggr_done, CT * n + CT)
                dve.tensor_scalar(ve[:, :], mv[:, :, 1], EPS, None, ALU.add).then_inc(ve_done, 1)

            def normalise(n):
                dve.wait_ge(rstd_done, n + 1)
                at_least(dve, tr_done, n)
                for j in range(CT):
                    dve.tensor_scalar(h[:, j, :], m.x[:, bass.ds(n * CT + j, 1), :], mv[:, j, 0:1],
                                      rstd[:, j:j + 1], ALU.subtract, ALU.mult).then_inc(h_done, 1)

            def body(n, i, u):
                dve.wait_ge(q_done, DT * n + 2)
                dve.wait_ge(s_done, CT * n)
                dve.tensor_copy(qT[:, 1, :], ps[:, 3, :]).then_inc(qT_dve, 1)
                dve.wait_ge(v_done, 2 * n + 2)
                dve.wait_ge(o_done, CT * n)
                dve.tensor_copy(V[:, 2:4, :], ps[:, 1, :].rearrange("p (k n) -> p k n", k=2)).then_inc(V_dve, 1)

                def row_max(t):
                    dve.wait_ge(s_done, CT * n + t + 1)
                    dve.tensor_reduce(nm[:, t:t + 1], ps[:, 4 + t % 2, 0:(t + 1) * P], AX.X, ALU.max,
                                      negate=True).then_inc(nm_done, 1)

                def probT_out(t):
                    dve.wait_ge(pT_done, CT * n + t + 1)
                    dve.wait_ge(o_done, CT * n + max(t - 1, 0))
                    dve.tensor_copy(probT[t % 2][:, 0:(t + 1) * P], ps[:, 2 + t % 2, 0:(t + 1) * P]).then_inc(pT_out, 1)

                def add_to_x(t):
                    dve.wait_ge(p_done, CT * n + t + 1)
                    dve.reciprocal(rec[:, t:t + 1], rowsum[:, t:t + 1]).then_inc(rec_done, 1)
                    dve.wait_ge(rec_done, CT * n + t + 1)
                    dve.tensor_scalar(sc[:, t:t + 1], rec[:, t:t + 1], m.gate[:, 0:1], None, ALU.mult).then_inc(sc_done, 1)
                    dve.wait_ge(sc_done, CT * n + t + 1)
                    dve.wait_ge(o_done, CT * n + t + 1)
                    xt = m.x[:, bass.ds(n * CT + t, 1), :]
                    dve.scalar_tensor_tensor(xt, ps[:, 6 + t % 2:7 + t % 2, 0:D], sc[:, t:t + 1], xt, ALU.mult, ALU.add)\
                       .then_inc(x_done, 1)

                more = not (isinstance(n, int) and n + 1 == B)
                row_max(0)
                row_max(1)
                if more:
                    dve.wait_ge(x_in, 16)
                    stats(n + 1)
                probT_out(0)
                row_max(2)
                probT_out(1)
                if more:
                    normalise(n + 1)
                row_max(3)
                add_to_x(0)
                probT_out(2)
                add_to_x(1)
                probT_out(3)
                add_to_x(2)
                add_to_x(3)

            dve.wait_ge(m.x0_in, 16)
            stats(0)
            normalise(0)
            turns(dve, body)


E0, K0, F0, SF = 64, 6, 128, 512
CAP = 2 * ((512 * K0 + E0 - 1) // E0)
R8 = 8
ROUNDS = CAP // R8
ROW = D + E0
LOW = -2.0e38
GELU_A, GELU_C = 0.044715, 0.7978845608028654


def route_0(nc, m):
    with ExitStack() as ctx:
        def sb(name, shape, dt=F32):
            return ctx.enter_context(nc.sbuf_tensor(name, shape, dt))

        def sem(name):
            return counter(nc, m, ctx, name)

        row = [sb(f"b_row{u}", [P, CT, ROW]) for u in range(2)]
        hT = [sb(f"b_hT{u}", [P, DT, S]) for u in range(2)]
        rwT = sb("b_rwT", [P, DT, E0])
        bias = sb("b_bias", [P, E0])
        zero = sb("b_zero", [P, 2048])
        keyc = sb("b_keyc", [P, NT])
        st = sb("b_st", [P, CT, 6])
        mv = sb("b_mv", [P, CT, 2])
        ve = sb("b_ve", [P, CT])
        rstd = sb("b_rstd", [P, CT])
        ex = [sb(f"b_ex{u}", [P, CT, E0]) for u in range(2)]
        ex1 = sb("b_expp", [P, CT, E0])
        score = sb("b_score", [P, CT, E0])
        biased = sb("b_biased", [P, CT, E0 + 2])
        top8 = sb("b_top8", [P, CT, R8])
        take8 = sb("b_take8", [P, CT, R8])
        left = sb("b_left", [P, CT, E0 + 2])
        chosen = sb("b_chosen", [P, CT, E0])
        wgt = sb("b_wgt", [P, CT, E0])
        wsum = sb("b_wsum", [P, CT])
        wrec = sb("b_wrec", [P, CT])
        key = [sb(f"b_key{u}", [P, CT, E0]) for u in range(2)]
        ps = ctx.enter_context(nc.psum_tensor("b_ps", [P, 8, 512], F32))

        w_in = sem("b_w_in")
        zeroed = sem("b_zeroed")
        zero_out = sem("b_zero_out")
        keyc_made = sem("b_keyc_made")
        preset = sem("b_preset")
        bn_done = sem("b_bn_done")
        aggr_done = sem("b_aggr_done")
        ve_done = sem("b_ve_done")
        rstd_done = sem("b_rstd_done")
        h_done = sem("b_h_done")
        tr_done = sem("b_tr_done")
        hT_out = sem("b_hT_out")
        hT_kept = sem("b_hT_kept")
        l_done = sem("b_l_done")
        ex_done = sem("b_ex_done")
        chain = sem("b_chain")
        row_done = sem("b_row_done")
        h_out = [sem(f"b_h_out{u}") for u in range(2)]
        wgt_out = [sem(f"b_wgt_out{u}") for u in range(2)]
        key_done = sem("b_key_done")
        keyT_done = sem("b_keyT_done")
        keyT_out = sem("b_keyT_out")
        block = ctx.enter_context(nc.Block())

        def steps(eng, body):
            def chunk(n):
                return (n, n // 2, n % 2) if 0 <= n < B else None
            body(chunk(0), None)
            with eng.Fori(0, B // 2 - 1) as i:
                for u in range(2):
                    body((2 * i + 1 + u, i + u, 1 - u), (2 * i + u, i, u))
            for s in range(B - 1, B + 1):
                body(chunk(s), chunk(s - 1))

        @block.sync
        def _(sp):
            sp.dma_start(rwT[:, :, :], m.ins["rwT"].rearrange("(t p) n -> p t n", p=P)).then_inc(w_in, 16)
            sp.dma_start(bias[:, :], m.ins["ebias"].rearrange("(a n) -> a n", a=1).to_broadcast([P, E0])).then_inc(w_in, 16)
            sp.wait_ge(zeroed, 1)
            for a in m.acc:
                for c in range(T * D // (P * 2048)):
                    sp.dma_start(a[0:T, :].rearrange("(c p r) n -> c p (r n)", p=P, r=8)[c], zero[:, :]).then_inc(zero_out, 16)
                sp.dma_start(a[T:T + CAP, :], zero[0:CAP, 0:D]).then_inc(zero_out, 16)
            sp.dma_start(m.rows[T:T + CAP, :], zero[0:CAP, 0:ROW]).then_inc(zero_out, 16)

            def body(a, b):
                if a:
                    n, i, u = a
                    sp.wait_ge(h_done, CT * (n + 1))
                    sp.dma_start(m.rows[bass.ds(n * S, S), 0:D].rearrange("(t p) n -> p t n", p=P), row[u][:, :, 0:D])\
                      .then_inc(h_out[u], 16)
                if b:
                    n, i, u = b
                    sp.wait_ge(row_done, n + 1)
                    sp.dma_start(m.rows[bass.ds(n * S, S), D:ROW].rearrange("(t p) n -> p t n", p=P), row[u][:, :, D:ROW])\
                      .then_inc(wgt_out[u], 16)

            steps(sp, body)
            sp.wait_ge(zero_out, 16 * (2 * (T * D // (P * 2048) + 1) + 1))
            for u in range(2):
                sp.wait_ge(h_out[u], 16 * (B // 2))
                sp.wait_ge(wgt_out[u], 16 * (B // 2))

        @block.gpsimd
        def _(pool):
            pool.memset(zero[:, :], 0.0).then_inc(zeroed, 1)
            pool.iota(keyc[:, :], pattern=[[-P, NT]], base=T, channel_multiplier=-1,
                      allow_small_or_imprecise_dtypes=True).then_inc(keyc_made, 1)
            with pool.Fori(0, B // 2) as i:
                for u in range(2):
                    n = 2 * i + u
                    pool.wait_ge(ve_done, n + 1)
                    pool.tensor_tensor(rstd[:, :], ve[:, :], m.minus_half[:, 0:CT], ALU.pow).then_inc(rstd_done, 1)
                    pool.wait_ge(hT_out, DT * (n + 1))
                    apart(m, pool)
                    pool.tensor_copy(m.hT_all[:, :, bass.ds(n * S, S)], hT[u][:, :, :]).then_inc(hT_kept, 1)

        @block.tensor
        def _(pe):
            pe.wait_ge(w_in, 32)

            def body(a, b):
                if a:
                    n, i, u = a
                    at_least(pe, hT_out, DT * n)
                    for j in range(CT):
                        pe.wait_ge(h_done, CT * n + j + 1)
                        for d in range(DT):
                            last = pe.transpose(ps[:, d, j * P:(j + 1) * P], row[u][:, j, d * P:(d + 1) * P], m.ident[:, :])
                    last.then_inc(tr_done, 1)
                    pe.wait_ge(hT_out, DT * (n + 1))
                    at_least(pe, ex_done, n)
                    for j in range(CT):
                        for d in range(DT):
                            last = pe.matmul(ps[:, 2, j * E0:(j + 1) * E0], hT[u][:, d, j * P:(j + 1) * P], rwT[:, d, :],
                                             start=(d == 0), stop=(d == DT - 1))
                    last.then_inc(l_done, 1)
                if b:
                    n, i, u = b
                    pe.wait_ge(key_done, n + 1)
                    at_least(pe, keyT_out, n)
                    for j in range(CT // 2):
                        last = pe.transpose(ps[:, 3, j * P:(j + 1) * P],
                                            key[u][:, 2 * j:2 * j + 2, :].rearrange("p a e -> p (a e)"), m.ident[:, :])
                    last.then_inc(keyT_done, 1)

            steps(pe, body)

        @block.scalar
        def _(act):
            def body(a, b):
                if a:
                    n, i, u = a
                    act.wait_ge(tr_done, n + 1)
                    at_least(act, hT_kept, n - 1)
                    for d in range(DT):
                        act.activation(hT[u][:, d, :], ps[:, d, :], ACT.Copy).then_inc(hT_out, 1)
                    act.wait_ge(l_done, n + 1)
                    at_least(act, key_done, n - 1)
                    act.activation(ex[u][:, :, :], ps[:, 2, 0:CT * E0].rearrange("p (t e) -> p t e", t=CT), ACT.Exp,
                                   scale=-1.0).then_inc(ex_done, 1)
                if b:
                    n, i, u = b
                    act.wait_ge(keyT_done, n + 1)
                    act.activation(m.keyT[:, bass.ds(n * 2 * P, 2 * P)], ps[:, 3, 0:2 * P], ACT.Copy).then_inc(keyT_out, 1)

            steps(act, body)

        LINKS = 2 * CT + 9

        @block.vector
        def _(dve):
            dve.memset(biased[:, :, E0:E0 + 2], NEG).then_inc(preset, 1)
            dve.memset(take8[:, :, K0:R8], NEG).then_inc(preset, 1)

            def statistics(n):
                for j in range(CT):
                    dve.bn_stats(st[:, j, :], m.x[:, bass.ds(n * CT + j, 1), :]).then_inc(bn_done, 1)
                dve.wait_ge(bn_done, CT * (n + 1))
                apart(m, dve)
                for j in range(CT):
                    dve.bn_aggr(mv[:, j, :], st[:, j, :]).then_inc(aggr_done, 1)
                dve.wait_ge(aggr_done, CT * (n + 1))
                dve.tensor_scalar(ve[:, :], mv[:, :, 1], EPS, None, ALU.add).then_inc(ve_done, 1)

            def normalised(n, i, u):
                dve.wait_ge(rstd_done, n + 1)
                at_least(dve, h_out[u], 16 * i)
                for j in range(CT):
                    dve.tensor_scalar(row[u][:, j, 0:D], m.x[:, bass.ds(n * CT + j, 1), :], mv[:, j, 0:1],
                                      rstd[:, j:j + 1], ALU.subtract, ALU.mult).then_inc(h_done, 1)

            def routed(n, i, u):
                at = [0]

                def link(ins):
                    at[0] += 1
                    ins.then_inc(chain, 1)

                def linked():
                    dve.wait_ge(chain, n * LINKS + at[0])

                dve.wait_ge(ex_done, n + 1)
                link(dve.tensor_scalar(ex1[:, :, :], ex[u][:, :, :], 1.0, None, ALU.add))
                linked()
                link(dve.reciprocal(score[:, :, :], ex1[:, :, :]))
                linked()
                link(dve.tensor_tensor(biased[:, :, 0:E0], score[:, :, :],
                                       bias[:, :].unsqueeze(1).to_broadcast([P, CT, E0]), ALU.add))
                linked()
                apart(m, dve)
                for j in range(CT):
                    link(dve.max(top8[:, j, :], biased[:, j, :]))
                linked()
                link(dve.tensor_copy(take8[:, :, 0:K0], top8[:, :, 0:K0]))
                linked()
                apart(m, dve)
                for j in range(CT):
                    link(dve.match_replace(left[:, j, :], take8[:, j, :], biased[:, j, :], LOW))
                linked()
                link(dve.tensor_scalar(chosen[:, :, :], left[:, :, 0:E0], LOW, None, ALU.is_equal))
                linked()
                at_least(dve, keyT_done, 2 * i)
                dve.tensor_tensor(key[u][:, :, :], chosen[:, :, :],
                                  keyc[:, bass.ds(n * CT, CT)].unsqueeze(2).to_broadcast([P, CT, E0]), ALU.mult)\
                   .then_inc(key_done, 1)
                link(dve.tensor_tensor(wgt[:, :, :], chosen[:, :, :], score[:, :, :], ALU.mult))
                linked()
                link(dve.tensor_reduce(wsum[:, :], wgt[:, :, :], AX.X, ALU.add))
                linked()
                link(dve.tensor_scalar(wsum[:, :], wsum[:, :], 1e-20, None, ALU.add))
                linked()
                link(dve.reciprocal(wrec[:, :], wsum[:, :]))
                linked()
                assert at[0] == LINKS, at[0]
                at_least(dve, wgt_out[u], 16 * i)
                dve.scalar_tensor_tensor(row[u][:, :, D:ROW], wgt[:, :, :], m.half_gate[:, 2:3],
                                         wrec[:, :].unsqueeze(2).to_broadcast([P, CT, E0]), ALU.mult, ALU.mult)\
                   .then_inc(row_done, 1)

            statistics(0)
            dve.wait_ge(preset, 2)
            dve.wait_ge(w_in, 32)
            dve.wait_ge(keyc_made, 1)

            def body(a, b):
                if a:
                    normalised(*a)
                    if not (isinstance(a[0], int) and a[0] + 1 >= B):
                        statistics(a[0] + 1)
                if b:
                    routed(*b)

            steps(dve, body)


def shared_0(nc, m):
    with ExitStack() as ctx:
        def sb(name, shape, dt=F32):
            return ctx.enter_context(nc.sbuf_tensor(name, shape, dt))

        def sem(name):
            return counter(nc, m, ctx, name)

        FT = SF // P
        w1 = sb("s_w1", [P, DT, SF])
        w2 = sb("s_w2", [P, FT, D])
        sq = [sb(f"s_sq{f}", [P, S]) for f in range(FT)]
        mid = [sb(f"s_mid{f}", [P, S]) for f in range(FT)]
        poly = [sb(f"s_poly{f}", [P, S]) for f in range(FT)]
        arg = [sb(f"s_arg{f}", [P, S]) for f in range(FT)]
        th = [sb(f"s_th{f}", [P, S]) for f in range(FT)]
        g = [sb(f"s_g{u}", [P, FT, S]) for u in range(2)]
        eight = [sb(f"s_eight{r}", [P, R8]) for r in range(2)]
        cand = sb("s_cand", [P, CAP])
        both = sb("s_both", [E0, 2 * CAP])
        first = sb("s_first", [E0, CAP])
        empty = sb("s_empty", [CAP, E0])
        slotp = sb("s_slotp", [CAP, 1])
        tok = sb("s_tok", [CAP, E0])
        tok2 = sb("s_tok2", [CAP, E0])
        ps = ctx.enter_context(nc.psum_tensor("s_ps", [P, 8, 512], F32))

        w_in = sem("s_w_in")
        slotp_made = sem("s_slotp_made")
        mid_done = sem("s_mid_done")
        mid_kept = sem("s_mid_kept")
        sq_done = sem("s_sq_done")
        poly_done = sem("s_poly_done")
        arg_done = sem("s_arg_done")
        th_done = sem("s_th_done")
        g_done = sem("s_g_done")
        y_done = sem("s_y_done")
        x_done = sem("s_x_done")
        found = sem("s_found")
        kept = sem("s_kept")
        moved = sem("s_moved")
        firstT = sem("s_firstT")
        tok_step = sem("s_tok_step")
        block = ctx.enter_context(nc.Block())

        def chunks(eng, body):
            with eng.Fori(0, B // 2 - 1) as i:
                for u in range(2):
                    body(2 * i + u, i, u, True)
            for u in range(2):
                body(B - 2 + u, B // 2 - 1, u, u == 0)

        @block.sync
        def _(sp):
            sp.dma_start(w1[:, :, :], m.ins["sw1T"].rearrange("(t p) n -> p t n", p=P)).then_inc(w_in, 16)
            sp.dma_start(w2[:, :, :], m.ins["sw2T"].rearrange("(t p) n -> p t n", p=P)).then_inc(w_in, 16)
            sp.wait_ge(kept, ROUNDS)
            sp.dma_start(both[:, 0:CAP], cand[0:E0, :]).then_inc(moved, 16)
            sp.dma_start(both[:, CAP:2 * CAP], cand[E0:2 * E0, :]).then_inc(moved, 16)

        @block.gpsimd
        def _(pool):
            pool.iota(slotp[:, :], pattern=[[0, 1]], base=0, channel_multiplier=1,
                      allow_small_or_imprecise_dtypes=True).then_inc(slotp_made, 1)
            with pool.Fori(0, B) as n:
                for f in range(FT):
                    pool.wait_ge(sq_done, FT * n + f + 1)
                    apart(m, pool)
                    pool.tensor_scalar(poly[f][:, :], sq[f][:, :], GELU_A, 1.0, ALU.mult, ALU.add)\
                        .then_inc(poly_done, 1)
                    pool.wait_ge(mid_kept, FT * n + f + 1)
                    pool.wait_ge(poly_done, FT * n + f + 1)
                    pool.wait_ge(th_done, FT * n)
                    pool.tensor_tensor(arg[f][:, :], poly[f][:, :], mid[f][:, :], ALU.mult).then_inc(arg_done, 1)

        @block.tensor
        def _(pe):
            pe.wait_ge(w_in, 32)

            def hidden(n):
                for f in range(FT):
                    if not (isinstance(n, int) and n == 0):
                        pe.wait_ge(g_done, FT * (n - 1) + f + 1)
                    for d in range(DT):
                        last = pe.matmul(ps[:, f, :], w1[:, d, f * P:(f + 1) * P],
                                         m.hT_all[:, d, bass.ds(n * S, S)], start=(d == 0), stop=(d == DT - 1))
                    last.then_inc(mid_done, 1)

            def body(n, i, u, ahead):
                if ahead:
                    hidden(n + 1)
                pe.wait_ge(g_done, FT * n + FT)
                if not ahead:
                    pe.wait_ge(found, 4 * ROUNDS)
                    pe.transpose(ps[0:CAP, 0, 0:E0], first[:, :], m.ident[0:E0, 0:E0]).then_inc(firstT, 1)
                for t in range(CT):
                    pe.wait_ge(x_done, CT * n)
                    for f in range(FT):
                        last = pe.matmul(ps[:, 4 + 2 * u + t // 2, (t % 2) * D:(t % 2 + 1) * D], g[u][:, f, t * P:(t + 1) * P], w2[:, f, :],
                                         start=(f == 0), stop=(f == FT - 1))
                    last.then_inc(y_done, 1)

            hidden(0)
            chunks(pe, body)

        @block.scalar
        def _(act):
            with act.Fori(0, B) as n:
                for f in range(FT + 1):
                    if f < FT:
                        act.wait_ge(mid_done, FT * n + f + 1)
                        act.wait_ge(poly_done, FT * n)
                        act.activation(sq[f][:, :], ps[:, f, :], ACT.Square).then_inc(sq_done, 1)
                        act.wait_ge(arg_done, FT * n)
                        act.activation(mid[f][:, :], ps[:, f, :], ACT.Copy).then_inc(mid_kept, 1)
                    if f:
                        act.wait_ge(arg_done, FT * n + f)
                        act.wait_ge(g_done, FT * n)
                        act.activation(th[f - 1][:, :], arg[f - 1][:, :], ACT.Tanh, scale=GELU_C)\
                           .then_inc(th_done, 1)

        @block.vector
        def _(dve):
            def find(keys, out, at):
                dve.wait_ge(found, at)
                apart(m, dve)
                dve.max(out, keys).then_inc(found, 1)
                dve.wait_ge(found, at + 1)
                apart(m, dve)
                dve.match_replace(keys, out, keys, 0.0).then_inc(found, 1)

            def slots():
                dve.wait_ge(firstT, 1)
                dve.wait_ge(slotp_made, 1)
                dve.tensor_scalar(empty[:, :], ps[0:CAP, 0, 0:E0], 0.0, slotp[:, 0:1], ALU.is_equal, ALU.mult).then_inc(tok_step, 1)
                dve.tensor_scalar(tok[:, :], ps[0:CAP, 0, 0:E0], -1.0, float(T), ALU.mult, ALU.add).then_inc(tok_step, 1)
                dve.wait_ge(tok_step, 2)
                dve.tensor_tensor(tok2[:, :], tok[:, :], empty[:, :], ALU.add).then_inc(tok_step, 1)
                dve.wait_ge(tok_step, 3)
                dve.tensor_copy(m.slots0[:, :], tok2[:, :]).then_inc(tok_step, 1)

            def gelu(n, u):
                for f in range(FT + 1):
                    if f:
                        dve.wait_ge(th_done, FT * n + f)
                        if not (isinstance(n, int) and n < 2):
                            dve.wait_ge(y_done, CT * (n - 1))
                        dve.scalar_tensor_tensor(g[u][:, f - 1, :], th[f - 1][:, :], 1.0, ps[:, f - 1, :],
                                                 ALU.add, ALU.mult).then_inc(g_done, 1)

            def body(n, i, u, ahead):
                if ahead:
                    gelu(n + 1, 1 - u)
                if not isinstance(n, int):
                    for r in range(2):
                        find(m.keyT[:, :], eight[r][:, :], 4 * n + 2 * r)
                        dve.tensor_copy(cand[:, bass.ds((2 * n + r) * R8, R8)], eight[r][:, :]).then_inc(kept, 1)
                elif n == B - 2:
                    dve.wait_ge(moved, 32)
                    for r in range(ROUNDS):
                        find(both[:, :], first[:, r * R8:(r + 1) * R8], 2 * ROUNDS + 2 * r)
                else:
                    slots()
                for t in range(CT):
                    dve.wait_ge(y_done, CT * n + t // 2 * 2 + 2)
                    xt = m.x[:, bass.ds(n * CT + t, 1), :]
                    dve.scalar_tensor_tensor(xt, ps[:, 4 + 2 * u + t // 2:5 + 2 * u + t // 2, (t % 2) * D:(t % 2 + 1) * D], m.half_gate[:, 2:3], xt, ALU.mult, ALU.add)\
                       .then_inc(x_done, 1)

            assert ROUNDS == 2 * (B - 2)
            dve.sem_inc(x_done, CT)
            gelu(0, 0)
            chunks(dve, body)
            dve.wait_ge(tok_step, 4)


def experts_0(nc, m):
    NB = 8
    AHEAD = 4
    with ExitStack() as ctx:
        def sb(name, shape, dt=F32):
            return ctx.enter_context(nc.sbuf_tensor(name, shape, dt))

        def sem(name):
            return counter(nc, m, ctx, name)

        w1 = [sb(f"e_w1{u}", [P, DT, F0]) for u in range(NB)]
        w2 = [sb(f"e_w2{u}", [P, D]) for u in range(NB)]
        idx = [sb(f"e_idx{u}", [CAP, 1], I32) for u in range(NB)]
        xg = [sb(f"e_xg{u}", [CAP, ROW]) for u in range(NB)]
        xgT = [sb(f"e_xgT{u}", [P, DT, CAP]) for u in range(2)]
        mid = [sb(f"e_mid{u}", [P, CAP]) for u in range(2)]
        sq = [sb(f"e_sq{u}", [P, CAP]) for u in range(2)]
        poly = [sb(f"e_poly{u}", [P, CAP]) for u in range(2)]
        arg = [sb(f"e_arg{u}", [P, CAP]) for u in range(2)]
        th = [sb(f"e_th{u}", [P, CAP]) for u in range(2)]
        g = [sb(f"e_g{u}", [P, CAP]) for u in range(2)]
        y = [sb(f"e_y{u}", [CAP, D]) for u in range(NB)]
        ps = ctx.enter_context(nc.psum_tensor("e_ps", [P, 8, 512], F32))

        w_in = [sem(f"e_w_in{u}") for u in range(NB)]
        idx_done = sem("e_idx_done")
        x_in = [dma_counter(nc, m, f"e_x_in{u}") for u in range(NB)]
        xT_done = sem("e_xT_done")
        xT_out = sem("e_xT_out")
        mid_done = sem("e_mid_done")
        mid_out = sem("e_mid_out")
        step = sem("e_step")
        th_done = sem("e_th_done")
        g_done = sem("e_g_done")
        y_done = sem("e_y_done")
        y_out = sem("e_y_out")
        added = [dma_counter(nc, m, f"e_added{u}") for u in range(NB)]
        block = ctx.enter_context(nc.Block())

        def experts(eng, body):
            with eng.Fori(0, E0 // NB - 1) as i:
                for u in range(NB):
                    body(NB * i + u, i, u)
            for u in range(NB):
                body(E0 - NB + u, E0 // NB - 1, u)

        def there(e):
            return not (isinstance(e, int) and e >= E0)

        @block.sync
        def _(sp):
            with sp.Fori(0, E0 // NB) as i:
                for u in range(NB):
                    e = NB * i + u
                    sp.wait_ge(added[u], 16 * i)
                    sp.dma_start(w1[u][:, :, :], m.ins["w1"][bass.ds(e, 1)].rearrange("a (t p) f -> p (a t) f", p=P)).then_inc(w_in[u], 16)
                    sp.dma_start(w2[u][:, :], m.ins["w2"][bass.ds(e, 1)].rearrange("a f d -> f (a d)")).then_inc(w_in[u], 16)

        @block.gpsimd
        def _(pool):
            def gather(e, u):
                pool.wait_ge(idx_done, e + 1)
                apart(m, pool)
                pool.indirect_dma_start(xg[u][:, :], None, m.rows[:, :],
                                        bass.IndirectOffsetOnAxis(ap=idx[u][:, :], axis=0)).then_inc(x_in[u], 16)

            for e in range(AHEAD):
                gather(e, e)

            def body(e, i, u):
                if there(e + AHEAD):
                    gather(e + AHEAD, (u + AHEAD) % NB)
                pool.wait_ge(y_out, e + 1)
                if u >= 2:
                    pool.wait_ge(added[u - 2], 16 * i + 16)
                else:
                    pool.wait_ge(added[NB + u - 2], 16 * i)
                apart(m, pool)
                pool.indirect_dma_start(m.acc[u % 2], bass.IndirectOffsetOnAxis(ap=idx[u][:, :], axis=0),
                                        y[u][:, :], None, compute_op=ALU.add).then_inc(added[u], 16)

            experts(pool, body)
            for u in range(NB):
                pool.wait_ge(added[u], 16 * (E0 // NB))

        @block.tensor
        def _(pe):
            def rows(e, i, u):
                v = u % 2
                pe.wait_ge(x_in[u], 16 * i + 16)
                if not (isinstance(e, int) and e < 2):
                    pe.wait_ge(xT_out, e - 1)
                for d in range(DT):
                    last = pe.transpose(ps[:, v, d * P:d * P + CAP], xg[u][:, d * P:(d + 1) * P], m.ident[0:CAP, 0:CAP])
                last.then_inc(xT_done, 1)

            def first_layer(e, i, u):
                v = u % 2
                pe.wait_ge(xT_out, e + 1)
                pe.wait_ge(w_in[u], 32 * i + 32)
                if not (isinstance(e, int) and e < 2):
                    pe.wait_ge(mid_out, e - 1)
                for d in range(DT):
                    last = pe.matmul(ps[:, 2 + v, 0:CAP], w1[u][:, d, :], xgT[v][:, d, :],
                                     start=(d == 0), stop=(d == DT - 1))
                last.then_inc(mid_done, 1)

            rows(0, 0, 0)
            rows(1, 0, 1)
            first_layer(0, 0, 0)

            def body(e, i, u):
                v = u % 2
                if there(e + 2):
                    rows(e + 2, i + (u + 2) // NB, (u + 2) % NB)
                if there(e + 1):
                    first_layer(e + 1, i + (u + 1) // NB, (u + 1) % NB)
                pe.wait_ge(g_done, e + 1)
                if u >= 2:
                    pe.wait_ge(y_out, e - 1)
                elif not (isinstance(i, int) and i == 0):
                    pe.wait_ge(y_out, e)
                pe.matmul(ps[0:CAP, 4 + v, 0:D], g[v][:, :], w2[u][:, :], start=True, stop=True).then_inc(y_done, 1)

            experts(pe, body)

        @block.scalar
        def _(act):
            def rows(e, v):
                act.wait_ge(xT_done, e + 1)
                if not (isinstance(e, int) and e < 2):
                    act.wait_ge(mid_done, e - 1)
                act.activation(xgT[v][:, :, :], ps[:, v, 0:DT * P].rearrange("p (d c) -> p d c", d=DT)[:, :, 0:CAP],
                               ACT.Copy).then_inc(xT_out, 1)

            def hidden(e, v):
                act.wait_ge(mid_done, e + 1)
                if not (isinstance(e, int) and e < 2):
                    act.wait_ge(g_done, e - 1)
                act.activation(mid[v][:, :], ps[:, 2 + v, 0:CAP], ACT.Copy).then_inc(mid_out, 1)

            def tanh(e, v):
                act.wait_ge(step, 3 * e + 3)
                act.activation(th[v][:, :], arg[v][:, :], ACT.Tanh, scale=GELU_C).then_inc(th_done, 1)

            rows(0, 0)
            rows(1, 1)
            hidden(0, 0)
            tanh(0, 0)

            def body(e, i, u):
                v = u % 2
                if there(e + 2):
                    rows(e + 2, v)
                if there(e + 1):
                    hidden(e + 1, 1 - v)
                act.wait_ge(y_done, e + 1)
                act.wait_ge(added[u], 16 * i)
                act.wait_ge(x_in[u], 16 * i + 16)
                act.activation(y[u][:, :], ps[0:CAP, 4 + v, 0:D], ACT.Copy, scale=xg[u][:, bass.ds(D + e, 1)])\
                   .then_inc(y_out, 1)
                if there(e + 1):
                    tanh(e + 1, 1 - v)

            experts(act, body)

        @block.vector
        def _(dve):
            def index(e, i, u):
                if not (isinstance(i, int) and i == 0):
                    dve.wait_ge(added[u], 16 * i)
                dve.tensor_copy(idx[u][:, :], m.slots0[:, bass.ds(e, 1)]).then_inc(idx_done, 1)

            def gelu(e, v):
                dve.wait_ge(mid_out, e + 1)
                dve.tensor_tensor(sq[v][:, :], mid[v][:, :], mid[v][:, :], ALU.mult).then_inc(step, 1)
                dve.wait_ge(step, 3 * e + 1)
                dve.tensor_scalar(poly[v][:, :], sq[v][:, :], GELU_A, 1.0, ALU.mult, ALU.add).then_inc(step, 1)
                dve.wait_ge(step, 3 * e + 2)
                dve.tensor_tensor(arg[v][:, :], poly[v][:, :], mid[v][:, :], ALU.mult).then_inc(step, 1)
                dve.wait_ge(th_done, e + 1)
                if not (isinstance(e, int) and e < 2):
                    dve.wait_ge(y_done, e - 1)
                dve.scalar_tensor_tensor(g[v][:, :], th[v][:, :], 1.0, mid[v][:, :], ALU.add, ALU.mult).then_inc(g_done, 1)

            for e in range(AHEAD):
                index(e, 0, e)
            gelu(0, 0)

            def body(e, i, u):
                if there(e + AHEAD):
                    index(e + AHEAD, i + (u + AHEAD) // NB, (u + AHEAD) % NB)
                if there(e + 1):
                    gelu(e + 1, (u + 1) % 2)

            experts(dve, body)


H1, HD = 16, 16
HG = 4
NGRP = H1 // HG
PARTS = 3
KS = 6 * HD
VW = 32


def project_1(nc, m):
    with ExitStack() as ctx:
        def sb(name, shape, dt=F32):
            return ctx.enter_context(nc.sbuf_tensor(name, shape, dt))

        def sem(name):
            return counter(nc, m, ctx, name)

        acc = [[sb(f"p_acc{a}{u}", [P, CT, D]) for u in range(2)] for a in range(2)]
        cT = [sb(f"p_cT{u}", [P, DT, S]) for u in range(2)]
        h = sb("p_h", [P, CT, D])
        hT = sb("p_hT", [P, DT, S])
        wq = sb("p_wq", [P, DT, D])
        wk = sb("p_wk", [P, DT, D])
        wv = sb("p_wv", [P, DT, D])
        qkb = sb("p_qkb", [P, 2, DT])
        vb = sb("p_vb", [P, D])
        st = sb("p_st", [P, CT, 6])
        mv = sb("p_mv", [P, CT, 2])
        ve = sb("p_ve", [P, CT])
        rstd = sb("p_rstd", [P, CT])
        full = [sb(f"p_full{a}", [P, DT, S]) for a in range(2)]
        rest = [sb(f"p_rest{a}", [P, DT, S]) for a in range(2)]
        part = [[sb(f"p_part{a}{c}", [P, DT, S], BF16) for c in range(PARTS)] for a in range(2)]
        v = [sb(f"p_v{u}", [P, CT, H1, VW]) for u in range(2)]
        ps = ctx.enter_context(nc.psum_tensor("p_ps", [P, 8, 512], F32))

        w_in = sem("p_w_in")
        b_in = sem("p_b_in")
        acc_in = [sem(f"p_acc_in{u}") for u in range(2)]
        ctx_in = [sem(f"p_ctx_in{u}") for u in range(2)]
        preset = sem("p_preset")
        chain = sem("p_chain")
        x_done = sem("p_x_done")
        x_stored = sem("p_x_stored")
        ve_done = sem("p_ve_done")
        rstd_done = sem("p_rstd_done")
        h_done = sem("p_h_done")
        tr_done = sem("p_tr_done")
        hT_out = sem("p_hT_out")
        q_done = sem("p_q_done")
        k_done = sem("p_k_done")
        v_done = sem("p_v_done")
        full_done = [sem(f"p_full_done{a}") for a in range(2)]
        hi_done = [sem(f"p_hi_done{a}") for a in range(2)]
        rest_done = [sem(f"p_rest_done{a}") for a in range(2)]
        mid_done = [sem(f"p_mid_done{a}") for a in range(2)]
        lo_done = [sem(f"p_lo_done{a}") for a in range(2)]
        part_out = [sem(f"p_part_out{a}") for a in range(2)]
        v_out = sem("p_v_out")
        v_stored = [sem(f"p_v_stored{u}") for u in range(2)]
        block = ctx.enter_context(nc.Block())

        def chunks(eng, body):
            with eng.Fori(0, B // 2 - 1) as i:
                for u in range(2):
                    body(2 * i + u, i, u, True)
            for u in range(2):
                body(B - 2 + u, B // 2 - 1, u, u == 0)

        @block.sync
        def _(sp):
            def load_acc(n, u):
                for a in range(2):
                    sp.dma_start(acc[a][u][:, :, :], m.acc[a][0:T, :].rearrange("(c t p) d -> p c t d", p=P, t=CT)
                                 [:, bass.ds(n, 1)].rearrange("p a t d -> p (a t) d")).then_inc(acc_in[u], 16)

            def load_ctx(n, u):
                sp.dma_start(cT[u][:, :, :], m.ins["ctxT"].rearrange("(t p) n -> p t n", p=P)[:, :, bass.ds(n * S, S)])\
                  .then_inc(ctx_in[u], 16)

            def store(a, n):
                sp.wait_ge(hi_done[a], n + 1)
                apart(m, sp)
                sp.wait_ge(mid_done[a], n + 1)
                sp.wait_ge(lo_done[a], n + 1)
                for c in range(PARTS):
                    dst = m.qk[a].rearrange("b c (t p) s -> p b c t s", p=P)[:, bass.ds(n, 1), c]
                    sp.dma_start(dst.rearrange("p b t s -> p (b t) s"), part[a][c][:, :, :]).then_inc(part_out[a], 16)

            load_acc(0, 0)
            load_ctx(0, 0)
            for w, name in ((wk, "WkT1"), (wv, "WvT1"), (wq, "WqT1")):
                sp.dma_start(w[:, :, :], m.ins[name].rearrange("(t p) n -> p t n", p=P)).then_inc(w_in, 16)
            load_acc(1, 1)
            load_ctx(1, 1)

            def body(n, i, u, ahead):
                more = not isinstance(i, int)
                if more:
                    sp.wait_ge(x_done, n + 1)
                    load_acc(n + 2, u)
                else:
                    sp.wait_ge(x_done, n + 1)
                sp.dma_start(m.sums[bass.ds(n * S, S), :].rearrange("(t p) n -> p t n", p=P), m.x[:, bass.ds(n * CT, CT), :])\
                  .then_inc(x_stored, 16)
                store(1, n)
                sp.wait_ge(v_out, 2 * n + 2)
                sp.dma_start(m.v.rearrange("(c t p) e -> p c t e", p=P, t=CT)[:, bass.ds(n, 1)]
                             .rearrange("p a t e -> p (a t) e"), v[u][:, :, :, :].rearrange("p t h w -> p t (h w)"))\
                  .then_inc(v_stored[u], 16)
                if more:
                    sp.wait_ge(v_done, 2 * n + 2)
                    load_ctx(n + 2, u)
                store(0, n)

            chunks(sp, body)
            sp.wait_ge(x_stored, 16 * B)
            for a in range(2):
                sp.wait_ge(part_out[a], 16 * PARTS * B)
            for u in range(2):
                sp.wait_ge(v_stored[u], 16 * (B // 2))

        @block.gpsimd
        def _(pool):
            for u in range(2):
                pool.memset(v[u][:, :, :, HD:VW], 0.0).then_inc(preset, 1)
            pool.wait_ge(preset, 2)
            for u in range(2):
                pool.memset(v[u][:, :, :, HD:HD + 1], 1.0).then_inc(preset, 1)
            with pool.Fori(0, B) as n:
                pool.wait_ge(ve_done, n + 1)
                pool.tensor_tensor(rstd[:, :], ve[:, :], m.minus_half[:, 0:CT], ALU.pow).then_inc(rstd_done, 1)

        @block.tensor
        def _(pe):
            pe.wait_ge(w_in, 48)

            def body(n, i, u, ahead):
                pe.wait_ge(hT_out, DT * n)
                for j in range(CT):
                    pe.wait_ge(h_done, CT * n + j + 1)
                    for d in range(DT):
                        last = pe.transpose(ps[:, d, j * P:(j + 1) * P], h[:, j, d * P:(d + 1) * P], m.ident[:, :])
                last.then_inc(tr_done, 1)
                pe.wait_ge(ctx_in[u], 16 * i + 16)
                pe.wait_ge(full_done[1], DT * n)
                for e in range(DT):
                    for d in range(DT):
                        last = pe.matmul(ps[:, 4 + e, :], wk[:, d, e * P:(e + 1) * P], cT[u][:, d, :],
                                         start=(d == 0), stop=(d == DT - 1))
                    last.then_inc(k_done, 1)
                pe.wait_ge(v_out, 2 * n)
                for t in range(CT):
                    for d in range(DT):
                        last = pe.matmul(ps[:, 6 + t // 2, (t % 2) * D:(t % 2 + 1) * D], cT[u][:, d, t * P:(t + 1) * P],
                                         wv[:, d, :], start=(d == 0), stop=(d == DT - 1))
                    if t % 2:
                        last.then_inc(v_done, 1)
                pe.wait_ge(hT_out, DT * (n + 1))
                pe.wait_ge(full_done[0], DT * n)
                for e in range(DT):
                    for d in range(DT):
                        last = pe.matmul(ps[:, 2 + e, :], wq[:, d, e * P:(e + 1) * P], hT[:, d, :],
                                         start=(d == 0), stop=(d == DT - 1))
                    last.then_inc(q_done, 1)

            chunks(pe, body)

        @block.scalar
        def _(act):
            act.dma_start(qkb[:, 0, :], m.ins["bq"]).then_inc(b_in, 16)
            act.dma_start(qkb[:, 1, :], m.ins["bk"]).then_inc(b_in, 16)
            act.dma_start(vb[:, :], m.ins["bv"].rearrange("(a n) -> a n", a=1).to_broadcast([P, D])).then_inc(b_in, 16)
            act.wait_ge(b_in, 48)

            def body(n, i, u, ahead):
                def biased(a, done):
                    act.wait_ge(rest_done[a], n)
                    for e in range(DT):
                        act.wait_ge(done, DT * n + e + 1)
                        act.activation(full[a][:, e, :], ps[:, (2, 4)[a] + e, :], ACT.Identity, bias=qkb[:, a, e:e + 1])\
                           .then_inc(full_done[a], 1)

                def part_0(a):
                    act.wait_ge(full_done[a], DT * (n + 1))
                    act.wait_ge(part_out[a], 16 * PARTS * n)
                    act.activation(part[a][0][:, :, :], full[a][:, :, :], ACT.Copy).then_inc(hi_done[a], 1)

                def part_1(a):
                    act.wait_ge(rest_done[a], n + 1)
                    act.activation(part[a][1][:, :, :], rest[a][:, :, :], ACT.Copy).then_inc(mid_done[a], 1)

                act.wait_ge(tr_done, n + 1)
                act.wait_ge(q_done, DT * n)
                for d in range(DT):
                    act.activation(hT[:, d, :], ps[:, d, :], ACT.Copy).then_inc(hT_out, 1)
                biased(1, k_done)
                part_0(1)
                part_1(1)
                biased(0, q_done)
                part_0(0)
                part_1(0)

            chunks(act, body)

        LINKS = 1 + 2 * CT

        @block.vector
        def _(dve):
            def statistics(n, i, u):
                at = [0]

                def link(ins):
                    at[0] += 1
                    ins.then_inc(chain, 1)

                def linked():
                    dve.wait_ge(chain, n * LINKS + at[0])

                xc = m.x[:, bass.ds(n * CT, CT), :]
                dve.wait_ge(acc_in[u], 32 * i + 32)
                link(dve.tensor_tensor(xc, xc, acc[0][u][:, :, :], ALU.add))
                linked()
                dve.tensor_tensor(xc, xc, acc[1][u][:, :, :], ALU.add).then_inc(x_done, 1)
                dve.wait_ge(x_done, n + 1)
                apart(m, dve)
                for j in range(CT):
                    link(dve.bn_stats(st[:, j, :], m.x[:, bass.ds(n * CT + j, 1), :]))
                linked()
                apart(m, dve)
                for j in range(CT):
                    link(dve.bn_aggr(mv[:, j, :], st[:, j, :]))
                linked()
                assert at[0] == LINKS
                dve.tensor_scalar(ve[:, :], mv[:, :, 1], EPS, None, ALU.add).then_inc(ve_done, 1)

            def normalised(n):
                dve.wait_ge(rstd_done, n + 1)
                if not (isinstance(n, int) and n == 0):
                    dve.wait_ge(tr_done, n)
                for j in range(CT):
                    dve.tensor_scalar(h[:, j, :], m.x[:, bass.ds(n * CT + j, 1), :], mv[:, j, 0:1],
                                      rstd[:, j:j + 1], ALU.subtract, ALU.mult).then_inc(h_done, 1)

            statistics(0, 0, 0)
            normalised(0)
            dve.wait_ge(preset, 4)
            dve.wait_ge(b_in, 48)

            def body(n, i, u, ahead):
                def remainders(a):
                    dve.wait_ge(hi_done[a], n + 1)
                    dve.tensor_tensor(rest[a][:, :, :], full[a][:, :, :], part[a][0][:, :, :], ALU.subtract)\
                       .then_inc(rest_done[a], 1)

                def last_part(a):
                    dve.wait_ge(mid_done[a], n + 1)
                    dve.tensor_tensor(part[a][2][:, :, :], rest[a][:, :, :], part[a][1][:, :, :], ALU.subtract)\
                       .then_inc(lo_done[a], 1)

                if ahead:
                    statistics(n + 1, i + u, 1 - u)
                remainders(1)
                if ahead:
                    normalised(n + 1)
                for w in range(2):
                    dve.wait_ge(v_done, 2 * n + w + 1)
                    if w == 0:
                        dve.wait_ge(v_stored[u], 16 * i)
                    dve.tensor_tensor(v[u][:, 2 * w:2 * w + 2, :, 0:HD],
                                      ps[:, 6 + w, :].rearrange("p (t h w) -> p t h w", t=2, w=HD),
                                      vb[:, :].rearrange("p (a h w) -> p a h w", a=1, w=HD).to_broadcast([P, 2, H1, HD]),
                                      ALU.add).then_inc(v_out, 1)
                last_part(1)
                remainders(0)
                last_part(0)

            chunks(dve, body)


def attention_1(nc, m):
    GROUPS = B * NGRP
    NB = 4
    NBANK = 3
    NPR = 8
    LAG_T, LAG_O = 6, 7
    STEPS = CT * HG
    MR = PARTS * HG
    with ExitStack() as ctx:
        def sb(name, shape, dt=F32):
            return ctx.enter_context(nc.sbuf_tensor(name, shape, dt))

        def sem(name):
            return counter(nc, m, ctx, name)

        qs = [sb(f"t_qs{g}", [P, HG, S], BF16) for g in range(NB)]
        ks = [sb(f"t_ks{g}", [P, HG, S], BF16) for g in range(NB)]
        va = [sb(f"t_va{g}", [P, CT, HG * VW]) for g in range(NB)]
        pr = sb("t_pr", [P, NPR, S])
        nm = [sb(f"t_nm{u}", [P, STEPS]) for u in range(2)]
        nr = [sb(f"t_nr{w}", [P, STEPS]) for w in range(2)]
        n3 = [sb(f"t_n3{u}", [P, STEPS, PARTS], BF16) for u in range(2)]
        mT = sb("t_mT", [P, S], BF16)
        pick = sb("t_pick", [P, HG], BF16)
        ot = [sb(f"t_ot{u}", [P, S]) for u in range(2)]
        rec = [sb(f"t_rec{u}", [P, STEPS]) for u in range(2)]
        att = [sb(f"t_att{u}", [P, CT, HG * HD]) for u in range(2)]
        ps = ctx.enter_context(nc.psum_tensor("t_ps", [P, 8, 512], F32))
        O, X = 2 * NBANK, 2 * NBANK + 1

        preset = sem("t_preset")
        picked = sem("t_picked")
        q_in = [sem(f"t_q_in{g}") for g in range(NB)]
        k_in = [sem(f"t_k_in{g}") for g in range(NB)]
        s_done = sem("t_s_done")
        max_done = sem("t_max_done")
        cut = sem("t_cut")
        mT_done = sem("t_mT_done")
        mT_out = sem("t_mT_out")
        mT_spread = sem("t_mT_spread")
        z_done = sem("t_z_done")
        p_done = sem("t_p_done")
        o_done = sem("t_o_done")
        pv_done = sem("t_pv_done")
        ot_out = sem("t_ot_out")
        oT_done = sem("t_oT_done")
        rec_done = sem("t_rec_done")
        att_done = sem("t_att_done")
        att_stored = [sem(f"t_att_stored{u}") for u in range(2)]
        block = ctx.enter_context(nc.Block())

        def parts(eng, part, last=GROUPS + 2):
            def whole(k):
                part(k, k // NB + 1, k % NB, (k - 2) // NGRP, (k < GROUPS, 1 <= k < GROUPS + 1, k >= 2))
            whole(0)
            whole(1)
            with eng.Fori(0, (GROUPS - NB) // NB) as i:
                for w in range(NB):
                    part(NB * i + 2 + w, i + (2 + w) // NB + 1, (2 + w) % NB, i, (True, True, True))
            for k in range(GROUPS - 2, last):
                whole(k)

        def lagged(k, b, lag):
            back = -((b - lag) // CT)
            return back, (b - lag) % CT

        @block.sync
        def _(sp):
            def load(g, n):
                def rows(a, c, parts):
                    whole = m.qk[a].rearrange("b c (g d j) s -> b c g d (j s)", g=NGRP, d=HD)
                    return whole[bass.ds(n, 1), c:c + parts, g].rearrange("a c d e -> (a c) d e")
                r = 0
                for parts in (3, 2, 1):
                    sp.dma_start(qs[g][r:r + parts * HD, :, :].rearrange("p j s -> p (j s)"), rows(0, 0, parts)).then_inc(q_in[g], 16)
                    sp.dma_start(ks[g][r:r + parts * HD, :, :].rearrange("p j s -> p (j s)"),
                                 rows(1, PARTS - parts, 1).to_broadcast([parts, HD, HG * S]))\
                      .then_inc(k_in[g], 16)
                    r += parts * HD
                src = m.v.rearrange("(b t p) (g e) -> p b g t e", p=P, t=CT, g=NGRP)
                sp.dma_start(va[g][:, :, :], src[:, bass.ds(n, 1), g].rearrange("p a t e -> p (a t) e"))\
                  .then_inc(k_in[g], 16)

            for g in range(NB):
                load(g, 0)

            def weights(e, piece):
                at = (0, DT * H2, 2 * DT * H2, 2 * DT * H2 + (FT1 - 1) * D)[piece]
                if piece < 2:
                    dst = m.W[:, bass.ds(e * WE + at, DT * H2)].rearrange("p (t h) -> p t h", t=DT)
                    src = m.ins[("W1T", "W3T")[piece]][bass.ds(e, 1)].rearrange("a (t p) h -> p (a t) h", p=P)
                elif piece == 2:
                    dst = m.W[:, bass.ds(e * WE + at, (FT1 - 1) * D)].rearrange("p (t d) -> p t d", d=D)
                    src = m.ins["W2T"][bass.ds(e, 1), 0:(FT1 - 1) * P, :].rearrange("a (t p) d -> p (a t) d", p=P)
                else:
                    dst = m.W[0:FL, bass.ds(e * WE + at, D)]
                    src = m.ins["W2T"][bass.ds(e, 1), (FT1 - 1) * P:H2, :].rearrange("a p d -> p (a d)")
                sp.dma_start(dst, src).then_inc(m.w_in, 16)

            def part(k, turn, g, n, live):
                if live[1]:
                    sp.wait_ge(mT_out, k)
                    sp.dma_start(qs[(g - 1) % NB][KS:KS + MR, :, :],
                                 mT[KS:KS + MR, :].unsqueeze(1).to_broadcast([MR, HG, S])).then_inc(mT_spread, 16)
                if live[0]:
                    weights(turn - 1, g)
                if live[2] and not (isinstance(k, int) and k + 2 >= GROUPS):
                    sp.wait_ge(o_done, k - 1)
                    load((g + 2) % NB, n + 1)

            assert GROUPS == NB * E1
            parts(sp, part, GROUPS + 1)

        @block.gpsimd
        def _(pool):
            pool.memset(pick[KS:P, :], 0.0).then_inc(preset, 1)
            for c in range(PARTS):
                pool.wait_ge(preset, c + 1)
                pool.affine_select(out=pick[KS:P, :], in_=pick[KS:P, :], compare_op=ALU.not_equal, fill=1.0,
                                   base=-c, pattern=[[-PARTS, HG]], channel_multiplier=1).then_inc(preset, 1)

            def part(k, turn, g, n, live):
                if live[0]:
                    u = g % 2
                    pool.wait_ge(max_done, STEPS * (k + 1))
                    at_least(pool, mT_done, k - 1)
                    apart(m, pool)
                    pool.tensor_copy(n3[u][:, :, 0], nm[u][:, :]).then_inc(cut, 1)
                    pool.wait_ge(cut, 5 * k + 1)
                    pool.tensor_tensor(nr[0][:, :], nm[u][:, :], n3[u][:, :, 0], ALU.subtract).then_inc(cut, 1)
                    pool.wait_ge(cut, 5 * k + 2)
                    apart(m, pool)
                    pool.tensor_copy(n3[u][:, :, 1], nr[0][:, :]).then_inc(cut, 1)
                    pool.wait_ge(cut, 5 * k + 3)
                    pool.tensor_tensor(nr[1][:, :], nr[0][:, :], n3[u][:, :, 1], ALU.subtract).then_inc(cut, 1)
                    pool.wait_ge(cut, 5 * k + 4)
                    apart(m, pool)
                    pool.tensor_copy(n3[u][:, :, 2], nr[1][:, :]).then_inc(cut, 1)
                if live[2]:
                    gg = (g - 2) % NB
                    pool.wait_ge(att_done, k - 1)
                    apart(m, pool)
                    rows = m.att[bass.ds(n * S, S), gg * HG * HD:(gg + 1) * HG * HD]
                    pool.dma_start(rows.rearrange("(t p) w -> p t w", p=P), att[g % 2][:, :, :])\
                        .then_inc(att_stored[g % 2], 16)

            parts(pool, part)
            for u in range(2):
                pool.wait_ge(att_stored[u], 16 * (GROUPS // 2))

        @block.tensor
        def _(pe):
            def maxima_scores(k, turn, g, b, j):
                if b == 0 and j == 0:
                    pe.wait_ge(q_in[g], 16 * 3 * turn)
                    pe.wait_ge(k_in[g], 16 * 4 * turn)
                x = HG * b + j
                at_least(pe, max_done, STEPS * k + (0 if x < NBANK else x - NBANK + 1))
                pe.matmul(ps[:, x % NBANK, :], qs[g][0:KS, j, b * P:(b + 1) * P], ks[g][0:KS, j, :],
                          start=True, stop=True).then_inc(s_done, 1)

            def probability_scores(k, g, b, j):
                if b == 0 and j == 0:
                    if isinstance(k, int) and k < NB:
                        pe.wait_ge(picked, k + 1)
                    pe.wait_ge(mT_spread, 16 * (k + 1))
                x = HG * b + j
                at_least(pe, p_done, STEPS * k + (0 if x < NBANK else x - NBANK + 1))
                pe.matmul(ps[:, NBANK + x % NBANK, :], ks[g][0:KS + MR, j, b * P:(b + 1) * P], qs[g][0:KS + MR, j, :],
                          start=True, stop=True).then_inc(z_done, 1)

            def times_v(k, g, b):
                if b == 0:
                    at_least(pe, ot_out, k)
                pe.wait_ge(p_done, STEPS * k + HG * b + HG)
                for j in range(HG):
                    last = pe.matmul(ps[j * VW:(j + 1) * VW, O, :], va[g][:, b, j * VW:(j + 1) * VW],
                                     pr[:, (HG * b + j) % NPR, :], start=(b == 0), stop=(b == CT - 1),
                                     tile_position=(0, j * VW))
                if b == CT - 1:
                    last.then_inc(o_done, 1)
                else:
                    last.then_inc(pv_done, 1)

            def maxima_rows(k, g):
                pe.wait_ge(cut, 5 * k + 5)
                at_least(pe, att_done, k - 1)
                for t in range(CT):
                    last = pe.transpose(ps[KS:KS + MR, X, 0:S // 2].bitcast(BF16)[:, t * P:(t + 1) * P],
                                        n3[g % 2][:, HG * t:HG * (t + 1), :].rearrange("p j c -> p (j c)"),
                                        m.ident_bf[:, :], tile_position=(0, KS))
                last.then_inc(mT_done, 1)

            def sums_rows(k, g):
                pe.wait_ge(ot_out, k + 1)
                at_least(pe, att_done, k)
                pe.wait_ge(mT_out, min(k + 2, GROUPS) if isinstance(k, int) else k + 2)
                for t in range(CT):
                    last = pe.transpose(ps[:, X, t * P:(t + 1) * P], ot[g % 2][:, t * P:(t + 1) * P], m.ident[:, :])
                last.then_inc(oT_done, 1)

            def part(k, turn, g, n, live):
                for b in range(CT):
                    back, tb = lagged(k, b, LAG_T)
                    for j in range(HG):
                        if live[0]:
                            maxima_scores(k, turn, g, b, j)
                        if live[back]:
                            probability_scores(k - back, (g - back) % NB, tb, j)
                    back, ob = lagged(k, b, LAG_O)
                    if live[back]:
                        times_v(k - back, (g - back) % NB, ob)
                    if b == 0 and live[1]:
                        maxima_rows(k - 1, (g - 1) % NB)
                    if b == CT - 1 and live[2]:
                        sums_rows(k - 2, (g - 2) % NB)

            parts(pe, part)

        @block.scalar
        def _(act):
            def probabilities(k, g, b):
                for j in range(HG):
                    x = HG * b + j
                    act.wait_ge(z_done, STEPS * k + x + 1)
                    if j == 0:
                        pr_free(k, b)
                    act.activation(pr[:, x % NPR, :], ps[:, NBANK + x % NBANK, :], ACT.Exp, scale=float(HD) ** -0.5)\
                       .then_inc(p_done, 1)

            def pr_free(k, b):
                if b >= 2:
                    at_least(act, pv_done, (CT - 1) * k + b - 1)
                elif b == 1:
                    at_least(act, o_done, k)
                else:
                    at_least(act, pv_done, (CT - 1) * k)

            def part(k, turn, g, n, live):
                for b in range(CT):
                    back, tb = lagged(k, b, LAG_T)
                    if live[back]:
                        probabilities(k - back, (g - back) % NB, tb)
                    back, ob = lagged(k, b, LAG_O)
                    if live[back] and ob == CT - 1:
                        kk = k - back
                        act.wait_ge(o_done, kk + 1)
                        at_least(act, oT_done, kk)
                        act.activation(ot[(g - back) % 2][:, :], ps[:, O, :], ACT.Copy).then_inc(ot_out, 1)

            parts(act, part)

        @block.vector
        def _(dve):
            dve.wait_ge(preset, 1 + PARTS)
            for g in range(NB):
                dve.tensor_copy(ks[g][KS:P, :, :], pick[KS:P, :].unsqueeze(2).to_broadcast([P - KS, HG, S]))\
                   .then_inc(picked, 1)

            def stored(k, turn, g):
                return 2 * (turn - 1) + g // 2 - 1

            def maxima_parts_out(k):
                dve.wait_ge(mT_done, k + 1)
                at_least(dve, mT_spread, 16 * k)
                dve.tensor_copy(mT[KS:KS + MR, :], ps[KS:KS + MR, X, 0:S // 2].bitcast(BF16)).then_inc(mT_out, 1)

            def part(k, turn, g, n, live):
                for b in range(CT):
                    if live[0]:
                        if b == 0:
                            at_least(dve, cut, 5 * (k - 1))
                        for j in range(HG):
                            x = HG * b + j
                            dve.wait_ge(s_done, STEPS * k + x + 1)
                            dve.tensor_reduce(nm[g % 2][:, x:x + 1], ps[:, x % NBANK, :], AX.X, ALU.max, negate=True)\
                               .then_inc(max_done, 1)
                            if b == 1 and j == 0 and live[1]:
                                maxima_parts_out(k - 1)
                    elif b == 1 and live[1]:
                        maxima_parts_out(k - 1)
                    if b == CT - 1 and live[2]:
                        kk = k - 2
                        u = g % 2
                        sums = ps[:, X, :].rearrange("p (x w) -> p x w", w=VW)
                        dve.wait_ge(oT_done, kk + 1)
                        dve.reciprocal(rec[u][:, :], sums[:, :, HD]).then_inc(rec_done, 1)
                        dve.wait_ge(rec_done, kk + 1)
                        at_least(dve, att_stored[u], 16 * stored(k, turn, g))
                        dve.tensor_tensor(att[u][:, :, :].rearrange("p t (j w) -> p t j w", w=HD),
                                          sums[:, :, 0:HD].rearrange("p (t j) w -> p t j w", t=CT),
                                          rec[u][:, :].rearrange("p (t j) -> p t j", t=CT).unsqueeze(3)
                                          .to_broadcast([P, CT, HG, HD]), ALU.mult).then_inc(att_done, 1)

            parts(dve, part)


E1, K1, H2 = 8, 2, 704
ROW1 = D + E1
SENT = 6
BLOCKS = (T * K1 + E1 * (P - 1)) // P
SLOTS = E1 * T
HH = H2 // 2
FT1 = -(-H2 // P)
FL = H2 - (FT1 - 1) * P
WE = 2 * DT * H2 + FT1 * D


def finish_1(nc, m):
    with ExitStack() as ctx:
        def sb(name, shape, dt=F32):
            return ctx.enter_context(nc.sbuf_tensor(name, shape, dt))

        def sem(name):
            return counter(nc, m, ctx, name)

        wo = sb("f_wo", [P, DT, D])
        wg = sb("f_wg", [P, DT, E1])
        spare = sb("f_spare", [P, 2, P], I32)
        tokid = sb("f_tokid", [P, NT], I32)
        tri = sb("f_tri", [P, P], BF16)
        ones = sb("f_ones", [P, P], BF16)
        att = [sb(f"f_att{u}", [P, CT, D]) for u in range(2)]
        xc = [sb(f"f_xc{u}", [P, CT, D]) for u in range(2)]
        x3 = [sb(f"f_x3{u}", [P, CT, D]) for u in range(2)]
        row = [sb(f"f_row{u}", [P, CT, ROW1]) for u in range(2)]
        attT = sb("f_attT", [P, DT, S])
        hT = sb("f_hT", [P, DT, S])
        st = sb("f_st", [P, CT, 6])
        mv = sb("f_mv", [P, CT, 2])
        ve = sb("f_ve", [P, CT])
        rstd = sb("f_rstd", [P, CT])
        nmx = sb("f_nmx", [P, CT])
        lg = sb("f_lg", [P, CT, E1])
        ex = sb("f_ex", [P, CT, E1])
        sm = sb("f_sm", [P, CT])
        rs = sb("f_rs", [P, CT])
        score = sb("f_score", [P, CT, E1 + SENT])
        top8 = sb("f_top8", [P, CT, 8])
        take8 = sb("f_take8", [P, CT, 8])
        left = sb("f_left", [P, CT, E1 + SENT])
        chosen = sb("f_chosen", [P, CT, E1])
        chosen_bf = [sb(f"f_chosen_bf{u}", [P, CT, E1], BF16) for u in range(2)]
        wgt = sb("f_wgt", [P, CT, E1])
        wsum = sb("f_wsum", [P, CT])
        wrec = sb("f_wrec", [P, CT])
        slot = sb("f_slot", [P, CT, E1])
        both = sb("f_both", [P, CT, E1])
        high = sb("f_high", [P, CT])
        total = sb("f_total", [P, CT])
        dst = [sb(f"f_dst{u}", [P, K1, CT], I32) for u in range(2)]
        src = [sb(f"f_src{u}", [P, CT], I32) for u in range(2)]
        zero = sb("f_zero", [P, ROW1])
        jb = sb("f_jb", [P, BLOCKS, E1])
        tile_no = sb("f_tile_no", [P, E1, NT])
        eT = sb("f_eT", [P, E1])
        count = sb("f_count", [P, E1])
        more = sb("f_more", [P, E1, NT])
        nblk = sb("f_nblk", [P, E1])
        end = sb("f_end", [P, E1])
        one8 = sb("f_one8", [P, E1])
        begin = sb("f_begin", [P, E1])
        base = sb("f_base", [P, E1])
        in_end = sb("f_in_end", [P, BLOCKS, E1])
        mine = sb("f_mine", [P, BLOCKS, E1])
        tmp = sb("f_tmp", [P, BLOCKS, E1])
        some = sb("f_some", [P, BLOCKS])
        first_slot = sb("f_first_slot", [P, BLOCKS])
        spare_slot = sb("f_spare_slot", [P, BLOCKS])
        expert = sb("f_expert", [P, BLOCKS])
        ps = ctx.enter_context(nc.psum_tensor("f_ps", [P, 8, 512], F32))

        w_in = sem("f_w_in")
        made = sem("f_made")
        att_in = [sem(f"f_att_in{u}") for u in range(2)]
        xc_in = [sem(f"f_xc_in{u}") for u in range(2)]
        spare_out = sem("f_spare_out")
        preset = sem("f_preset")
        aT_done = sem("f_aT_done")
        aT_out = sem("f_aT_out")
        o_done = sem("f_o_done")
        x_done = sem("f_x_done")
        ve_done = sem("f_ve_done")
        rstd_done = sem("f_rstd_done")
        h_done = sem("f_h_done")
        tr_done = sem("f_tr_done")
        hT_out = sem("f_hT_out")
        l_done = sem("f_l_done")
        lg_done = sem("f_lg_done")
        ex_done = sem("f_ex_done")
        chain = sem("f_chain")
        stats = sem("f_stats")
        slots = sem("f_slots")
        zeroed = sem("f_zeroed")
        zero_out = sem("f_zero_out")
        table_step = sem("f_table_step")
        row_done = sem("f_row_done")
        chosen_done = sem("f_chosen_done")
        pos_done = sem("f_pos_done")
        pos_used = sem("f_pos_used")
        src_done = sem("f_src_done")
        dst_done = sem("f_dst_done")
        scattered = [sem(f"f_scattered{u}") for u in range(2)]
        x_out = [sem(f"f_x_out{u}") for u in range(2)]
        row_out = [sem(f"f_row_out{u}") for u in range(2)]
        block = ctx.enter_context(nc.Block())

        def steps(eng, body):
            def chunk(n):
                return (n, n // 2, n % 2) if 0 <= n < B else None
            for s in range(2):
                body(chunk(s), chunk(s - 1), chunk(s - 2))
            with eng.Fori(0, B // 2 - 2) as i:
                for u in range(2):
                    body((2 * i + 2 + u, i + 1, u), (2 * i + 1 + u, i + u, 1 - u), (2 * i + u, i, u))
            for s in range(B - 2, B + 2):
                body(chunk(s), chunk(s - 1), chunk(s - 2))

        def follows(a):
            if a is None or (isinstance(a[0], int) and a[0] + 1 >= B):
                return None
            return a[0] + 1, a[1] + a[2], 1 - a[2]

        @block.sync
        def _(sp):
            sp.dma_start(wo[:, :, :], m.ins["WoT1"].rearrange("(t p) n -> p t n", p=P)).then_inc(w_in, 16)
            sp.dma_start(wg[:, :, :], m.ins["WgT"].rearrange("(t p) n -> p t n", p=P)).then_inc(w_in, 16)
            sp.wait_ge(made, 1)
            sp.dma_start(m.slots1[0:SLOTS, :].rearrange("(p r s) a -> p r (s a)", p=P, s=2 * P)[:, 0:1, :],
                         spare[:, :, :].rearrange("p r s -> p (r s)").unsqueeze(1)).then_inc(spare_out, 16)
            sp.dma_start(m.slots1[SLOTS:SLOTS + P, :].rearrange("s a -> a s"), spare[0:1, 0, :]).then_inc(spare_out, 16)

            def load(n, i, u):
                if not (isinstance(n, int) and n == 0):
                    sp.wait_ge(aT_done, n)
                at_least(sp, x_done, CT * (n - 1))
                for src, dst, there in ((m.att, att, att_in), (m.sums, xc, xc_in)):
                    sp.dma_start(dst[u][:, :, :], src[bass.ds(n * S, S), :].rearrange("(t p) d -> p t d", p=P))\
                      .then_inc(there[u], 16)

            sp.wait_ge(zeroed, 1)
            sp.dma_start(m.rows1[T:T + P, :], zero[:, :]).then_inc(zero_out, 16)
            sp.dma_start(m.sums[T:T + P, :], zero[:, 0:D]).then_inc(zero_out, 16)
            load(0, 0, 0)

            def body(a, b, c):
                if follows(a):
                    load(*follows(a))
                if a:
                    n, i, u = a
                    sp.wait_ge(x_done, CT * (n + 1))
                    sp.dma_start(m.sums[bass.ds(n * S, S), :].rearrange("(t p) n -> p t n", p=P), x3[u][:, :, :])\
                      .then_inc(x_out[u], 16)
                if b:
                    n, i, u = b
                    sp.wait_ge(row_done, n + 1)
                    sp.dma_start(m.rows1[bass.ds(n * S, S), :].rearrange("(t p) n -> p t n", p=P), row[u][:, :, :])\
                      .then_inc(row_out[u], 16)

            steps(sp, body)
            sp.wait_ge(zero_out, 32)
            for u in range(2):
                sp.wait_ge(x_out[u], 16 * (B // 2))
                sp.wait_ge(row_out[u], 16 * (B // 2))

        @block.gpsimd
        def _(pool):
            pool.iota(spare[:, :, :], pattern=[[0, 2], [1, P]], base=T, channel_multiplier=0).then_inc(made, 1)
            pool.iota(tokid[:, :], pattern=[[P, NT]], base=0, channel_multiplier=1).then_inc(made, 1)
            pool.iota(m.next_slot[:, :], pattern=[[T, E1]], base=0, channel_multiplier=0,
                      allow_small_or_imprecise_dtypes=True).then_inc(made, 1)
            pool.memset(ones[:, :], 1.0).then_inc(made, 1)
            pool.memset(tri[:, :], 1.0).then_inc(made, 1)
            pool.wait_ge(made, 5)
            pool.affine_select(out=tri[:, :], in_=tri[:, :], compare_op=ALU.is_gt, fill=0.0, base=0,
                               pattern=[[1, P]], channel_multiplier=-1).then_inc(made, 1)
            pool.memset(zero[:, :], 0.0).then_inc(zeroed, 1)
            pool.iota(jb[:, :, :], pattern=[[1, BLOCKS], [0, E1]], base=0, channel_multiplier=0,
                      allow_small_or_imprecise_dtypes=True).then_inc(zeroed, 1)
            pool.iota(tile_no[:, :, :], pattern=[[0, E1], [P, NT]], base=0, channel_multiplier=0,
                      allow_small_or_imprecise_dtypes=True).then_inc(zeroed, 1)
            pool.iota(eT[:, :], pattern=[[T, E1]], base=0, channel_multiplier=0,
                      allow_small_or_imprecise_dtypes=True).then_inc(zeroed, 1)
            pool.memset(one8[:, :], 1.0).then_inc(zeroed, 1)
            pool.wait_ge(spare_out, 32)

            def body(a, b, c):
                if a:
                    n, i, u = a
                    pool.wait_ge(ve_done, n + 1)
                    pool.tensor_tensor(rstd[:, :], ve[:, :], m.minus_half[:, 0:CT], ALU.pow).then_inc(rstd_done, 1)
                if c:
                    n, i, u = c
                    at_least(pool, scattered[u], 16 * K1 * CT * i)
                    apart(m, pool)
                    pool.tensor_copy(src[u][:, :], tokid[:, bass.ds(n * CT, CT)]).then_inc(src_done, 1)
                    pool.wait_ge(src_done, n + 1)
                    pool.wait_ge(dst_done, 2 * (n + 1))
                    apart(m, pool)
                    for k in range(K1):
                        for j in range(CT):
                            pool.indirect_dma_start(m.slots1, bass.IndirectOffsetOnAxis(ap=dst[u][:, k, j:j + 1], axis=0),
                                                    src[u][:, j:j + 1], None).then_inc(scattered[u], 16)

            steps(pool, body)
            for u in range(2):
                pool.wait_ge(scattered[u], 16 * K1 * CT * (B // 2))

        @block.tensor
        def _(pe):
            pe.wait_ge(w_in, 32)
            pe.wait_ge(made, 6)

            def turned(n, i, u):
                pe.wait_ge(att_in[u], 16 * (i + 1))
                at_least(pe, aT_out, DT * n)
                for j in range(CT):
                    for d in range(DT):
                        last = pe.transpose(ps[:, d, j * P:(j + 1) * P], att[u][:, j, d * P:(d + 1) * P], m.ident[:, :])
                last.then_inc(aT_done, 1)

            def projected(n, i, u):
                pe.wait_ge(aT_out, DT * (n + 1))
                at_least(pe, x_done, CT * n)
                for j in range(CT):
                    for d in range(DT):
                        last = pe.matmul(ps[:, 2 + j // 2, (j % 2) * D:(j % 2 + 1) * D], attT[:, d, j * P:(j + 1) * P],
                                         wo[:, d, :], start=(d == 0), stop=(d == DT - 1))
                    if j % 2:
                        last.then_inc(o_done, 1)

            def logits(n, i, u):
                at_least(pe, hT_out, DT * n)
                for j in range(CT):
                    pe.wait_ge(h_done, CT * n + j + 1)
                    for d in range(DT):
                        last = pe.transpose(ps[:, 4 + d, j * P:(j + 1) * P], row[u][:, j, d * P:(d + 1) * P], m.ident[:, :])
                last.then_inc(tr_done, 1)
                pe.wait_ge(hT_out, DT * (n + 1))
                at_least(pe, lg_done, n)
                for j in range(CT):
                    for d in range(DT):
                        last = pe.matmul(ps[:, 6, j * E1:(j + 1) * E1], hT[:, d, j * P:(j + 1) * P], wg[:, d, :],
                                         start=(d == 0), stop=(d == DT - 1))
                last.then_inc(l_done, 1)

            def places(n, i, u):
                pe.wait_ge(chosen_done, n + 1)
                at_least(pe, pos_used, 2 * n)
                for j in range(CT + 1):
                    for k in range(min(j + 1, CT)):
                        last = pe.matmul(ps[:, 7, j * E1:(j + 1) * E1], tri[:, :] if k == j else ones[:, :],
                                         chosen_bf[u][:, k, :], start=(k == 0), stop=(k == min(j, CT - 1)))
                last.then_inc(pos_done, 1)

            turned(0, 0, 0)

            def body(a, b, c):
                if a:
                    projected(*a)
                if c:
                    places(*c)
                if b:
                    logits(*b)
                if follows(a):
                    turned(*follows(a))

            steps(pe, body)

        @block.scalar
        def _(act):
            def turned_out(n, i, u):
                act.wait_ge(aT_done, n + 1)
                at_least(act, o_done, 2 * n)
                for d in range(DT):
                    act.activation(attT[:, d, :], ps[:, d, :], ACT.Copy).then_inc(aT_out, 1)

            turned_out(0, 0, 0)

            def body(a, b, c):
                if b:
                    n, i, u = b
                    act.wait_ge(tr_done, n + 1)
                    at_least(act, l_done, n)
                    for d in range(DT):
                        act.activation(hT[:, d, :], ps[:, 4 + d, :], ACT.Copy).then_inc(hT_out, 1)
                    act.wait_ge(lg_done, n + 1)
                    act.activation(ex[:, :, :], lg[:, :, :], ACT.Exp).then_inc(ex_done, 1)
                if follows(a):
                    turned_out(*follows(a))

            steps(act, body)

        ROUTE_LINKS = 4 + CT + 1 + CT + 1 + 4

        @block.vector
        def _(dve):
            dve.memset(score[:, :, E1:], NEG).then_inc(preset, 1)
            dve.memset(take8[:, :, K1:8], NEG).then_inc(preset, 1)
            dve.wait_ge(preset, 2)
            dve.wait_ge(made, 3)

            def wide(t, width=E1):
                return t.unsqueeze(2).to_broadcast([P, CT, width])

            def statistics(n, i, u):
                at_least(dve, x_out[u], 16 * i)
                dve.wait_ge(xc_in[u], 16 * (i + 1))
                for j in range(CT):
                    dve.wait_ge(o_done, 2 * n + j // 2 + 1)
                    dve.scalar_tensor_tensor(x3[u][:, j, :], ps[:, 2 + j // 2, (j % 2) * D:(j % 2 + 1) * D],
                                             m.gate[:, 1:2], xc[u][:, j, :],
                                             ALU.mult, ALU.add).then_inc(x_done, 1)
                for j in range(CT):
                    dve.wait_ge(x_done, CT * n + j + 1)
                    apart(m, dve)
                    dve.bn_stats(st[:, j, :], x3[u][:, j, :]).then_inc(stats, 1)
                dve.wait_ge(stats, 2 * CT * n + CT)
                apart(m, dve)
                for j in range(CT):
                    dve.bn_aggr(mv[:, j, :], st[:, j, :]).then_inc(stats, 1)
                dve.wait_ge(stats, 2 * CT * (n + 1))
                dve.tensor_scalar(ve[:, :], mv[:, :, 1], EPS, None, ALU.add).then_inc(ve_done, 1)

            def normalised(n, i, u):
                dve.wait_ge(rstd_done, n + 1)
                at_least(dve, row_out[u], 16 * i)
                for j in range(CT):
                    dve.tensor_scalar(row[u][:, j, 0:D], x3[u][:, j, :], mv[:, j, 0:1], rstd[:, j:j + 1],
                                      ALU.subtract, ALU.mult).then_inc(h_done, 1)

            def routed(n, i, u):
                at = [0]

                def link(ins):
                    at[0] += 1
                    ins.then_inc(chain, 1)

                def linked():
                    dve.wait_ge(chain, n * ROUTE_LINKS + at[0])

                logits = ps[:, 6, 0:CT * E1].rearrange("p (t e) -> p t e", t=CT)
                dve.wait_ge(l_done, n + 1)
                link(dve.tensor_reduce(nmx[:, :], logits, AX.X, ALU.max, negate=True))
                linked()
                dve.tensor_tensor(lg[:, :, :], logits, wide(nmx[:, :]), ALU.add).then_inc(lg_done, 1)
                dve.wait_ge(ex_done, n + 1)
                link(dve.tensor_reduce(sm[:, :], ex[:, :, :], AX.X, ALU.add))
                linked()
                link(dve.reciprocal(rs[:, :], sm[:, :]))
                linked()
                link(dve.tensor_tensor(score[:, :, 0:E1], ex[:, :, :], wide(rs[:, :]), ALU.mult))
                linked()
                apart(m, dve)
                for j in range(CT):
                    link(dve.max(top8[:, j, :], score[:, j, :]))
                linked()
                link(dve.tensor_copy(take8[:, :, 0:K1], top8[:, :, 0:K1]))
                linked()
                apart(m, dve)
                for j in range(CT):
                    link(dve.match_replace(left[:, j, :], take8[:, j, :], score[:, j, :], LOW))
                linked()
                link(dve.tensor_scalar(chosen[:, :, :], left[:, :, 0:E1], LOW, None, ALU.is_equal))
                linked()
                dve.tensor_copy(chosen_bf[u][:, :, :], chosen[:, :, :]).then_inc(chosen_done, 1)
                link(dve.tensor_tensor(wgt[:, :, :], chosen[:, :, :], score[:, :, 0:E1], ALU.mult))
                linked()
                link(dve.tensor_reduce(wsum[:, :], wgt[:, :, :], AX.X, ALU.add))
                linked()
                link(dve.tensor_scalar(wsum[:, :], wsum[:, :], 1e-20, None, ALU.add))
                linked()
                link(dve.reciprocal(wrec[:, :], wsum[:, :]))
                linked()
                assert at[0] == ROUTE_LINKS, at[0]
                dve.scalar_tensor_tensor(row[u][:, :, D:ROW1], wgt[:, :, :], m.half_gate[:, 3:4], wide(wrec[:, :]),
                                         ALU.mult, ALU.mult).then_inc(row_done, 1)

            def slotted(n, i, u):
                dve.wait_ge(pos_done, n + 1)
                dve.tensor_tensor(slot[:, :, :], ps[:, 7, 0:CT * E1].rearrange("p (t e) -> p t e", t=CT),
                                  m.next_slot[:, :].unsqueeze(1).to_broadcast([P, CT, E1]), ALU.add).then_inc(pos_used, 1)
                dve.wait_ge(pos_used, 2 * n + 1)
                dve.tensor_tensor(m.next_slot[:, :], m.next_slot[:, :], ps[:, 7, CT * E1:(CT + 1) * E1], ALU.add)\
                   .then_inc(pos_used, 1)
                dve.tensor_tensor(both[:, :, :], chosen[:, :, :], slot[:, :, :], ALU.mult).then_inc(slots, 1)
                dve.wait_ge(slots, 3 * n + 1)
                dve.tensor_reduce(high[:, :], both[:, :, :], AX.X, ALU.max).then_inc(slots, 1)
                dve.tensor_reduce(total[:, :], both[:, :, :], AX.X, ALU.add).then_inc(slots, 1)
                dve.wait_ge(slots, 3 * n + 3)
                at_least(dve, scattered[u], 16 * K1 * CT * i)
                dve.tensor_copy(dst[u][:, 0, :], high[:, :]).then_inc(dst_done, 1)
                dve.tensor_tensor(dst[u][:, 1, :], total[:, :], high[:, :], ALU.subtract).then_inc(dst_done, 1)

            def body(a, b, c):
                if b:
                    normalised(*b)
                if a:
                    statistics(*a)
                if c:
                    slotted(*c)
                if b:
                    routed(*b)

            steps(dve, body)
            at = [0]

            def link(ins):
                at[0] += 1
                ins.then_inc(table_step, 1)
                dve.wait_ge(table_step, at[0])

            def over_blocks(t):
                return t.unsqueeze(1).to_broadcast([P, BLOCKS, E1])

            dve.wait_ge(zeroed, 5)
            link(dve.tensor_tensor(count[:, :], m.next_slot[:, :], eT[:, :], ALU.subtract))
            link(dve.tensor_tensor(more[:, :, :], count[:, :].unsqueeze(2).to_broadcast([P, E1, NT]), tile_no[:, :, :], ALU.is_gt))
            link(dve.tensor_reduce(nblk[:, :], more[:, :, :], AX.X, ALU.add))
            link(dve.tensor_tensor_scan(end[:, :], one8[:, :], nblk[:, :], 0.0, ALU.mult, ALU.add))
            link(dve.tensor_tensor(begin[:, :], end[:, :], nblk[:, :], ALU.subtract))
            link(dve.tensor_tensor(in_end[:, :, :], over_blocks(end[:, :]), jb[:, :, :], ALU.is_gt))
            link(dve.tensor_tensor(tmp[:, :, :], over_blocks(begin[:, :]), jb[:, :, :], ALU.is_gt))
            link(dve.tensor_tensor(mine[:, :, :], in_end[:, :, :], tmp[:, :, :], ALU.subtract))
            link(dve.tensor_reduce(some[:, :], mine[:, :, :], AX.X, ALU.add))
            link(dve.scalar_tensor_tensor(base[:, :], begin[:, :], -float(P), eT[:, :], ALU.mult, ALU.add))
            link(dve.scalar_tensor_tensor(tmp[:, :, :], jb[:, :, :], float(P), over_blocks(base[:, :]), ALU.mult, ALU.add))
            link(dve.tensor_tensor(in_end[:, :, :], tmp[:, :, :], mine[:, :, :], ALU.mult))
            link(dve.tensor_reduce(first_slot[:, :], in_end[:, :, :], AX.X, ALU.add))
            link(dve.tensor_scalar(spare_slot[:, :], some[:, :], -float(SLOTS), float(SLOTS), ALU.mult, ALU.add))
            link(dve.tensor_tensor(m.table[:, 0, :], first_slot[:, :], spare_slot[:, :], ALU.add))
            link(dve.tensor_tensor(tmp[:, :, :], over_blocks(eT[:, :]), mine[:, :, :], ALU.mult))
            link(dve.tensor_reduce(expert[:, :], tmp[:, :, :], AX.X, ALU.add))
            link(dve.tensor_scalar(m.table[:, 1, :], expert[:, :], float(WE) / T, None, ALU.mult))
            link(dve.tensor_scalar(m.table[:, 2, :], expert[:, :], 1.0 / T, None, ALU.mult))


def experts_1(nc, m):
    NBUF = 4
    with ExitStack() as ctx:
        def sb(name, shape, dt=F32):
            return ctx.enter_context(nc.sbuf_tensor(name, shape, dt))

        def sem(name):
            return counter(nc, m, ctx, name)

        idx = [sb(f"d_idx{g}", [P, 1], I32) for g in range(NBUF)]
        xg = [sb(f"d_xg{g}", [P, ROW1]) for g in range(NBUF)]
        xT = [sb(f"d_xT{u}", [P, DT, P]) for u in range(2)]
        th = sb("d_th", [P, 2, HH])
        a = sb("d_a", [P, 2, HH])
        b = [sb(f"d_b{u}", [P, 2, HH]) for u in range(2)]
        bT = [sb(f"d_bT{u}", [P, FT1, P]) for u in range(2)]
        y = [sb(f"d_y{g}", [P, D]) for g in range(NBUF)]
        ps = ctx.enter_context(nc.psum_tensor("d_ps", [P, 8, 512], F32))
        XB, HB, TB, YB = 0, 1, 5, 7

        idx_in = [sem(f"d_idx_in{g}") for g in range(NBUF)]
        x_in = [sem(f"d_x_in{g}") for g in range(NBUF)]
        xT_done = sem("d_xT_done")
        xT_out = sem("d_xT_out")
        h_done = sem("d_h_done")
        th_done = sem("d_th_done")
        a_done = sem("d_a_done")
        b_done = sem("d_b_done")
        bT_done = sem("d_bT_done")
        bT_act = sem("d_bT_act")
        bT_dve = sem("d_bT_dve")
        tail = sem("d_tail")
        y_done = sem("d_y_done")
        y_out = sem("d_y_out")
        added = [sem(f"d_added{g}") for g in range(NBUF)]
        block = ctx.enter_context(nc.Block())

        def parts(eng, part):
            LEAD = NBUF - 1
            for j in range(LEAD):
                part(j, 0, j, True, j > 0)
            passes = (BLOCKS - LEAD - 2) // NBUF
            with eng.Fori(0, passes) as i:
                for w in range(NBUF):
                    j = LEAD + w
                    part(NBUF * i + j, i + j // NBUF, j % NBUF, True, True)
            for j in range(LEAD + NBUF * passes, BLOCKS + 1):
                part(j, j // NBUF, j % NBUF, j < BLOCKS, True)

        def before(t, g, back):
            return t + (g - back) // NBUF, (g - back) % NBUF

        @block.sync
        def _(sp):
            def load(j, t, g):
                r = sp.value_load(m.table[0:1, 0, bass.ds(j, 1)], min_val=0, max_val=SLOTS)
                sp.dma_start(idx[g][:, :], m.slots1[bass.ds(r, P), :]).then_inc(idx_in[g], 16)

            for g in range(NBUF - 1):
                load(g, 0, g)

            with sp.Fori(0, (BLOCKS - NBUF + 1) // NBUF) as i:
                for w in range(NBUF):
                    g = (w + NBUF - 1) % NBUF
                    if w == 0:
                        sp.wait_ge(added[g], 16 * i)
                    else:
                        sp.wait_ge(added[g], 16 * (i + 1))
                    apart(m, sp)
                    load(NBUF * i + NBUF - 1 + w, i, g)
            assert (BLOCKS - NBUF + 1) % NBUF == 0
            for g in range(NBUF):
                sp.wait_ge(added[g], 16 * len(range(g, BLOCKS, NBUF)))

        @block.gpsimd
        def _(pool):
            def gather(t, g):
                pool.wait_ge(idx_in[g], 16 * (t + 1))
                apart(m, pool)
                pool.indirect_dma_start(xg[g][:, :], None, m.rows1[:, :],
                                        bass.IndirectOffsetOnAxis(ap=idx[g][:, :], axis=0)).then_inc(x_in[g], 16)

            for g in range(2):
                gather(0, g)

            def part(j, t, g, hid, res):
                ahead = j + 2
                if not isinstance(j, int) or ahead < BLOCKS:
                    tt, gg = before(t, g, -2)
                    if not (isinstance(j, int) and j < 2):
                        pool.wait_ge(added[gg], 16 * tt)
                    gather(tt, gg)
                if res:
                    tt, gg = before(t, g, 1)
                    pool.wait_ge(y_out, j)
                    if not (isinstance(j, int) and j < 2):
                        t2, g2 = before(t, g, 2)
                        pool.wait_ge(added[g2], 16 * (t2 + 1))
                    apart(m, pool)
                    pool.indirect_dma_start(m.sums, bass.IndirectOffsetOnAxis(ap=idx[gg][:, :], axis=0),
                                            y[gg][:, :], None, compute_op=ALU.add).then_inc(added[gg], 16)

            parts(pool, part)

        @block.tensor
        def _(pe):
            pe.wait_ge(m.w_in, 16 * 4 * E1)

            def x_rows(j, t, g):
                pe.wait_ge(x_in[g], 16 * (t + 1))
                if not (isinstance(j, int) and j == 0):
                    pe.wait_ge(xT_out, j)
                for d in range(DT):
                    last = pe.transpose(ps[:, XB, d * P:(d + 1) * P], xg[g][:, d * P:(d + 1) * P], m.ident[:, :])
                last.then_inc(xT_done, 1)

            def hidden(j, u, half, off):
                for w in range(2):
                    if not (isinstance(j, int) and j == 0):
                        pe.wait_ge(b_done, 2 * j - 1 + half)
                    for d in range(DT):
                        last = pe.matmul(ps[:, HB + 2 * half + w, 0:HH], xT[u][:, d, :],
                                         m.W[:, bass.ds(off + ((w * DT + d) * H2 + half * HH), HH)],
                                         start=(d == 0), stop=(d == DT - 1))
                last.then_inc(h_done, 1)

            def part(j, t, g, hid, res):
                if isinstance(j, int) and j == 0:
                    x_rows(0, 0, 0)
                if hid:
                    off = pe.value_load(m.table[0:1, 1, bass.ds(j, 1)], min_val=0, max_val=(E1 - 1) * WE)
                    pe.wait_ge(xT_out, j + 1)
                    hidden(j, g % 2, 0, off)
                if res:
                    u = (g - 1) % 2
                    pe.wait_ge(b_done, 2 * j)
                    if not (isinstance(j, int) and j == 1):
                        pe.wait_ge(bT_act, j - 1)
                        pe.wait_ge(bT_dve, j - 1)
                    flat = b[u][:, :, :].rearrange("p a h -> p (a h)")
                    for f in range(FT1):
                        rows = P if f < FT1 - 1 else FL
                        last = pe.transpose(ps[0:rows, TB + f // CT, (f % CT) * P:(f % CT + 1) * P],
                                            flat[:, f * P:f * P + rows], m.ident[:, :])
                        if f == CT - 1 or f == FT1 - 1:
                            last.then_inc(bT_done, 1)
                if hid:
                    hidden(j, g % 2, 1, off)
                    tt, gg = before(t, g, -1)
                    if not isinstance(j, int) or j + 1 < BLOCKS:
                        x_rows(j + 1, tt, gg)
                if res:
                    u = (g - 1) % 2
                    off2 = pe.value_load(m.table[0:1, 1, bass.ds(j - 1, 1)], min_val=0, max_val=(E1 - 1) * WE)
                    pe.wait_ge(bT_act, j)
                    pe.wait_ge(bT_dve, j)
                    if not (isinstance(j, int) and j == 1):
                        pe.wait_ge(y_out, j - 1)
                    for f in range(FT1):
                        rows = P if f < FT1 - 1 else FL
                        last = pe.matmul(ps[:, YB, 0:D], bT[u][0:rows, f, :],
                                         m.W[0:rows, bass.ds(off2 + (2 * DT * H2 + f * D), D)],
                                         start=(f == 0), stop=(f == FT1 - 1))
                    last.then_inc(y_done, 1)

            parts(pe, part)

        @block.scalar
        def _(act):
            def x_out(j, u):
                act.wait_ge(xT_done, j + 1)
                if not (isinstance(j, int) and j < 2):
                    act.wait_ge(h_done, 2 * (j - 1))
                act.activation(xT[u][:, :, :], ps[:, XB, 0:D].rearrange("p (d t) -> p d t", d=DT), ACT.Copy).then_inc(xT_out, 1)

            def part(j, t, g, hid, res):
                if isinstance(j, int) and j == 0:
                    x_out(0, 0)
                if hid:
                    act.wait_ge(h_done, 2 * j + 1)
                    if not (isinstance(j, int) and j == 0):
                        act.wait_ge(a_done, 2 * j - 1)
                    act.activation(th[:, 0, :], ps[:, HB, 0:HH], ACT.Tanh, scale=0.5).then_inc(th_done, 1)
                if res:
                    u = (g - 1) % 2
                    act.wait_ge(bT_done, 2 * j - 1)
                    if not (isinstance(j, int) and j < 3):
                        act.wait_ge(y_done, j - 2)
                    act.activation(bT[u][:, 0:CT, :], ps[:, TB, :].rearrange("p (f t) -> p f t", f=CT), ACT.Copy)\
                       .then_inc(bT_act, 1)
                if hid:
                    act.wait_ge(h_done, 2 * j + 2)
                    if not (isinstance(j, int) and j == 0):
                        act.wait_ge(a_done, 2 * j)
                    act.activation(th[:, 1, :], ps[:, HB + 2, 0:HH], ACT.Tanh, scale=0.5).then_inc(th_done, 1)
                    if not isinstance(j, int) or j + 1 < BLOCKS:
                        x_out(j + 1, (g + 1) % 2)
                if res:
                    tt, gg = before(t, g, 1)
                    e = act.value_load(m.table[0:1, 2, bass.ds(j - 1, 1)], min_val=0, max_val=E1 - 1)
                    act.wait_ge(y_done, j)
                    if not (isinstance(j, int) and j - 1 < NBUF):
                        act.wait_ge(added[gg], 16 * tt)
                    act.activation(y[gg][:, :], ps[:, YB, 0:D], ACT.Copy, scale=xg[gg][:, bass.ds(e + D, 1)]).then_inc(y_out, 1)

            parts(act, part)

        @block.vector
        def _(dve):
            def part(j, t, g, hid, res):
                def gated(half, u):
                    dve.wait_ge(th_done, 2 * j + half + 1)
                    dve.scalar_tensor_tensor(a[:, half, :], th[:, half, :], 1.0, ps[:, HB + 2 * half, 0:HH], ALU.add, ALU.mult)\
                       .then_inc(a_done, 1)
                    dve.wait_ge(a_done, 2 * j + half + 1)
                    if not (isinstance(j, int) and j < 2):
                        dve.wait_ge(bT_done, 2 * (j - 1))
                    dve.tensor_tensor(b[u][:, half, :], a[:, half, :], ps[:, HB + 2 * half + 1, 0:HH], ALU.mult)\
                       .then_inc(b_done, 1)

                if hid:
                    gated(0, g % 2)
                if res:
                    u = (g - 1) % 2
                    dve.wait_ge(bT_done, 2 * j)
                    if not (isinstance(j, int) and j < 3):
                        dve.wait_ge(y_done, j - 2)
                    dve.tensor_copy(bT[u][:, CT, :], ps[:, TB + 1, 0:P]).then_inc(tail, 1)
                    dve.tensor_copy(bT[u][0:FL, CT + 1, :], ps[0:FL, TB + 1, P:2 * P]).then_inc(bT_dve, 1)
                if hid:
                    gated(1, g % 2)

            parts(dve, part)



class Memory:
    pass


def flamingo_kernel(nc, ins, out):
    m = Memory()
    m.ins = ins

    def dram(name, shape, dt=F32):
        return nc.dram_tensor(name, shape, dt, kind="Internal").ap()

    m.acc = [dram(f"acc{u}", (T + CAP, D)) for u in range(2)]
    m.rows = dram("rows0", (T + CAP, ROW))
    m.qk = [dram(f"qk{a}", (B, PARTS, D, S), BF16) for a in range(2)]
    m.v = dram("v_heads", (T, H1 * VW))
    m.rows1 = dram("rows1", (T + P, ROW1))
    m.sums = out
    m.att = dram("att", (T, D))
    m.slots1 = dram("slots1", (SLOTS + P, 1), I32)

    with ExitStack() as keep:
        m.keep = keep

        def sb(where, name, shape, dt=F32):
            return where.enter_context(nc.sbuf_tensor(name, shape, dt))

        m.counted = set()
        m.x0_in = keep.enter_context(nc.semaphore("x0_in"))
        m.passed = keep.enter_context(nc.semaphore("passed"))
        m.ident = sb(keep, "ident", [P, P])
        m.ident_bf = sb(keep, "ident_bf", [P, P], BF16)
        m.causal = sb(keep, "causal", [P, P], BF16)
        m.minus_half = sb(keep, "minus_half", [P, CT])
        m.gate = sb(keep, "gate", [P, 4])
        m.half_gate = sb(keep, "half_gate", [P, 4])
        m.next_slot = sb(keep, "next_slot", [P, E1])
        m.w_in = keep.enter_context(nc.semaphore("w_in"))
        with ExitStack() as stream:
            m.x = sb(stream, "x", [P, NT, D])
            with ExitStack() as first:
                m.A = sb(first, "A", [P, DT, D])
                m.wv0 = sb(first, "wv0", [P, DT, D])
                constants(nc, m)
                attention_0(nc, m)
            with ExitStack() as experts:
                m.hT_all = sb(experts, "hT_all", [P, DT, T])
                m.keyT = sb(experts, "keyT", [P, T // 2])
                m.slots0 = sb(experts, "slots0", [CAP, E0], I32)
                route_0(nc, m)
                shared_0(nc, m)
                experts_0(nc, m)
            clear_counters(nc, m)
            project_1(nc, m)
        m.W = sb(keep, "W", [P, E1 * WE])
        m.table = sb(keep, "table", [P, 3, BLOCKS], I32)
        attention_1(nc, m)
        finish_1(nc, m)
        experts_1(nc, m)


def kernel(**inputs):
    import numpy as _np
    import concourse.bacc as _bacc
    from concourse import mybir as _mybir
    from concourse.bass_utils import run_bass_kernel_spmd as _run

    a = {k: _np.asarray(v) for k, v in inputs.items()}

    def dims_first(w):
        return w.reshape(*w.shape[:-1], NGRP, HG, HD).swapaxes(-1, -2).reshape(w.shape)

    laid = {
        "x": a["x"],
        "ctxT": a["ctx_1024"].reshape(T, D).T,
        "g_xattn": a["g_xattn"],
        "g_ffn": a["g_ffn"],
        "WqT0": a["L0_xattn_Wq"].T,
        "WkT0": a["L0_xattn_Wk"].T,
        "Wv0": a["L0_xattn_Wv"],
        "rwT": a["L0_ffn_router_weight"].T,
        "ebias": a["L0_ffn_expert_bias"],
        "w1": a["L0_ffn_w1"],
        "w2": a["L0_ffn_w2"],
        "sw1T": a["L0_ffn_sw1"].T,
        "sw2T": a["L0_ffn_sw2"].T,
        "WqT1": dims_first(a["L1_xattn_Wq"].T),
        "WkT1": dims_first(a["L1_xattn_Wk"].T),
        "WvT1": a["L1_xattn_Wv"].T,
        "WoT1": a["L1_xattn_Wo"].T,
        "bq": dims_first(a["L1_xattn_bq"]).reshape(DT, P).T,
        "bk": dims_first(a["L1_xattn_bk"]).reshape(DT, P).T,
        "bv": a["L1_xattn_bv"],
        "WgT": a["L1_ffn_Wg"].T,
        "W1T": a["L1_ffn_W1"].transpose(0, 2, 1),
        "W3T": a["L1_ffn_W3"].transpose(0, 2, 1),
        "W2T": a["L1_ffn_W2"].transpose(0, 2, 1),
    }
    nc = _bacc.Bacc("TRN2", target_bir_lowering=False, num_devices=1)
    arrays, ins = {}, {}
    for name, value in laid.items():
        value = _np.ascontiguousarray(value)
        arrays[f"in_{name}"] = value
        ins[name] = nc.dram_tensor(f"in_{name}", value.shape, _mybir.dt.from_np(value.dtype), kind="ExternalInput").ap()
    out = nc.dram_tensor("out_0", (T + P, D), _mybir.dt.float32, kind="ExternalOutput").ap()
    flamingo_kernel(nc, ins, out)
    r = _run(nc, [arrays], core_ids=[0])
    return r.results[0]["out_0"][0:T].reshape(B, S, D)
```
